# Optimizing a Trainium2 kernel written in Bass

```python
import numpy as np
import jax
import jax.numpy as jnp

def _softmax(x, axis=-1):
    return jax.nn.softmax(x, axis=axis)

def _gelu(x):
    return jax.nn.gelu(x, approximate=True)

def _silu(x):
    return jax.nn.silu(x)

def _sigmoid(x):
    return jax.nn.sigmoid(x)

def _layernorm(x, axis=-1, eps=1e-05):
    m = jnp.mean(x, axis=axis, keepdims=True)
    v = jnp.var(x, axis=axis, keepdims=True)
    return (x - m) / jnp.sqrt(v + eps)

def _scatter_add(tgt, idx, src, axis=0):
    return tgt.at[idx].add(src)

def _segment_sum(src, seg, n):
    return jax.ops.segment_sum(src, seg, n)
kernel_name = 'mk_decoder_postln_d2_seqx_r8_d3c98e'

def setup_inputs(seed: int=0):
    np.random.seed(seed)
    _w = jnp.asarray

    def _rec_inputs():
        import jax
        import jax.numpy as jnp
        _rk = jax.random.key(seed)
        x = 7.22e-05 + 1 * jax.random.normal(jax.random.fold_in(_rk, 1), (16, 256, 128), jnp.float32)
        _lenS = 256 - jax.random.randint(jax.random.fold_in(_rk, 7), (16,), 0, max(1, 256 // 4) + 1, jnp.int32)
        _lenS2 = 64 - jax.random.randint(jax.random.fold_in(_rk, 8), (16,), 0, max(1, 64 // 4) + 1, jnp.int32)
        _ctx_768P = jax.random.normal(jax.random.fold_in(_rk, 11), (16, 16, 96), jnp.float32)
        _ctx_768c = jax.random.dirichlet(jax.random.fold_in(_rk, 511), 0.3 * jnp.ones((16,), jnp.float32), (16, 64))
        _ctx_768t = jnp.einsum('bsk,bkd->bsd', _ctx_768c, _ctx_768P)
        _ctx_768t = _ctx_768t * jax.lax.rsqrt(jnp.mean(jnp.square(_ctx_768t)) + 1e-12) * 0.953939
        ctx_768 = -0.00055796 + 0.999787 * (_ctx_768t + 0.3 * jax.random.normal(jax.random.fold_in(_rk, 611), (16, 64, 96), jnp.float32))
        return (x, ctx_768)
    x, ctx_768 = _rec_inputs()

    def _L0_attn_setup():
        import jax, jax.numpy as jnp
        import numpy as np
        B, T, D, H = (8, 256, 128, 2)
        DK = D // H
        GAMMA_INIT, LAMBDA_INIT = (0.9, 0.1)
        key = jax.random.key(seed)
        ks = jax.random.split(key, 8)
        xav = float(np.sqrt(6.0 / (D + D)))

        def lin(k):
            return jax.random.uniform(k, (D, D), jnp.float32, -xav, xav)
        logit_g = float(np.log(GAMMA_INIT / (1.0 - GAMMA_INIT)))
        logit_l = float(np.log(LAMBDA_INIT / (1.0 - LAMBDA_INIT)))
        return {'x': jax.random.normal(ks[0], (B, T, D), jnp.float32), 'Wq': lin(ks[1]), 'Wk': lin(ks[2]), 'Wv': lin(ks[3]), 'Wo': lin(ks[4]), 'W_gamma': 0.02 * jax.random.normal(ks[5], (H, DK), jnp.float32), 'b_gamma': jnp.full((H, DK), logit_g, jnp.float32), 'W_lambda': 0.02 * jax.random.normal(ks[6], (H, DK), jnp.float32), 'b_lambda': jnp.full((H, DK), logit_l, jnp.float32)}
    _L0_attn_all = _L0_attn_setup()
    _L0_attn_in = {k: v for k, v in _L0_attn_all.items() if k in ('Wq', 'Wk', 'Wv', 'Wo', 'W_gamma', 'b_gamma', 'W_lambda', 'b_lambda')}
    del _L0_attn_all

    def _L0_xattn_setup():
        import jax, jax.numpy as jnp
        import numpy as np
        H = 8
        key = jax.random.key(seed)
        ks = jax.random.split(key, 7)
        B, Lq, Lkv = (4, 256, 64)
        dim_q, dim_kv = (128, 96)
        q = jax.random.normal(ks[0], (B, Lq, dim_q), dtype=jnp.float32)
        kv = jax.random.normal(ks[1], (B, Lkv, dim_kv), dtype=jnp.float32)
        Wq = jax.random.normal(ks[2], (dim_q, dim_q), dtype=jnp.float32) / np.sqrt(dim_q)
        Wk = jax.random.normal(ks[3], (dim_kv, dim_q), dtype=jnp.float32) / np.sqrt(dim_kv)
        Wv = jax.random.normal(ks[4], (dim_kv, dim_q), dtype=jnp.float32) / np.sqrt(dim_kv)
        Wo = jax.random.normal(ks[5], (dim_q, dim_q), dtype=jnp.float32) / np.sqrt(dim_q)
        bo = jax.random.normal(ks[6], (dim_q,), dtype=jnp.float32) * 0.01
        return {'q': q, 'kv': kv, 'Wq': Wq, 'Wk': Wk, 'Wv': Wv, 'Wo': Wo, 'bo': bo}
    _L0_xattn_all = _L0_xattn_setup()
    _L0_xattn_in = {k: v for k, v in _L0_xattn_all.items() if k in ('Wq', 'Wk', 'Wv', 'Wo', 'bo')}
    del _L0_xattn_all

    def _L0_ffn_setup():
        import jax, jax.numpy as jnp
        import numpy as np
        B, S = (2, 128)
        E, TOPK = (8, 2)
        HIDDEN, HEADS, NSLOTS = (128, 4, 64)
        HEAD_K = HIDDEN // HEADS
        HEAD_V = HIDDEN // HEADS
        GATE_NORM = 8.0
        SCALE = 1.0
        EPS = 1e-05
        CHUNK = 64
        CAP = S

        def rms_norm(x, w, eps=EPS):
            y = x * jax.lax.rsqrt(jnp.mean(x * x, axis=-1, keepdims=True) + eps)
            return y * w

        def swish(x):
            return x * jax.nn.sigmoid(x)

        def gsa_chunk(q, k, v, s, g):
            EBH = q.shape[:3]
            T, Dk, Dv, M = (q.shape[3], q.shape[-1], v.shape[-1], s.shape[-1])
            Nc = T // CHUNK

            def to_chunks(x):
                return jnp.moveaxis(x.reshape(EBH + (Nc, CHUNK, x.shape[-1])), 3, 0)
            qc, kc, vc, sc, gc = map(to_chunks, (q, k, v, s, g))
            Gc = jnp.cumsum(gc, axis=-2)
            tril = jnp.tril(jnp.ones((CHUNK, CHUNK), q.dtype))
            hk0 = jnp.zeros(EBH + (Dk, M), q.dtype)
            hv0 = jnp.zeros(EBH + (M, Dv), q.dtype)

            def step(carry, xs):
                hk, hv = carry
                qt, kt, vt, st, Gt = xs
                dec = jnp.exp(Gt)
                s_in = st * jnp.exp(-Gt)
                A = jnp.einsum('ebhik,ebhjk->ebhij', qt, kt) * SCALE * tril
                ok = dec * (jnp.einsum('ebhij,ebhjm->ebhim', A, s_in) + SCALE * jnp.einsum('ebhik,ebhkm->ebhim', qt, hk))
                qv = jax.nn.softmax(ok, axis=-1)
                qvg = qv * dec
                Tm = jnp.einsum('ebhim,ebhjm->ebhij', qvg, s_in) * tril
                ov = jnp.einsum('ebhij,ebhjd->ebhid', Tm, vt) + jnp.einsum('ebhim,ebhmd->ebhid', qvg, hv)
                gl = jnp.exp(Gt[..., -1, :])
                s_rem = st * jnp.exp(Gt[..., -1:, :] - Gt)
                hk = hk * gl[..., None, :] + jnp.einsum('ebhck,ebhcm->ebhkm', kt, s_rem)
                hv = hv * gl[..., :, None] + jnp.einsum('ebhcm,ebhcd->ebhmd', s_rem, vt)
                return ((hk, hv), ov)
            _, ov = jax.lax.scan(step, (hk0, hv0), (qc, kc, vc, sc, Gc))
            return jnp.moveaxis(ov, 0, 3).reshape(EBH + (T, Dv))

        def forward(hidden_states, norm_w, Wg, Wq, Wk, Wv, Wf, gnorm_w, Wo):
            b, s, d = hidden_states.shape
            x = rms_norm(hidden_states, norm_w)
            scores = jax.nn.softmax(jnp.einsum('bsd,ed->bse', x, Wg), axis=-1)
            rw, sel = jax.lax.top_k(scores, TOPK)
            rw = rw / jnp.sum(rw, axis=-1, keepdims=True)
            routing_mask = jax.nn.one_hot(sel, E, dtype=jnp.int32).sum(2)
            s_eff = s * TOPK
            xr = jnp.repeat(x, TOPK, axis=1).reshape(b * s_eff, d)
            batch_idx = jnp.repeat(jnp.arange(b), s_eff)
            combined = batch_idx * E + sel.reshape(-1)
            sorted_indices = jnp.argsort(combined)
            x_sorted = xr[sorted_indices]
            counts = routing_mask.sum(1)
            flat_end = (jnp.cumsum(counts, axis=1) + jnp.arange(b)[:, None] * s_eff).reshape(-1)
            start = jnp.concatenate([jnp.zeros((1,), flat_end.dtype), flat_end[:-1]])
            pos = jnp.arange(CAP)[None, :] + start[:, None]
            trunc = pos + counts.reshape(-1)[:, None] - CAP
            mask = (trunc < flat_end[:, None]) & (trunc >= 0) & (trunc >= start[:, None])
            trunc = jnp.where(mask, trunc, 0)
            xe = x_sorted[trunc.reshape(-1)].reshape(b * E, CAP, d) * mask[..., None]
            xe = xe.reshape(b, E, CAP, d).transpose(1, 0, 2, 3)
            q = jnp.einsum('ebtd,kd->ebtk', xe, Wq).reshape(E, b, CAP, HEADS, HEAD_K)
            k = jnp.einsum('ebtd,ekd->ebtk', xe, Wk).reshape(E, b, CAP, HEADS, HEAD_K)
            v = jnp.einsum('ebtd,ekd->ebtk', xe, Wv).reshape(E, b, CAP, HEADS, HEAD_V)
            f = jnp.einsum('ebtd,ekd->ebtk', xe, Wf).reshape(E, b, CAP, HEADS, NSLOTS)
            g = jax.nn.log_sigmoid(f) / GATE_NORM
            slot = 1.0 - jnp.exp(g)
            q, k = (swish(q), swish(k))
            tr = lambda a: a.transpose(0, 1, 3, 2, 4)
            o = gsa_chunk(tr(q), tr(k), tr(v), tr(slot), tr(g)).transpose(0, 1, 3, 2, 4)
            gathered = o.transpose(1, 0, 2, 3, 4).reshape(b * E * CAP, HEADS, HEAD_V)
            gathered = gathered * mask.reshape(-1)[:, None, None]
            resort = jnp.zeros((b * s_eff, HEADS, HEAD_V), gathered.dtype).at[trunc.reshape(-1)].add(gathered)
            restored = resort[jnp.argsort(sorted_indices)].reshape(b, s, TOPK, HEADS, HEAD_V)
            out = (restored * rw[..., None, None]).sum(2).reshape(b, s, HIDDEN)
            return jnp.einsum('bsd,od->bso', rms_norm(out, gnorm_w), Wo)
        key = jax.random.key(seed)
        ks = jax.random.split(key, 8)
        w = 0.02
        return {'hidden_states': jax.random.normal(ks[0], (B, S, HIDDEN), jnp.float32), 'norm_w': jnp.ones((HIDDEN,), jnp.float32), 'Wg': jax.random.normal(ks[1], (E, HIDDEN), jnp.float32) * w, 'Wq': jax.random.normal(ks[2], (HIDDEN, HIDDEN), jnp.float32) * w, 'Wk': jax.random.normal(ks[3], (E, HIDDEN, HIDDEN), jnp.float32) * w, 'Wv': jax.random.normal(ks[4], (E, HIDDEN, HIDDEN), jnp.float32) * w, 'Wf': jax.random.normal(ks[5], (E, HEADS * NSLOTS, HIDDEN), jnp.float32) * w, 'gnorm_w': jnp.ones((HIDDEN,), jnp.float32), 'Wo': jax.random.normal(ks[6], (HIDDEN, HIDDEN), jnp.float32) * w}
    _L0_ffn_all = _L0_ffn_setup()
    _L0_ffn_in = {k: v for k, v in _L0_ffn_all.items() if k in ('norm_w', 'Wg', 'Wq', 'Wk', 'Wv', 'Wf', 'gnorm_w', 'Wo')}
    del _L0_ffn_all

    def _L1_attn_setup():
        import jax, jax.numpy as jnp
        import numpy as np
        B, L, H = (8, 256, 128)
        MASK_IDENTITY = True
        key = jax.random.key(seed)
        ks = jax.random.split(key, 7)
        s = 1.0 / np.sqrt(H)
        return {'x': jax.random.normal(ks[0], (B, L, H), dtype=jnp.float32), 'Wq': jax.random.uniform(ks[1], (H, H), jnp.float32, -s, s), 'bq': jax.random.uniform(ks[2], (H,), jnp.float32, -s, s), 'Wk': jax.random.uniform(ks[3], (H, H), jnp.float32, -s, s), 'bk': jax.random.uniform(ks[4], (H,), jnp.float32, -s, s), 'Wv': jax.random.uniform(ks[5], (H, H), jnp.float32, -s, s), 'bv': jax.random.uniform(ks[6], (H,), jnp.float32, -s, s)}
    _L1_attn_all = _L1_attn_setup()
    _L1_attn_in = {k: v for k, v in _L1_attn_all.items() if k in ('Wq', 'bq', 'Wk', 'bk', 'Wv', 'bv')}
    del _L1_attn_all

    def _L1_xattn_setup():
        import jax, jax.numpy as jnp
        import numpy as np
        LATENT_CH = 128
        INPUT_CH = 96
        QK_CH = 128
        V_CH = 128
        OUT_CH = 128
        NHEADS = 8
        EPS = 1e-05

        def layer_norm(x, gamma, beta):
            mu = jnp.mean(x, axis=-1, keepdims=True)
            var = jnp.var(x, axis=-1, keepdims=True)
            return (x - mu) * jax.lax.rsqrt(var + EPS) * gamma + beta
        key = jax.random.key(seed)
        ks = jax.random.split(key, 6)
        B, Lq, Lkv = (8, 64, 2048)
        latent_q = jax.random.normal(ks[0], (B, Lq, LATENT_CH), dtype=jnp.float32)
        input_kv = jax.random.normal(ks[1], (B, Lkv, INPUT_CH), dtype=jnp.float32)
        W_Q = jax.random.normal(ks[2], (LATENT_CH, QK_CH), dtype=jnp.float32) / np.sqrt(LATENT_CH)
        W_K = jax.random.normal(ks[3], (INPUT_CH, QK_CH), dtype=jnp.float32) / np.sqrt(INPUT_CH)
        W_V = jax.random.normal(ks[4], (INPUT_CH, V_CH), dtype=jnp.float32) / np.sqrt(INPUT_CH)
        W_O = jax.random.normal(ks[5], (V_CH, OUT_CH), dtype=jnp.float32) / np.sqrt(V_CH)
        ln_lat_g = jnp.ones((LATENT_CH,), jnp.float32)
        ln_lat_b = jnp.zeros((LATENT_CH,), jnp.float32)
        ln_in_g = jnp.ones((INPUT_CH,), jnp.float32)
        ln_in_b = jnp.zeros((INPUT_CH,), jnp.float32)
        return dict(latent_q=latent_q, input_kv=input_kv, W_Q=W_Q, W_K=W_K, W_V=W_V, W_O=W_O, ln_lat_g=ln_lat_g, ln_lat_b=ln_lat_b, ln_in_g=ln_in_g, ln_in_b=ln_in_b)
    _L1_xattn_all = _L1_xattn_setup()
    _L1_xattn_in = {k: v for k, v in _L1_xattn_all.items() if k in ('W_Q', 'W_K', 'W_V', 'W_O', 'ln_lat_g', 'ln_lat_b', 'ln_in_g', 'ln_in_b')}
    del _L1_xattn_all

    def _L1_ffn_setup():
        import jax, jax.numpy as jnp
        import numpy as np
        NUM_HEADS = 16
        TOP_K = 2
        key = jax.random.key(seed)
        ks = jax.random.split(key, 5)
        B, S, D, E = (4, 256, 128, 8)
        scale = 0.02
        return {'x': jax.random.normal(ks[0], (B, S, D), dtype=jnp.float32), 'W_qkv': jax.random.normal(ks[1], (D, 3 * D), dtype=jnp.float32) * scale, 'b_qkv': jnp.zeros((3 * D,), dtype=jnp.float32), 'W_gate': jax.random.normal(ks[2], (D, E), dtype=jnp.float32) * scale, 'b_gate': jnp.zeros((E,), dtype=jnp.float32), 'W_experts': jax.random.normal(ks[3], (E, D, D), dtype=jnp.float32) * scale, 'b_experts': jnp.zeros((E, D), dtype=jnp.float32)}
    _L1_ffn_all = _L1_ffn_setup()
    _L1_ffn_in = {k: v for k, v in _L1_ffn_all.items() if k in ('W_qkv', 'b_qkv', 'W_gate', 'b_gate', 'W_experts', 'b_experts')}
    del _L1_ffn_all
    return {'x': x, 'ctx_768': ctx_768, 'L0_attn_Wq': _L0_attn_in['Wq'], 'L0_attn_Wk': _L0_attn_in['Wk'], 'L0_attn_Wv': _L0_attn_in['Wv'], 'L0_attn_Wo': _L0_attn_in['Wo'], 'L0_attn_W_gamma': _L0_attn_in['W_gamma'], 'L0_attn_b_gamma': _L0_attn_in['b_gamma'], 'L0_attn_W_lambda': _L0_attn_in['W_lambda'], 'L0_attn_b_lambda': _L0_attn_in['b_lambda'], 'L0_xattn_Wq': _L0_xattn_in['Wq'], 'L0_xattn_Wk': _L0_xattn_in['Wk'], 'L0_xattn_Wv': _L0_xattn_in['Wv'], 'L0_xattn_Wo': _L0_xattn_in['Wo'], 'L0_xattn_bo': _L0_xattn_in['bo'], 'L0_ffn_norm_w': _L0_ffn_in['norm_w'], 'L0_ffn_Wg': _L0_ffn_in['Wg'], 'L0_ffn_Wq': _L0_ffn_in['Wq'], 'L0_ffn_Wk': _L0_ffn_in['Wk'], 'L0_ffn_Wv': _L0_ffn_in['Wv'], 'L0_ffn_Wf': _L0_ffn_in['Wf'], 'L0_ffn_gnorm_w': _L0_ffn_in['gnorm_w'], 'L0_ffn_Wo': _L0_ffn_in['Wo'], 'L1_attn_Wq': _L1_attn_in['Wq'], 'L1_attn_bq': _L1_attn_in['bq'], 'L1_attn_Wk': _L1_attn_in['Wk'], 'L1_attn_bk': _L1_attn_in['bk'], 'L1_attn_Wv': _L1_attn_in['Wv'], 'L1_attn_bv': _L1_attn_in['bv'], 'L1_xattn_W_Q': _L1_xattn_in['W_Q'], 'L1_xattn_W_K': _L1_xattn_in['W_K'], 'L1_xattn_W_V': _L1_xattn_in['W_V'], 'L1_xattn_W_O': _L1_xattn_in['W_O'], 'L1_xattn_ln_lat_g': _L1_xattn_in['ln_lat_g'], 'L1_xattn_ln_lat_b': _L1_xattn_in['ln_lat_b'], 'L1_xattn_ln_in_g': _L1_xattn_in['ln_in_g'], 'L1_xattn_ln_in_b': _L1_xattn_in['ln_in_b'], 'L1_ffn_W_qkv': _L1_ffn_in['W_qkv'], 'L1_ffn_b_qkv': _L1_ffn_in['b_qkv'], 'L1_ffn_W_gate': _L1_ffn_in['W_gate'], 'L1_ffn_b_gate': _L1_ffn_in['b_gate'], 'L1_ffn_W_experts': _L1_ffn_in['W_experts'], 'L1_ffn_b_experts': _L1_ffn_in['b_experts']}

def reference(x, ctx_768, L0_attn_Wq, L0_attn_Wk, L0_attn_Wv, L0_attn_Wo, L0_attn_W_gamma, L0_attn_b_gamma, L0_attn_W_lambda, L0_attn_b_lambda, L0_xattn_Wq, L0_xattn_Wk, L0_xattn_Wv, L0_xattn_Wo, L0_xattn_bo, L0_ffn_norm_w, L0_ffn_Wg, L0_ffn_Wq, L0_ffn_Wk, L0_ffn_Wv, L0_ffn_Wf, L0_ffn_gnorm_w, L0_ffn_Wo, L1_attn_Wq, L1_attn_bq, L1_attn_Wk, L1_attn_bk, L1_attn_Wv, L1_attn_bv, L1_xattn_W_Q, L1_xattn_W_K, L1_xattn_W_V, L1_xattn_W_O, L1_xattn_ln_lat_g, L1_xattn_ln_lat_b, L1_xattn_ln_in_g, L1_xattn_ln_in_b, L1_ffn_W_qkv, L1_ffn_b_qkv, L1_ffn_W_gate, L1_ffn_b_gate, L1_ffn_W_experts, L1_ffn_b_experts):
    import jax
    import jax.numpy as jnp

    def _L0_attn_ref(x, Wq, Wk, Wv, Wo, W_gamma, b_gamma, W_lambda, b_lambda):
        import jax, jax.numpy as jnp
        import numpy as np
        B, T, D, H = (8, 256, 128, 2)
        DK = D // H
        GAMMA_INIT, LAMBDA_INIT = (0.9, 0.1)
        Bn, Tn, Dn = x.shape

        def heads(w):
            return (x @ w.T).reshape(Bn, Tn, H, DK).transpose(0, 2, 1, 3)
        q, k, v = (heads(Wq), heads(Wk), heads(Wv))
        k = k / jnp.maximum(jnp.linalg.norm(k, axis=-1, keepdims=True), 1e-12)
        Wg = W_gamma[None, :, None, :]
        bg = b_gamma[None, :, None, :]
        Wl = W_lambda[None, :, None, :]
        bl = b_lambda[None, :, None, :]
        gamma = jax.nn.sigmoid(Wg * k + bg)
        lam = jax.nn.sigmoid(Wl * k + bl)
        rho = (1.0 - lam) * gamma
        qs = q.transpose(2, 0, 1, 3)
        ks_ = k.transpose(2, 0, 1, 3)
        vs = v.transpose(2, 0, 1, 3)
        rs = rho.transpose(2, 0, 1, 3)
        S0 = jnp.zeros((Bn, H, DK, DK), x.dtype)

        def step(S, inp):
            q_t, k_t, v_t, r_t = inp
            rho_col = r_t[:, :, None, :]
            outer = v_t[:, :, :, None] * k_t[:, :, None, :]
            S = rho_col * S + (1.0 - rho_col) * outer
            y_t = jnp.einsum('bhv,bhvk->bhk', q_t, S)
            return (S, y_t)
        _, ys = jax.lax.scan(step, S0, (qs, ks_, vs, rs))
        out = ys.transpose(1, 0, 2, 3).reshape(Bn, Tn, Dn)
        return out @ Wo.T

    def _L0_xattn_ref(q, kv, Wq, Wk, Wv, Wo, bo):
        import jax, jax.numpy as jnp
        import numpy as np
        H = 8
        B, Lq, dim_q = q.shape
        hd = dim_q // H
        scale = jnp.asarray(hd, q.dtype) ** (-0.5)
        qp = q @ Wq
        kp = kv @ Wk
        vp = kv @ Wv
        qh = qp.reshape(B, Lq, H, hd)
        kh = kp.reshape(B, kv.shape[1], H, hd)
        vh = vp.reshape(B, kv.shape[1], H, hd)
        scores = jnp.einsum('bqhd,bkhd->bhqk', qh, kh) * scale
        attn = jax.nn.softmax(scores, axis=-1)
        out = jnp.einsum('bhqk,bkhd->bqhd', attn, vh).reshape(B, Lq, dim_q)
        return out @ Wo + bo

    def _L0_ffn_ref(hidden_states, norm_w, Wg, Wq, Wk, Wv, Wf, gnorm_w, Wo):
        import jax, jax.numpy as jnp
        import numpy as np
        B, S = (2, 128)
        E, TOPK = (8, 2)
        HIDDEN, HEADS, NSLOTS = (128, 4, 64)
        HEAD_K = HIDDEN // HEADS
        HEAD_V = HIDDEN // HEADS
        GATE_NORM = 8.0
        SCALE = 1.0
        EPS = 1e-05
        CHUNK = 64
        CAP = S

        def rms_norm(x, w, eps=EPS):
            y = x * jax.lax.rsqrt(jnp.mean(x * x, axis=-1, keepdims=True) + eps)
            return y * w

        def swish(x):
            return x * jax.nn.sigmoid(x)

        def gsa_chunk(q, k, v, s, g):
            EBH = q.shape[:3]
            T, Dk, Dv, M = (q.shape[3], q.shape[-1], v.shape[-1], s.shape[-1])
            Nc = T // CHUNK

            def to_chunks(x):
                return jnp.moveaxis(x.reshape(EBH + (Nc, CHUNK, x.shape[-1])), 3, 0)
            qc, kc, vc, sc, gc = map(to_chunks, (q, k, v, s, g))
            Gc = jnp.cumsum(gc, axis=-2)
            tril = jnp.tril(jnp.ones((CHUNK, CHUNK), q.dtype))
            hk0 = jnp.zeros(EBH + (Dk, M), q.dtype)
            hv0 = jnp.zeros(EBH + (M, Dv), q.dtype)

            def step(carry, xs):
                hk, hv = carry
                qt, kt, vt, st, Gt = xs
                dec = jnp.exp(Gt)
                s_in = st * jnp.exp(-Gt)
                A = jnp.einsum('ebhik,ebhjk->ebhij', qt, kt) * SCALE * tril
                ok = dec * (jnp.einsum('ebhij,ebhjm->ebhim', A, s_in) + SCALE * jnp.einsum('ebhik,ebhkm->ebhim', qt, hk))
                qv = jax.nn.softmax(ok, axis=-1)
                qvg = qv * dec
                Tm = jnp.einsum('ebhim,ebhjm->ebhij', qvg, s_in) * tril
                ov = jnp.einsum('ebhij,ebhjd->ebhid', Tm, vt) + jnp.einsum('ebhim,ebhmd->ebhid', qvg, hv)
                gl = jnp.exp(Gt[..., -1, :])
                s_rem = st * jnp.exp(Gt[..., -1:, :] - Gt)
                hk = hk * gl[..., None, :] + jnp.einsum('ebhck,ebhcm->ebhkm', kt, s_rem)
                hv = hv * gl[..., :, None] + jnp.einsum('ebhcm,ebhcd->ebhmd', s_rem, vt)
                return ((hk, hv), ov)
            _, ov = jax.lax.scan(step, (hk0, hv0), (qc, kc, vc, sc, Gc))
            return jnp.moveaxis(ov, 0, 3).reshape(EBH + (T, Dv))

        def forward(hidden_states, norm_w, Wg, Wq, Wk, Wv, Wf, gnorm_w, Wo):
            b, s, d = hidden_states.shape
            x = rms_norm(hidden_states, norm_w)
            scores = jax.nn.softmax(jnp.einsum('bsd,ed->bse', x, Wg), axis=-1)
            rw, sel = jax.lax.top_k(scores, TOPK)
            rw = rw / jnp.sum(rw, axis=-1, keepdims=True)
            routing_mask = jax.nn.one_hot(sel, E, dtype=jnp.int32).sum(2)
            s_eff = s * TOPK
            xr = jnp.repeat(x, TOPK, axis=1).reshape(b * s_eff, d)
            batch_idx = jnp.repeat(jnp.arange(b), s_eff)
            combined = batch_idx * E + sel.reshape(-1)
            sorted_indices = jnp.argsort(combined)
            x_sorted = xr[sorted_indices]
            counts = routing_mask.sum(1)
            flat_end = (jnp.cumsum(counts, axis=1) + jnp.arange(b)[:, None] * s_eff).reshape(-1)
            start = jnp.concatenate([jnp.zeros((1,), flat_end.dtype), flat_end[:-1]])
            pos = jnp.arange(CAP)[None, :] + start[:, None]
            trunc = pos + counts.reshape(-1)[:, None] - CAP
            mask = (trunc < flat_end[:, None]) & (trunc >= 0) & (trunc >= start[:, None])
            trunc = jnp.where(mask, trunc, 0)
            xe = x_sorted[trunc.reshape(-1)].reshape(b * E, CAP, d) * mask[..., None]
            xe = xe.reshape(b, E, CAP, d).transpose(1, 0, 2, 3)
            q = jnp.einsum('ebtd,kd->ebtk', xe, Wq).reshape(E, b, CAP, HEADS, HEAD_K)
            k = jnp.einsum('ebtd,ekd->ebtk', xe, Wk).reshape(E, b, CAP, HEADS, HEAD_K)
            v = jnp.einsum('ebtd,ekd->ebtk', xe, Wv).reshape(E, b, CAP, HEADS, HEAD_V)
            f = jnp.einsum('ebtd,ekd->ebtk', xe, Wf).reshape(E, b, CAP, HEADS, NSLOTS)
            g = jax.nn.log_sigmoid(f) / GATE_NORM
            slot = 1.0 - jnp.exp(g)
            q, k = (swish(q), swish(k))
            tr = lambda a: a.transpose(0, 1, 3, 2, 4)
            o = gsa_chunk(tr(q), tr(k), tr(v), tr(slot), tr(g)).transpose(0, 1, 3, 2, 4)
            gathered = o.transpose(1, 0, 2, 3, 4).reshape(b * E * CAP, HEADS, HEAD_V)
            gathered = gathered * mask.reshape(-1)[:, None, None]
            resort = jnp.zeros((b * s_eff, HEADS, HEAD_V), gathered.dtype).at[trunc.reshape(-1)].add(gathered)
            restored = resort[jnp.argsort(sorted_indices)].reshape(b, s, TOPK, HEADS, HEAD_V)
            out = (restored * rw[..., None, None]).sum(2).reshape(b, s, HIDDEN)
            return jnp.einsum('bsd,od->bso', rms_norm(out, gnorm_w), Wo)
        return forward(hidden_states, norm_w, Wg, Wq, Wk, Wv, Wf, gnorm_w, Wo)

    def _L1_attn_ref(x, Wq, bq, Wk, bk, Wv, bv):
        import jax, jax.numpy as jnp
        import numpy as np
        B, L, H = (8, 256, 128)
        MASK_IDENTITY = True
        q = jnp.einsum('blh,oh->blo', x, Wq) + bq
        k = jnp.einsum('blh,oh->blo', x, Wk) + bk
        v = jnp.einsum('blh,oh->blo', x, Wv) + bv
        hidden = q.shape[-1]
        attn = jnp.einsum('blh,bmh->blm', q / hidden, k)
        if MASK_IDENTITY:
            mask_value = -jnp.finfo(attn.dtype).max
            eye = jnp.eye(attn.shape[-1], dtype=bool)
            attn = jnp.where(eye[None, :, :], mask_value, attn)
        attn = jax.nn.softmax(attn, axis=-1)
        return jnp.einsum('blm,bmh->blh', attn, v)

    def _L1_xattn_ref(latent_q, input_kv, W_Q, W_K, W_V, W_O, ln_lat_g, ln_lat_b, ln_in_g, ln_in_b):
        import jax, jax.numpy as jnp
        import numpy as np
        LATENT_CH = 128
        INPUT_CH = 96
        QK_CH = 128
        V_CH = 128
        OUT_CH = 128
        NHEADS = 8
        EPS = 1e-05

        def layer_norm(x, gamma, beta):
            mu = jnp.mean(x, axis=-1, keepdims=True)
            var = jnp.var(x, axis=-1, keepdims=True)
            return (x - mu) * jax.lax.rsqrt(var + EPS) * gamma + beta
        B, Lq, _ = latent_q.shape
        _, Lkv, _ = input_kv.shape
        H = NHEADS
        dqk = QK_CH // H
        dv = V_CH // H
        lat = layer_norm(latent_q, ln_lat_g, ln_lat_b)
        inp = layer_norm(input_kv, ln_in_g, ln_in_b)
        Q = (lat @ W_Q).reshape(B, Lq, H, dqk)
        K = (inp @ W_K).reshape(B, Lkv, H, dqk)
        V = (inp @ W_V).reshape(B, Lkv, H, dv)
        scale = 1.0 / np.sqrt(dqk).astype(np.float32)
        attn = jnp.einsum('bqhd,bkhd->bhqk', Q, K) * scale
        attn = jax.nn.softmax(attn, axis=-1)
        out = jnp.einsum('bhqk,bkhd->bqhd', attn, V).reshape(B, Lq, V_CH)
        return out @ W_O

    def _L1_ffn_ref(x, W_qkv, b_qkv, W_gate, b_gate, W_experts, b_experts):
        import jax, jax.numpy as jnp
        import numpy as np
        NUM_HEADS = 16
        TOP_K = 2
        B, S, D = x.shape
        H = NUM_HEADS
        hd = D // H
        E = W_gate.shape[-1]
        qkv = (x @ W_qkv + b_qkv).reshape(B, S, 3, H, hd)
        q, k, v = (qkv[:, :, 0], qkv[:, :, 1], qkv[:, :, 2])
        attn = jnp.einsum('bqhd,bkhd->bhqk', q, k) / jnp.sqrt(jnp.asarray(hd, x.dtype))
        attn = jax.nn.softmax(attn, axis=-1)
        attn_out = jnp.einsum('bhqk,bkhd->bqhd', attn, v).reshape(B, S, D)
        gate = jax.nn.softmax(x @ W_gate + b_gate, axis=-1)
        top_g, top_i = jax.lax.top_k(gate, TOP_K)
        combine = jnp.sum(jax.nn.one_hot(top_i, E, dtype=x.dtype) * top_g[..., None], axis=2)
        expert_out = jnp.einsum('bsd,edf->bsef', x, W_experts) + b_experts
        moe_out = jnp.einsum('bsef,bse->bsf', expert_out, combine)
        return attn_out + moe_out
    x = _layernorm(x + _L0_attn_ref(x, L0_attn_Wq, L0_attn_Wk, L0_attn_Wv, L0_attn_Wo, L0_attn_W_gamma, L0_attn_b_gamma, L0_attn_W_lambda, L0_attn_b_lambda), axis=-1)
    x = _layernorm(x + _L0_xattn_ref(x, ctx_768, L0_xattn_Wq, L0_xattn_Wk, L0_xattn_Wv, L0_xattn_Wo, L0_xattn_bo), axis=-1)
    x = _layernorm(x + _L0_ffn_ref(x, L0_ffn_norm_w, L0_ffn_Wg, L0_ffn_Wq, L0_ffn_Wk, L0_ffn_Wv, L0_ffn_Wf, L0_ffn_gnorm_w, L0_ffn_Wo), axis=-1)
    x = _layernorm(x + _L1_attn_ref(x, L1_attn_Wq, L1_attn_bq, L1_attn_Wk, L1_attn_bk, L1_attn_Wv, L1_attn_bv), axis=-1)
    x = _layernorm(x + _L1_xattn_ref(x, ctx_768, L1_xattn_W_Q, L1_xattn_W_K, L1_xattn_W_V, L1_xattn_W_O, L1_xattn_ln_lat_g, L1_xattn_ln_lat_b, L1_xattn_ln_in_g, L1_xattn_ln_in_b), axis=-1)
    x = _layernorm(x + _L1_ffn_ref(x, L1_ffn_W_qkv, L1_ffn_b_qkv, L1_ffn_W_gate, L1_ffn_b_gate, L1_ffn_W_experts, L1_ffn_b_experts), axis=-1)
    return x

_drawn_inputs = setup_inputs


def setup_inputs(seed=0):
    import zlib

    import numpy as np

    out = dict(_drawn_inputs(seed))
    spreads = {'L0_attn_b_gamma': (2.1972246170043945, 0.2),
     'L0_attn_b_lambda': (-2.1972246170043945, 0.2),
     'L0_ffn_norm_w': (1.0, 0.2),
     'L0_ffn_gnorm_w': (1.0, 0.2),
     'L1_xattn_ln_lat_g': (1.0, 0.2),
     'L1_xattn_ln_lat_b': (0.0, 0.458),
     'L1_xattn_ln_in_g': (1.0, 0.2),
     'L1_xattn_ln_in_b': (0.0, 0.1),
     'L1_ffn_b_qkv': (0.0, 0.1),
     'L1_ffn_b_gate': (0.0, 0.1),
     'L1_ffn_b_experts': (0.0, 0.366)}
    factors = {'L0_attn_W_gamma': 34.408,
     'L0_attn_W_lambda': 32.936,
     'L0_ffn_Wq': 8.0,
     'L0_ffn_Wk': 8.0,
     'L0_ffn_Wf': 8.0,
     'L1_attn_Wq': 8.0,
     'L1_attn_bq': 35.772,
     'L1_attn_Wk': 8.0,
     'L1_attn_bk': 64.0}
    for name, (base, spread) in spreads.items():
        noise = np.random.default_rng([zlib.crc32(name.encode()), seed]).standard_normal(out[name].shape)
        drawn = base * np.exp(spread * noise) if base else spread * noise
        out[name] = jnp.asarray(drawn.astype(out[name].dtype))
    for name, factor in factors.items():
        out[name] = (out[name] * factor).astype(out[name].dtype)
    return out
```

```python
from contextlib import ExitStack

import concourse.bass as bass
from concourse import mybir

P = 128
B, T, D = 16, 256, 128
KV, CC = 64, 96
ITEMS, IB = 2, 2
ROUNDS = B // (ITEMS * IB)
TILES = IB * T // P
TOK = IB * T
HALF = T // P
EXPERTS, TOPK, CAP = 8, 2, 128
GH, GK, GM = 4, 32, 64
XH, XD = 8, 16
SH, SD = 16, 8
GATE_NORM = 8.0
EPS = 1e-5
BANK = 512
LAYERS = 6
LAST = LAYERS
PAIRS, QUADS = SH // 2, SH // 4
TERMS = 9
STACK = TERMS * SD

F32 = mybir.dt.float32
BF16 = mybir.dt.bfloat16
ALU = mybir.AluOpType
ACT = mybir.ActivationFunctionType
AX = mybir.AxisListType

_WIDTHS = [
    ("a_wq", D), ("a_wk", D), ("a_wv", D), ("a_wo", D),
    ("x0_wq", D), ("x0_wo", D),
    ("g_wg", EXPERTS), ("g_wq", D), ("g_wo", D),
    ("g_wk", EXPERTS * D), ("g_wv", EXPERTS * D), ("g_wf", EXPERTS * GH * GM),
    ("s_wq", D), ("s_wk", D), ("s_wv", D),
    ("x1_wq", D), ("x1_wo", D),
    ("m_wq", D), ("m_wk", D), ("m_wv", D), ("m_wg", EXPERTS), ("m_we", EXPERTS * D),
]
_COLS = ["a_wgamma", "a_bgamma", "a_wlambda", "a_blambda", "g_norm", "g_gnorm",
         "s_bq", "s_bk", "lat_g", "lat_b", "m_bq", "m_bk"]
_CONSTS = [("ident", P), ("causal", P), ("decay_mask", 3 * P), ("mid_sum", P), ("suffix", P), ("ones", T),
           ("head_sum", P), ("kv_heads", XH), ("v_heads", BANK), ("slot", P), ("tie", EXPERTS * EXPERTS),
           ("no_self", HALF * T)]
_ROWS = [("bo", D), ("s_bv", D), ("m_bv", D), ("m_bg", EXPERTS)]


def _places(widths):
    out, at = {}, 0
    for name, width in widths:
        out[name] = (at, at + width)
        at += width
    return out, at


W_AT, W_COLS = _places(_WIDTHS)
V_AT, V_COLS = _places([(n, 1) for n in _COLS])
C_AT, C_COLS = _places(_CONSTS)
R_AT, R_COLS = _places(_ROWS)


RISES = {
    "stored": (32, 0), "x_free": (2, 0), "x_kv": (4, 0), "m_split": (2, 0), "m_spilled0": (16, 0), "m_spilled1":
    (16, 0), "m_stacked": (608, 0), "m_row": (2, 0), "m_max_spilled0": (16, 0), "m_max_spilled1": (16, 0),
    "m_max_stacked": (32, 0), "x_made": (12, 0), "g_xe": (16, 2), "g_qkf_made": (16, 2), "m_pv": (32, 4),
    "xT_made": (12, 0), "xT_kept": (12, 0), "a_qkv": (2, 0), "a_sq": (2, 0), "a_ss": (2, 0), "a_UT": (2, 0),
    "a_U": (2, 0), "a_qv_kept": (2, 0), "a_A": (4, 0), "a_Am": (4, 0), "a_U_kept": (2, 0), "a_y": (2, 0),
    "a_yT": (2, 0), "y_made": (10, 0), "x_q": (4, 0), "x_q_kept": (4, 0), "x_kv_kept": (4, 0), "x_scores": (8,
    0), "x_norm": (8, 0), "x_PT": (8, 0), "x_PT_kept": (8, 0), "x_o": (4, 0), "x_o_kept": (4, 0), "g_xn": (2,
    0), "logits": (4, 0), "sel_made": (4, 0), "g_count": (2, 0), "g_place": (16, 2), "g_o0": (8, 1), "g_o1": (8,
    1), "g_xe_kept": (16, 2), "g_wk": (8, 1), "g_PwT_kept": (16, 2), "g_v_made": (16, 2), "g_sp": (16, 2),
    "g_decay": (16, 2), "g_dec": (16, 2), "g_qk": (16, 2), "g_A": (16, 2), "g_Am": (16, 2), "g_s": (16, 2),
    "g_ok": (16, 2), "g_qd": (16, 2), "g_qdT": (16, 2), "g_qdT_kept": (16, 2), "g_T": (16, 2), "g_Tm": (16, 2),
    "g_ov": (16, 2), "g_out": (2, 0), "g_on": (2, 0), "g_onT": (2, 0), "g_onT_kept": (2, 0), "s_qkv": (2, 0),
    "s_q": (2, 0), "s_kv": (2, 0), "s_scores": (2, 0), "s_exp": (2, 0), "s_PT": (2, 0), "s_PT_kept": (2, 0),
    "l_made": (2, 0), "m_qkv": (2, 0), "w_made": (4, 0), "m_qkv_kept": (2, 0), "m_wT": (2, 0), "m_wT_kept": (2,
    0), "m_bias": (2, 0), "m_moe": (8, 0), "m_moe_read": (8, 0), "m_max_read": (32, 8), "m_max_scores": (32, 8),
    "m_mxT": (2, 0), "m_exp": (32, 4), "m_scores": (32, 4), "act_own": (36, 0), "a_ss_kept": (2, 0), "a_rn": (2,
    0), "a_kn": (2, 0), "a_e": (2, 0), "a_den": (2, 0), "a_L": (2, 0), "a_D": (2, 0), "a_E": (2, 0), "a_Ep": (2,
    0), "var_made": (12, 0), "rstd_made": (12, 0), "x_less_max": (8, 0), "x_exp": (8, 0), "g_rms": (4, 0),
    "less_max": (4, 0), "gate_exp": (4, 0), "g_exp": (16, 2), "g_v": (16, 2), "g_exp_cut": (16, 2), "g_ln": (16,
    2), "g_sig": (16, 2), "g_sT": (16, 2), "g_less_max": (16, 2), "g_p": (16, 2), "s_max": (2, 0), "l_var": (2,
    0), "l_rstd": (2, 0), "m_qk": (2, 0), "dve_own": (214, 0), "x_rs": (8, 0), "g_slot": (2, 0),
    "dve_own_experts": (64, 8),
}

PRIMED = ("x_made", "stored", "g_o0", "g_o1", "g_xe", "g_qkf_made", "m_max_read", "m_exp", "m_pv")


class Signal:

    def __init__(self, sem, primed, per_round, per_step):
        self.primed = primed
        self.sem, self.per_round, self.per_step = sem, per_round, per_step
        self.raised_round, self.raised_step, self.frozen = 0, 0, False

    def at(self, now, n):
        value = now.round * self.per_round + (n + self.primed)
        if now.step is not None and self.per_step:
            value = value + now.step * self.per_step
        return self.sem, value

    def up(self, now, n=1):
        if self.frozen:
            return self.sem, n
        if now.step is None:
            self.raised_round += n
        else:
            self.raised_step += n
            self.raised_round += n * now.steps
        return self.sem, n


class Signals:

    def __init__(self, nc, ctx):
        self.nc, self.ctx, self.all = nc, ctx, {}

    def __getitem__(self, name):
        if name not in self.all:
            sem = self.ctx.enter_context(self.nc.semaphore(name))
            fixed = {"x_loaded0": (16, 0), "x_loaded1": (16, 0), "ctx_loaded": (ITEMS * 32, 0)}
            self.all[name] = Signal(sem, int(name in PRIMED), *fixed.get(name, RISES.get(name, (0, 0))))
        return self.all[name]

    def rises(self):
        return {k: (s.raised_round, s.raised_step) for k, s in self.all.items()}


class Now:

    def __init__(self, round_):
        self.round, self.step, self.steps = round_, None, 1

    def inner(self, step, steps):
        now = Now(self.round)
        now.step, now.steps = step, steps
        return now


class Own:

    def __init__(self, counter, now):
        self.counter, self.now, self.n = counter, now, 0

    def next(self):
        self.n += 1
        return self.counter.up(self.now)

    def all(self):
        return self.counter.at(self.now, self.n)


def build(nc, x, ctx_tok, ctx_T, w_pack, w_ctx, col_pack, ctx_cols, const_pack, rows, b_experts, ones_row, out):
    ctx = ExitStack()
    with ctx:
        S = Signals(nc, ctx)

        def sb(name, shape, dt=F32):
            return ctx.enter_context(nc.sbuf_tensor(name, shape, dt))

        weights = sb("weights", [P, W_COLS])
        wctx = sb("wctx", [CC, 4 * D])
        cols = sb("cols", [P, V_COLS])
        neg_cols = sb("neg_cols", [P, V_COLS])
        ccols = sb("ccols", [CC, 2])
        consts = sb("consts", [P, C_COLS])
        row_sb = sb("row_sb", [1, R_COLS])
        bexp = sb("bexp", [EXPERTS, D])
        x_in = sb("x_in", [P, ITEMS, TILES, D])
        ctx_k = sb("ctx_k", [P, ITEMS, CC])
        ctx_t = sb("ctx_t", [CC, ITEMS, P])
        xs = sb("xs", [P, ITEMS, TILES, D])
        zs = sb("zs", [P, ITEMS, TILES, D])
        stats = sb("stats", [P, ITEMS, TILES + 1, 6])
        mv = sb("mv", [P, ITEMS, TILES + 1, 2])
        rstd = sb("rstd", [P, ITEMS, TILES + 1])
        tick = sb("tick", [1, 1])
        wk_now = sb("wk_now", [P, D])
        PS = ctx.enter_context(nc.psum_tensor("PS", [P, 8, BANK], F32))
        ARENA = 15744
        arena = sb("arena", [P, ITEMS, ARENA])
        spill_qk = nc.dram_tensor("spill_qk", [ITEMS, P, 2, 3, TOK], BF16).ap()
        spill_max = nc.dram_tensor("spill_max", [ITEMS, SH, TOK], BF16).ap()

        class Arena:
            def __init__(self):
                self.at = 0

            def __call__(self, *shape, parts=P, dt=F32):
                n = 1
                for s in shape:
                    n *= s
                words = n if dt == F32 else n // 2
                a = self.at
                self.at += words + words % 2
                assert self.at <= ARENA, self.at
                views = []
                for it in range(ITEMS):
                    v = arena[0:parts, it, a:a + words]
                    if dt != F32:
                        v = v.bitcast(dt)
                    if len(shape) == 2:
                        v = v.rearrange("p (a b) -> p a b", b=shape[1])
                    elif len(shape) == 3:
                        v = v.rearrange("p (a b c) -> p a b c", b=shape[1], c=shape[2])
                    elif len(shape) == 4:
                        v = v.rearrange("p (a b c d) -> p a b c d", b=shape[1], c=shape[2], d=shape[3])
                    views.append(v)
                return views

        def W(name):
            a, b = W_AT[name]
            return weights[:, a:b]

        def col(name, n=P):
            return cols[0:n, V_AT[name][0]:V_AT[name][1]]

        def neg(name):
            return neg_cols[:, V_AT[name][0]:V_AT[name][1]]

        def K(name):
            a, b = C_AT[name]
            return consts[:, a:b]

        def row(name):
            a, b = R_AT[name]
            return row_sb[:, a:b]

        ident = K("ident")
        one_row = K("ones")[0:1, 0:P]

        def bank(it, n, m=None):
            return PS[:, 4 * it + n, :] if m is None else PS[:, 4 * it + n:4 * it + m, :]

        def over(ap, dim, n):
            v = ap.unsqueeze(dim)
            shape = list(v.shape)
            shape[dim] = n
            return v.broadcast_to(shape)

        items = range(ITEMS)
        tiles = range(TILES)

        al = Arena()
        a_xT, a_qT, a_vT, a_sq, a_rn, a_kn, a_e1, a_e2, a_den, a_G, a_um = (al(TOK) for _ in range(11))
        a_D = al(6, P)
        a_E = al(6, P)
        a_Ep = al(4, P)
        a_UT = al(6, P)
        a_U = al(6, P)
        a_Am = al(IB, 2, 3 * P)
        a_yT = al(TOK)
        al = Arena()
        x_xn = al(TILES, D)
        x_cn = al(CC)
        x_xT = al(TOK)
        x_cT = al(P, parts=CC)
        x_qT = al(TOK)
        x_K = al(IB, BANK)
        x_V = al(IB, 4, P)
        x_P = al(TILES, BANK)
        x_mx = al(TILES, XH)
        x_sm = al(TILES, XH)
        x_rs = al(TILES, XH)
        x_PT = al(IB, 4, T)
        x_yT = al(TOK)
        al = Arena()
        g_xn = al(TILES, D)
        g_ss = al(TILES)
        g_r = al(TILES)
        g_xT = al(TOK)
        r_mx = al(TILES)
        r_lg = al(TILES, EXPERTS)
        r_E = al(TILES, EXPERTS)
        r_gt = al(TILES, EXPERTS, EXPERTS)
        r_eq = al(TILES, EXPERTS, EXPERTS)
        r_rank = al(TILES, EXPERTS)
        r_sel = al(TILES, EXPERTS)
        r_den = al(TILES)
        r_w = al(TILES, EXPERTS)
        r_end = al.at
        g_slot = al(TILES, EXPERTS)
        g_P = al(TILES, CAP)
        g_Pw = al(TILES, CAP)
        g_PwT = al(EXPERTS, TOK)
        g_o = al(EXPERTS, IB, P)
        g_xe = al(IB, CAP)
        g_v = al(IB, P)
        g_qk = al(2, IB, CAP)
        g_ln = al(2, BANK)
        g_sp = al(2, BANK)
        g_eqk = [a[:, 0] for a in g_ln]
        g_s = al(BANK)
        g_dec = al(BANK)
        g_inv = al(BANK)
        g_A = al(GH, IB, CAP)
        g_ok = g_eqk
        g_mx = al(IB * GH)
        g_rs = al(IB * GH)
        g_sT = al(IB, 2, CAP)
        g_qd = g_inv
        g_qT = al(IB, 2, CAP)
        g_onT = [a[:, 0] for a in g_sp]
        al = Arena()
        s_xT, s_qT, s_kT = al(TOK), al(TOK), al(TOK)
        s_v = al(TILES, D)
        s_S = al(TILES, T)
        s_mx = al(TILES)
        s_sum = al(TILES)
        s_rs = al(TILES)
        s_PT = al(IB, 2, T)
        al = Arena()
        al.at = r_end
        m_xT = al(TOK)
        m_qk = al(2, TOK)
        r_at = al.at
        m_r = al(2, TOK)
        m_parts = al(2, 3, TOK, dt=BF16)
        m_Q = al(SH, TOK, parts=STACK + 1, dt=BF16)
        m_K = al(SH, TOK, parts=STACK + 1, dt=BF16)
        m_V = al(TILES, SH, SD + 1)
        m_acc = al(TILES, D)
        m_mx = al(TILES, SH)
        row_at = al.at
        m_cT = al(TOK, parts=EXPERTS)
        m_rec = al(IB, HALF, SH)
        al.at = row_at
        m_row = al(TOK, parts=SH, dt=BF16)
        al.at = r_at
        m_P = al(2, 2, T)

        block = ctx.enter_context(nc.Block())

        @block.sync
        def _(sp):
            sp.sem_inc(S["stored"].sem, 1)
            for dst, src in ((weights[:], w_pack), (wctx[:], w_ctx), (cols[:], col_pack), (ccols[:], ctx_cols),
                             (consts[:], const_pack), (row_sb[:], rows), (bexp[:], b_experts)):
                sp.dma_start(dst, src).then_inc(S["consts_loaded"].sem, 16)

            def load_x(now, r):
                for it in items:
                    sp.dma_start(x_in[:, it].rearrange("p (b h) d -> p b h d", b=IB),
                                 x[bass.ds(r * (ITEMS * IB) + it * IB, IB)].rearrange("b (h p) d -> p b h d", p=P)
                                 ).then_inc(S[f"x_loaded{it}"].sem, 16)

            def load_context(now, r):
                for it in items:
                    sp.dma_start(ctx_k[:, it], ctx_tok[bass.ds(r * (ITEMS * P) + it * P, P)]
                                 ).then_inc(S["ctx_loaded"].sem, 16)
                    sp.dma_start(ctx_t[:, it], ctx_T[bass.ds(r * ITEMS + it, 1)].rearrange("a c n -> (a c) n")
                                 ).then_inc(S["ctx_loaded"].sem, 16)

            def one_round(now, ahead):
                if ahead:
                    sp.wait_ge(*S["x_free"].at(now, ITEMS))
                    load_x(now, now.round + 1)
                    if LAST > 1:
                        sp.wait_ge(*S["x_kv"].at(now, (2 if LAST > 4 else 1) * ITEMS))
                    load_context(now, now.round + 1)
                if LAST > 5:
                    for it in items:
                        sp.wait_ge(*S["m_split"].at(now, it + 1))
                        sp.dma_start(spill_qk[it], m_parts[it]).then_inc(*S[f"m_spilled{it}"].up(now, 16))
                    for it in items:
                        sp.wait_ge(*S[f"m_spilled{it}"].at(now, 16))
                        for t in range(TERMS):
                            for side, part, stack in ((0, t // 3, m_Q), (1, t % 3, m_K)):
                                src = spill_qk[it, :, side, part, :].rearrange("(h d) n -> d h n", d=SD)
                                sp.dma_start(stack[it][SD * t:SD * t + SD], src
                                             ).then_inc(*S["m_stacked"].up(now, 16))
                        sp.dma_start(m_K[it][STACK:STACK + 1], ones_row.rearrange("a (h n) -> a h n", h=SH)
                                     ).then_inc(*S["m_stacked"].up(now, 16))
                    for it in items:
                        sp.wait_ge(*S["m_row"].at(now, it + 1))
                        sp.dma_start(spill_max[it], m_row[it]).then_inc(*S[f"m_max_spilled{it}"].up(now, 16))
                    for it in items:
                        sp.wait_ge(*S[f"m_max_spilled{it}"].at(now, 16))
                        sp.dma_start(m_Q[it][STACK:STACK + 1], spill_max[it].rearrange("(a h) n -> a h n", a=1)
                                     ).then_inc(*S["m_max_stacked"].up(now, 16))
                for it in items:
                    sp.wait_ge(*S["x_made"].at(now, (LAST - 1) * ITEMS + it + 1))
                    sp.dma_start(out[bass.ds(now.round * (ITEMS * IB) + it * IB, IB)].rearrange("b (h p) d -> p b h d", p=P),
                                 xs[:, it].rearrange("p (b h) d -> p b h d", b=IB)
                                 ).then_inc(*S["stored"].up(now, 16))

            load_x(None, 0)
            load_context(None, 0)
            if ROUNDS > 1:
                with sp.Fori(0, ROUNDS - 1) as r:
                    one_round(Now(r), True)
                for s_ in S.all.values():
                    s_.frozen = True
            one_round(Now(ROUNDS - 1), False)
            sp.wait_ge(S["stored"].sem, 1 + ROUNDS * ITEMS * 16)
            for s_ in S.all.values():
                s_.frozen = False

        @block.tensor
        def _(pe):
            def transpose4(it, src, dst_bank):
                for t in tiles:
                    mm = pe.transpose(bank(it, dst_bank)[:, t * P:(t + 1) * P], src[:, t, :], ident)
                return mm

            def tokens_out(it, dst_bank, lhs, w, bias=None):
                for t in tiles:
                    o = bank(it, dst_bank)[:, t * P:(t + 1) * P]
                    mm = pe.matmul(o, lhsT=lhs[:, t * P:(t + 1) * P], rhs=w, start=True, stop=bias is None)
                    if bias is not None:
                        mm = pe.matmul(o, lhsT=one_row, rhs=bias, start=False, stop=True)
                return mm

            def linear_attention(now):
                for it in items:
                    pe.wait_ge(*S[f"x_loaded{it}"].at(now, 16))
                    pe.wait_ge(*S["x_made"].at(now, 0))
                    transpose4(it, x_in[:, it], 0).then_inc(*S["xT_made"].up(now))
                for it in items:
                    pe.wait_ge(*S["xT_kept"].at(now, it + 1))
                    for n, w in ((1, "a_wq"), (2, "a_wv"), (3, "a_wk")):
                        mm = pe.matmul(bank(it, n), lhsT=W(w), rhs=a_xT[it], start=True, stop=True)
                    mm.then_inc(*S["a_qkv"].up(now))
                for it in items:
                    pe.wait_ge(*S["a_sq"].at(now, it + 1))
                    pe.matmul(bank(it, 0), lhsT=K("head_sum"), rhs=a_sq[it], start=True, stop=True
                              ).then_inc(*S["a_ss"].up(now))
                for it in items:
                    pe.wait_ge(*S["a_UT"].at(now, it + 1))
                    for n in range(6):
                        mm = pe.transpose(bank(it, n // 4)[:, n % 4 * P:(n % 4 + 1) * P], a_UT[it][:, n], ident)
                    mm.then_inc(*S["a_U"].up(now))
                for b in range(IB):
                    for it in items:
                        if b:
                            pe.wait_ge(*S["a_Am"].at(now, it + 1))
                        else:
                            pe.wait_ge(*S["a_qv_kept"].at(now, it + 1))
                        for part, (s0, t0, n) in enumerate(((0, 0, 2), (1, 1, 1))):
                            for h in range(2):
                                lanes = slice(64 * h, 64 * h + 64)
                                s = (b * HALF + s0) * P
                                t = (b * HALF + t0) * P
                                mm = pe.matmul(bank(it, 2 + h)[:, 256 * part:256 * part + n * P],
                                               lhsT=a_vT[it][lanes, s:s + P], rhs=a_qT[it][lanes, t:t + n * P],
                                               start=True, stop=True)
                        mm.then_inc(*S["a_A"].up(now))
                for it in items:
                    pe.wait_ge(*S["a_U_kept"].at(now, it + 1))
                    pe.wait_ge(*S["a_Am"].at(now, ITEMS + it + 1))
                    for b in range(IB):
                        for h in range(2):
                            lanes = slice(64 * h, 64 * h + 64)
                            A = a_Am[it][:, b, h]

                            def U(n):
                                return a_U[it][:, n, lanes]
                            first = bank(it, 0)[lanes, b * T:b * T + P]
                            second = bank(it, 0)[lanes, b * T + P:(b + 1) * T]
                            pe.matmul(first, lhsT=U(2 * b), rhs=A[:, 0:P], start=True, stop=True)
                            pe.matmul(second, lhsT=U(4 + b), rhs=A[:, P:2 * P], start=True, stop=False)
                            mm = pe.matmul(second, lhsT=U(2 * b + 1), rhs=A[:, 2 * P:], start=False, stop=True)
                    mm.then_inc(*S["a_y"].up(now))
                for it in items:
                    pe.wait_ge(*S["a_yT"].at(now, it + 1))
                    tokens_out(it, 1, a_yT[it], W("a_wo")).then_inc(*S["y_made"].up(now))

            def cross_attention(now, s, c):
                for it in items:
                    if c:
                        pe.wait_ge(*S["l_made"].at(now, it + 1))
                        transpose4(it, x_xn[it], 0)
                        pe.transpose(bank(it, 1)[0:CC, 0:P], x_cn[it], ident).then_inc(*S["xT_made"].up(now))
                    else:
                        pe.wait_ge(*S["x_made"].at(now, (s - 1) * ITEMS + it + 1))
                        transpose4(it, xs[:, it], 0).then_inc(*S["xT_made"].up(now))
                wk, wv = (wctx[:, (2 * c + n) * D:(2 * c + n + 1) * D] for n in range(2))
                pe.wait_ge(*S["ctx_loaded"].at(now, ITEMS * 32))
                for it in items:
                    cT = x_cT[it] if c else ctx_t[:, it]
                    pe.wait_ge(*S["xT_kept"].at(now, s * ITEMS + it + 1))
                    pe.matmul(bank(it, 1)[:, 0:P], lhsT=wk, rhs=cT, start=True, stop=True)
                    for b in range(IB):
                        for half in range(2):
                            mm = pe.matmul(bank(it, 3)[64 * half:64 * half + 64, b * D:(b + 1) * D],
                                           lhsT=cT[:, b * KV:(b + 1) * KV], rhs=wv, start=True, stop=True)
                    mm.then_inc(*S["x_kv"].up(now))
                    pe.matmul(bank(it, 2), lhsT=W(f"x{c}_wq"), rhs=x_xT[it], start=True, stop=True
                              ).then_inc(*S["x_q"].up(now))
                for b in range(IB):
                    for it in items:
                        pe.wait_ge(*S["x_q_kept"].at(now, c * ITEMS + it + 1))
                        pe.wait_ge(*S["x_kv_kept"].at(now, c * ITEMS + it + 1))
                        for t in range(HALF * b, HALF * b + HALF):
                            mm = pe.matmul(bank(it, t), lhsT=x_qT[it][:, t * P:(t + 1) * P], rhs=x_K[it][:, b],
                                           start=True, stop=True)
                        mm.then_inc(*S["x_scores"].up(now))
                for b in range(IB):
                    for it in items:
                        pe.wait_ge(*S["x_norm"].at(now, (c * IB + b) * ITEMS + it + 1))
                        for h in range(4):
                            for t in range(HALF):
                                o = bank(it, 2 * b + h // 2)[:, h % 2 * T + t * P:h % 2 * T + (t + 1) * P]
                                mm = pe.transpose(o, x_P[it][:, HALF * b + t, h * P:(h + 1) * P], ident)
                        mm.then_inc(*S["x_PT"].up(now))
                for it in items:
                    for b in range(IB):
                        pe.wait_ge(*S["x_PT_kept"].at(now, (c * IB + b) * ITEMS + it + 1))
                        for h in range(4):
                            mm = pe.matmul(bank(it, 0)[:, b * T:(b + 1) * T], lhsT=x_V[it][:, b, h],
                                           rhs=x_PT[it][:, b, h], start=(h == 0), stop=(h == 3))
                    mm.then_inc(*S["x_o"].up(now))
                for it in items:
                    pe.wait_ge(*S["x_o_kept"].at(now, c * ITEMS + it + 1))
                    tokens_out(it, 1, x_yT[it], W(f"x{c}_wo"), None if c else row("bo")).then_inc(*S["y_made"].up(now))

            def experts(now):
                for it in items:
                    pe.wait_ge(*S["g_xn"].at(now, it + 1))
                    transpose4(it, g_xn[it], 0).then_inc(*S["xT_made"].up(now))
                for it in items:
                    pe.wait_ge(*S["xT_kept"].at(now, 2 * ITEMS + it + 1))
                    for t in tiles:
                        mm = pe.matmul(bank(it, 1)[:, t * EXPERTS:(t + 1) * EXPERTS],
                                       lhsT=g_xT[it][:, t * P:(t + 1) * P], rhs=W("g_wg"), start=True, stop=True)
                    mm.then_inc(*S["logits"].up(now))
                for it in items:
                    pe.wait_ge(*S["sel_made"].at(now, it + 1))
                    for t in tiles:
                        o = bank(it, 2)[:, t * EXPERTS:(t + 1) * EXPERTS]
                        mm = pe.matmul(o, lhsT=K("suffix"), rhs=r_sel[it][:, t], start=True, stop=t % 2 == 1)
                        if t % 2 == 0:
                            mm = pe.matmul(o, lhsT=K("ones")[:, 0:P], rhs=r_sel[it][:, t + 1], start=False, stop=True)
                    mm.then_inc(*S["g_count"].up(now))
                with pe.Fori(0, EXPERTS) as e:
                    expert_step(now.inner(e, EXPERTS), e)
                for it in items:
                    pe.wait_ge(*S[f"g_o{it}"].at(now, EXPERTS))
                    for t in tiles:
                        for e in range(EXPERTS):
                            mm = pe.matmul(bank(it, 0)[:, t * P:(t + 1) * P],
                                           lhsT=g_PwT[it][:, e, t * P:(t + 1) * P], rhs=g_o[it][:, e, t // HALF],
                                           start=(e == 0), stop=(e == EXPERTS - 1))
                    mm.then_inc(*S["g_out"].up(now))
                for it in items:
                    pe.wait_ge(*S["g_on"].at(now, it + 1))
                    transpose4(it, g_xn[it], 1).then_inc(*S["g_onT"].up(now))
                for it in items:
                    pe.wait_ge(*S["g_onT_kept"].at(now, it + 1))
                    tokens_out(it, 2, g_onT[it], W("g_wo")).then_inc(*S["y_made"].up(now))

            def expert_step(now, e):
                for it in items:
                    pe.wait_ge(*S["g_place"].at(now, it + 1))
                    pe.wait_ge(*S[f"g_o{it}"].at(now, 0))
                    for t in tiles:
                        pe.transpose(bank(it, 0)[:, t * P:(t + 1) * P], g_Pw[it][:, t], ident)
                    for b in range(IB):
                        for t in range(HALF):
                            mm = pe.matmul(bank(it, 1)[:, b * CAP:(b + 1) * CAP], lhsT=g_xn[it][:, HALF * b + t],
                                           rhs=g_P[it][:, HALF * b + t], start=(t == 0), stop=(t == HALF - 1))
                    mm.then_inc(*S["g_xe"].up(now))
                for it in items:
                    pe.wait_ge(*S["g_xe_kept"].at(now, it + 1))
                    if it == 0:
                        pe.wait_ge(*S["g_wk"].at(now, 1))
                    xe = g_xe[it].rearrange("p b s -> p (b s)")
                    pe.matmul(bank(it, 2)[:, 0:IB * CAP], lhsT=W("g_wq"), rhs=xe, start=True, stop=True)
                    pe.matmul(bank(it, 2)[:, IB * CAP:], lhsT=wk_now[:], rhs=xe, start=True, stop=True)
                    for b in range(IB):
                        mm = pe.matmul(bank(it, 3)[:, b * GH * GM:(b + 1) * GH * GM], lhsT=g_xe[it][:, b],
                                       rhs=W("g_wf")[:, bass.ds(e * (GH * GM), GH * GM)], start=True, stop=True)
                    mm.then_inc(*S["g_qkf_made"].up(now))
                    pe.wait_ge(*S["g_PwT_kept"].at(now, it + 1))
                    for b in range(IB):
                        mm = pe.matmul(bank(it, 0)[:, b * P:(b + 1) * P], lhsT=g_xe[it][:, b],
                                       rhs=W("g_wv")[:, bass.ds(e * D, D)], start=True, stop=True)
                    mm.then_inc(*S["g_v_made"].up(now))
                for it in items:
                    pe.wait_ge(*S["g_sp"].at(now, it + 1))
                    pe.matmul(bank(it, 1), lhsT=K("mid_sum"), rhs=g_sp[it][:, 1], start=True, stop=True
                              ).then_inc(*S["g_decay"].up(now))
                for it in items:
                    pe.wait_ge(*S["g_dec"].at(now, it + 1))
                    pe.wait_ge(*S["g_qk"].at(now, it + 1))
                    for b in range(IB):
                        for h in range(GH):
                            lanes = slice(GK * h, GK * h + GK)
                            mm = pe.matmul(bank(it, h)[:, b * CAP:(b + 1) * CAP], lhsT=g_qk[it][lanes, 1, b],
                                           rhs=g_qk[it][lanes, 0, b], start=True, stop=True)
                    mm.then_inc(*S["g_A"].up(now))
                for it in items:
                    pe.wait_ge(*S["g_Am"].at(now, it + 1))
                    pe.wait_ge(*S["g_s"].at(now, it + 1))
                    for b in range(IB):
                        for h in range(GH):
                            at = (b * GH + h) * GM
                            pe.matmul(bank(it, 0)[:, at:at + GM], lhsT=g_A[it][:, h, b], rhs=g_s[it][:, at:at + GM],
                                      start=True, stop=True)
                    for n in range(4):
                        mm = pe.transpose(bank(it, 1)[:, n * P:(n + 1) * P], g_s[it][:, n * P:(n + 1) * P], ident)
                    mm.then_inc(*S["g_ok"].up(now))
                for it in items:
                    pe.wait_ge(*S["g_qd"].at(now, it + 1))
                    for n in range(4):
                        mm = pe.transpose(bank(it, 2)[:, n * P:(n + 1) * P], g_qd[it][:, n * P:(n + 1) * P], ident)
                    mm.then_inc(*S["g_qdT"].up(now))
                for it in items:
                    pe.wait_ge(*S["g_qdT_kept"].at(now, it + 1))
                    for b in range(IB):
                        for h in range(GH):
                            lanes = slice(64 * (h % 2), 64 * (h % 2) + 64)
                            mm = pe.matmul(bank(it, h)[:, b * CAP:(b + 1) * CAP], lhsT=g_sT[it][lanes, b, h // 2],
                                           rhs=g_qT[it][lanes, b, h // 2], start=True, stop=True)
                    mm.then_inc(*S["g_T"].up(now))
                for it in items:
                    pe.wait_ge(*S["g_Tm"].at(now, it + 1))
                    for b in range(IB):
                        for h in range(GH):
                            at = b * P + h * GK
                            mm = pe.matmul(bank(it, 0)[:, at:at + GK], lhsT=g_A[it][:, h, b],
                                           rhs=g_v[it][:, b, h * GK:(h + 1) * GK], start=True, stop=True)
                    mm.then_inc(*S["g_ov"].up(now))

            def self_attention(now):
                for it in items:
                    pe.wait_ge(*S["x_made"].at(now, 2 * ITEMS + it + 1))
                    transpose4(it, xs[:, it], 0).then_inc(*S["xT_made"].up(now))
                for it in items:
                    pe.wait_ge(*S["xT_kept"].at(now, 3 * ITEMS + it + 1))
                    for n, w in ((1, "s_wq"), (2, "s_wk")):
                        pe.matmul(bank(it, n), lhsT=W(w), rhs=s_xT[it], start=True, stop=True)
                    tokens_out(it, 3, s_xT[it], W("s_wv"), row("s_bv")).then_inc(*S["s_qkv"].up(now))
                for it in items:
                    pe.wait_ge(*S["s_q"].at(now, it + 1))
                    pe.wait_ge(*S["s_kv"].at(now, it + 1))
                    for t in tiles:
                        b = t // HALF
                        mm = pe.matmul(bank(it, b)[:, t % HALF * T:(t % HALF + 1) * T],
                                       lhsT=s_qT[it][:, t * P:(t + 1) * P], rhs=s_kT[it][:, b * T:(b + 1) * T],
                                       start=True, stop=True)
                    mm.then_inc(*S["s_scores"].up(now))
                for it in items:
                    pe.wait_ge(*S["s_exp"].at(now, it + 1))
                    for t in tiles:
                        b = t // HALF
                        for k in range(HALF):
                            o = bank(it, 2 + b)[:, k * T + t % HALF * P:k * T + (t % HALF + 1) * P]
                            mm = pe.transpose(o, s_S[it][:, t, k * P:(k + 1) * P], ident)
                    mm.then_inc(*S["s_PT"].up(now))
                for it in items:
                    pe.wait_ge(*S["s_PT_kept"].at(now, it + 1))
                    for t in tiles:
                        b = t // HALF
                        for k in range(HALF):
                            mm = pe.matmul(bank(it, 0)[:, t * P:(t + 1) * P],
                                           lhsT=s_PT[it][:, b, k, t % HALF * P:(t % HALF + 1) * P],
                                           rhs=s_v[it][:, HALF * b + k], start=(k == 0), stop=(k == HALF - 1))
                    mm.then_inc(*S["y_made"].up(now))

            def heads_and_experts(now):
                for it in items:
                    pe.wait_ge(*S["x_made"].at(now, 4 * ITEMS + it + 1))
                    transpose4(it, xs[:, it], 0).then_inc(*S["xT_made"].up(now))
                for it in items:
                    pe.wait_ge(*S["xT_kept"].at(now, 5 * ITEMS + it + 1))
                    for n, w in ((1, "m_wq"), (2, "m_wk")):
                        pe.matmul(bank(it, n), lhsT=W(w), rhs=m_xT[it], start=True, stop=True)
                    tokens_out(it, 3, m_xT[it], W("m_wv"), row("m_bv")).then_inc(*S["m_qkv"].up(now))
                    for t in tiles:
                        o = bank(it, 0)[:, t * EXPERTS:(t + 1) * EXPERTS]
                        pe.matmul(o, lhsT=m_xT[it][:, t * P:(t + 1) * P], rhs=W("m_wg"), start=True, stop=False)
                        mm = pe.matmul(o, lhsT=one_row, rhs=row("m_bg"), start=False, stop=True)
                    mm.then_inc(*S["logits"].up(now))
                for it in items:
                    pe.wait_ge(*S["w_made"].at(now, ITEMS + it + 1))
                    pe.wait_ge(*S["m_qkv_kept"].at(now, it + 1))
                    for t in tiles:
                        mm = pe.transpose(bank(it, 3)[0:EXPERTS, t * P:(t + 1) * P], r_w[it][:, t], ident)
                    mm.then_inc(*S["m_wT"].up(now))
                for it in items:
                    pe.wait_ge(*S["m_wT_kept"].at(now, it + 1))
                    tokens_out(it, 2, m_cT[it], bexp[:]).then_inc(*S["m_bias"].up(now))
                for t in tiles:
                    for it in items:
                        if t:
                            pe.wait_ge(*S["m_moe_read"].at(now, (t - 1) * ITEMS + it + 1))
                        for n in range(2):
                            mm = pe.matmul(bank(it, n), lhsT=m_xT[it][:, t * P:(t + 1) * P],
                                           rhs=W("m_we")[:, n * BANK:(n + 1) * BANK], start=True, stop=True)
                        mm.then_inc(*S["m_moe"].up(now))
                with pe.Fori(0, QUADS) as q:
                    inner = now.inner(q, QUADS)
                    pe.wait_ge(*S["m_stacked"].at(now, ITEMS * 16 * (2 * TERMS + 1)))
                    pe.wait_ge(*S["m_moe_read"].at(now, TILES * ITEMS))
                    for t in tiles:
                        for it in items:
                            if t < 2:
                                pe.wait_ge(*S["m_max_read"].at(inner, 0))
                            else:
                                pe.wait_ge(*S["m_max_read"].at(inner, (t - 2) * ITEMS + it + 1))
                            b = t // HALF
                            for h in range(4):
                                mm = pe.matmul(bank(it, 2 * (t % 2) + h // 2)[:, h % 2 * T:(h % 2 + 1) * T],
                                               lhsT=m_Q[it][0:STACK, bass.ds(q * 4 + h, 1), t * P:(t + 1) * P
                                                            ].rearrange("p a n -> p (a n)"),
                                               rhs=m_K[it][0:STACK, bass.ds(q * 4 + h, 1), b * T:(b + 1) * T
                                                           ].rearrange("p a n -> p (a n)"),
                                               start=True, stop=True)
                            mm.then_inc(*S["m_max_scores"].up(inner))
                for it in items:
                    pe.wait_ge(*S["m_max_read"].at(now, QUADS * TILES * ITEMS))
                    for t in tiles:
                        mm = pe.transpose(bank(it, 0)[0:SH, t * P:(t + 1) * P], m_mx[it][:, t], ident)
                    mm.then_inc(*S["m_mxT"].up(now))
                with pe.Fori(0, PAIRS) as q:
                    inner = now.inner(q, PAIRS)
                    pe.wait_ge(*S["m_max_stacked"].at(now, ITEMS * 16))
                    for b in range(IB):
                        for it in items:
                            if b:
                                pe.wait_ge(*S["m_exp"].at(inner, it + 1))
                            else:
                                pe.wait_ge(*S["m_exp"].at(inner, 0))
                            for h in range(2):
                                for k in range(HALF):
                                    at = b * T + k * P
                                    mm = pe.matmul(bank(it, h)[:, k * T:(k + 1) * T],
                                                   lhsT=m_K[it][:, bass.ds(q * 2 + h, 1), at:at + P
                                                                ].rearrange("p a n -> p (a n)"),
                                                   rhs=m_Q[it][:, bass.ds(q * 2 + h, 1), b * T:(b + 1) * T
                                                               ].rearrange("p a n -> p (a n)"),
                                                   start=True, stop=True)
                            mm.then_inc(*S["m_scores"].up(inner))
                        for it in items:
                            pe.wait_ge(*S["m_exp"].at(inner, b * ITEMS + it + 1))
                            for h in range(2):
                                for t in range(HALF):
                                    o = bank(it, 2 + b)[:, bass.ds(t * SH * (SD + 1) + (q * 2 + h) * (SD + 1), SD + 1)]
                                    for k in range(HALF):
                                        mm = pe.matmul(o, lhsT=m_P[it][:, h, k, t * P:(t + 1) * P],
                                                       rhs=m_V[it][:, HALF * b + k, bass.ds(q * 2 + h, 1), :
                                                                   ].rearrange("p a n -> p (a n)"),
                                                       start=(k == 0), stop=(k == HALF - 1))
                            mm.then_inc(*S["m_pv"].up(inner))

            pe.sem_inc(S["g_xe"].sem, 1)
            pe.sem_inc(S["g_qkf_made"].sem, 1)
            pe.sem_inc(S["m_pv"].sem, 1)
            pe.wait_ge(S["consts_loaded"].sem, 16 * 7)
            with pe.Fori(0, ROUNDS) as r:
                now = Now(r)
                linear_attention(now)
                if LAST > 1:
                    cross_attention(now, 1, 0)
                if LAST > 2:
                    experts(now)
                if LAST > 3:
                    self_attention(now)
                if LAST > 4:
                    cross_attention(now, 4, 1)
                if LAST > 5:
                    heads_and_experts(now)

        @block.scalar
        def _(act):
            act.preload_act_table_set("natural_log_exp_and_others")
            act.sem_inc(S["m_exp"].sem, 1)
            act.wait_ge(S["consts_loaded"].sem, 16 * 7)

            def power(own, out_, in_, scale, bias):
                act.activation(out_, in_, ACT.Ln, scale=scale, bias=bias).then_inc(*own.next())
                act.wait_ge(*own.all())
                return act.activation(out_, out_, ACT.Exp, scale=-0.5)

            def layernorm(own, now, s):
                for it in items:
                    act.wait_ge(*S["var_made"].at(now, s * ITEMS + it + 1))
                    power(own, rstd[:, it, 0:TILES], mv[:, it, 0:TILES, 1], 1.0, EPS
                          ).then_inc(*S["rstd_made"].up(now))

            def keep_xT(now, s, dst, scale=1.0, bias=0.0):
                for it in items:
                    act.wait_ge(*S["xT_made"].at(now, s * ITEMS + it + 1))
                    act.activation(dst[it], bank(it, 0), ACT.Identity, scale=scale, bias=bias
                                   ).then_inc(*S["xT_kept"].up(now))

            def linear_attention(own, now):
                keep_xT(now, 0, a_xT)
                for it in items:
                    act.wait_ge(*S["a_qkv"].at(now, it + 1))
                    act.activation(a_sq[it], bank(it, 3), ACT.Square).then_inc(*S["a_sq"].up(now))
                    act.activation(a_qT[it], bank(it, 1), ACT.Copy)
                    act.activation(a_vT[it], bank(it, 2), ACT.Copy).then_inc(*S["a_qv_kept"].up(now))
                for it in items:
                    act.wait_ge(*S["a_ss_kept"].at(now, it + 1))
                    act.activation(a_rn[it], a_rn[it], ACT.Ln).then_inc(*own.next())
                    act.wait_ge(*own.all())
                    act.activation(a_rn[it], a_rn[it], ACT.Exp, scale=-0.5).then_inc(*S["a_rn"].up(now))
                for it in items:
                    act.wait_ge(*S["a_kn"].at(now, it + 1))
                    act.activation(a_e1[it], a_kn[it], ACT.Exp, scale=neg("a_wgamma"), bias=neg("a_bgamma"))
                    act.activation(a_e2[it], a_kn[it], ACT.Exp, scale=col("a_wlambda"), bias=col("a_blambda")
                                   ).then_inc(*S["a_e"].up(now))
                for it in items:
                    act.wait_ge(*S["a_den"].at(now, it + 1))
                    act.activation(a_e1[it], a_den[it], ACT.Ln).then_inc(*S["a_L"].up(now))
                for it in items:
                    act.wait_ge(*S["a_D"].at(now, it + 1))
                    act.activation(a_E[it], a_D[it], ACT.Exp).then_inc(*S["a_E"].up(now))
                    act.activation(a_Ep[it], a_D[it][:, 0:4], ACT.Exp, scale=-1.0).then_inc(*S["a_Ep"].up(now))
                for it in items:
                    act.wait_ge(*S["a_U"].at(now, it + 1))
                    act.activation(a_U[it][:, 0:4], bank(it, 0).rearrange("p (a b) -> p a b", b=P), ACT.Copy)
                    act.activation(a_U[it][:, 4:6], bank(it, 1)[:, 0:2 * P].rearrange("p (a b) -> p a b", b=P), ACT.Copy
                                   ).then_inc(*S["a_U_kept"].up(now))
                layernorm(own, now, 0)

            def cross_attention(own, now, s, c):
                if c:
                    for it in items:
                        act.wait_ge(*S["l_var"].at(now, it + 1))
                        power(own, rstd[:, it], mv[:, it, :, 1], 1.0, EPS).then_inc(*S["l_rstd"].up(now))
                    for it in items:
                        act.wait_ge(*S["xT_made"].at(now, s * ITEMS + it + 1))
                        act.activation(x_cT[it], bank(it, 1)[0:CC, 0:P], ACT.Identity, scale=ccols[:, 0:1],
                                       bias=ccols[:, 1:2])
                        act.activation(x_xT[it], bank(it, 0), ACT.Identity, scale=col("lat_g"), bias=col("lat_b")
                                       ).then_inc(*S["xT_kept"].up(now))
                else:
                    keep_xT(now, s, x_xT)
                for it in items:
                    act.wait_ge(*S["x_q"].at(now, c * ITEMS + it + 1))
                    act.activation(x_qT[it], bank(it, 2), ACT.Copy).then_inc(*S["x_q_kept"].up(now))
                for b in range(IB):
                    for it in items:
                        act.wait_ge(*S["x_less_max"].at(now, (c * IB + b) * ITEMS + it + 1))
                        p = x_P[it][:, HALF * b:HALF * (b + 1)]
                        act.activation(p, p, ACT.Exp, scale=float(XD) ** -0.5).then_inc(*S["x_exp"].up(now))
                for b in range(IB):
                    for it in items:
                        act.wait_ge(*S["x_PT"].at(now, (c * IB + b) * ITEMS + it + 1))
                        act.activation(x_PT[it][:, b].rearrange("p (a h) t -> p a (h t)", a=2),
                                       bank(it, 2 * b, 2 * b + 2), ACT.Copy).then_inc(*S["x_PT_kept"].up(now))
                for it in items:
                    act.wait_ge(*S["x_o"].at(now, c * ITEMS + it + 1))
                    act.activation(x_yT[it], bank(it, 0), ACT.Copy).then_inc(*S["x_o_kept"].up(now))
                layernorm(own, now, s)

            def rms(own, now, it, src, done):
                for t in tiles:
                    act.activation(g_s[it][:, t * P:(t + 1) * P], src[:, t * P:(t + 1) * P], ACT.Square,
                                           accum_out=g_ss[it][:, t:t + 1]).then_inc(*own.next())
                act.wait_ge(*own.all())
                power(own, g_r[it], g_ss[it], 1.0 / D, EPS).then_inc(*S[done].up(now))

            def experts(own, now):
                for it in items:
                    act.wait_ge(*S["x_made"].at(now, ITEMS + it + 1))
                    rms(own, now, it, xs[:, it].rearrange("p t d -> p (t d)"), "g_rms")
                keep_xT(now, 2, g_xT, scale=col("g_norm"))
                for it in items:
                    act.wait_ge(*S["less_max"].at(now, it + 1))
                    act.activation(r_E[it], r_lg[it], ACT.Exp).then_inc(*S["gate_exp"].up(now))
                with act.Fori(0, EXPERTS) as e:
                    expert_step(now.inner(e, EXPERTS), e)
                for it in items:
                    act.wait_ge(*S["g_out"].at(now, it + 1))
                    rms(own, now, it, bank(it, 0), "g_rms")
                for it in items:
                    act.wait_ge(*S["g_onT"].at(now, it + 1))
                    act.activation(g_onT[it], bank(it, 1), ACT.Copy, scale=col("g_gnorm")
                                   ).then_inc(*S["g_onT_kept"].up(now))
                layernorm(own, now, 2)

            def expert_step(now, e):
                act.wait_ge(*S["g_qkf_made"].at(now, 0))
                act.activation(wk_now[:], W("g_wk")[:, bass.ds(e * D, D)], ACT.Copy).then_inc(*S["g_wk"].up(now))
                for it in items:
                    act.wait_ge(*S["g_xe"].at(now, it + 1))
                    act.activation(g_xe[it].rearrange("p b s -> p (b s)"), bank(it, 1)[:, 0:IB * CAP], ACT.Copy,
                                   scale=col("g_norm")).then_inc(*S["g_xe_kept"].up(now))
                    act.activation(g_PwT[it][:, bass.ds(e, 1)].rearrange("p a n -> p (a n)"), bank(it, 0), ACT.Copy
                                   ).then_inc(*S["g_PwT_kept"].up(now))
                for it in items:
                    act.wait_ge(*S["g_qkf_made"].at(now, it + 1))
                    act.activation(g_ln[it], bank(it, 2, 4), ACT.Exp, scale=-1.0).then_inc(*S["g_exp"].up(now))
                    act.wait_ge(*S["g_v_made"].at(now, it + 1))
                    act.activation(g_v[it].rearrange("p b d -> p (b d)"), bank(it, 0)[:, 0:IB * P], ACT.Copy
                                   ).then_inc(*S["g_v"].up(now))
                for it in items:
                    act.wait_ge(*S["g_exp_cut"].at(now, it + 1))
                    act.activation(g_ln[it], g_ln[it], ACT.Ln, bias=1.0).then_inc(*S["g_ln"].up(now))
                for it in items:
                    act.wait_ge(*S["g_sp"].at(now, it + 1))
                    act.activation(g_eqk[it], g_sp[it][:, 0], ACT.Exp, scale=-1.0).then_inc(*S["g_sig"].up(now))
                    act.activation(g_s[it], g_sp[it][:, 1], ACT.Exp, scale=-1.0 / GATE_NORM)
                for it in items:
                    act.wait_ge(*S["g_decay"].at(now, it + 1))
                    act.activation(g_inv[it], bank(it, 1), ACT.Exp, scale=1.0 / GATE_NORM)
                    act.activation(g_dec[it], bank(it, 1), ACT.Exp, scale=-1.0 / GATE_NORM
                                   ).then_inc(*S["g_dec"].up(now))
                for it in items:
                    act.wait_ge(*S["g_ok"].at(now, it + 1))
                    act.activation(g_sT[it].rearrange("p b a n -> p (b a n)"), bank(it, 1), ACT.Copy
                                   ).then_inc(*S["g_sT"].up(now))
                for it in items:
                    act.wait_ge(*S["g_less_max"].at(now, it + 1))
                    act.activation(g_ok[it], g_ok[it], ACT.Exp).then_inc(*S["g_p"].up(now))
                for it in items:
                    act.wait_ge(*S["g_qdT"].at(now, it + 1))
                    act.activation(g_qT[it].rearrange("p b a n -> p (b a n)"), bank(it, 2), ACT.Copy
                                   ).then_inc(*S["g_qdT_kept"].up(now))

            def self_attention(own, now):
                keep_xT(now, 3, s_xT)
                for it in items:
                    act.wait_ge(*S["s_qkv"].at(now, it + 1))
                    act.activation(s_kT[it], bank(it, 2), ACT.Identity, bias=col("s_bk"))
                    act.activation(s_v[it].rearrange("p t d -> p (t d)"), bank(it, 3), ACT.Copy
                                   ).then_inc(*S["s_kv"].up(now))
                for it in items:
                    act.wait_ge(*S["s_max"].at(now, it + 1))
                    for t in tiles:
                        e = act.activation(s_S[it][:, t], s_S[it][:, t], ACT.Exp, bias=s_mx[it][:, t:t + 1],
                                           accum_out=s_sum[it][:, t:t + 1])
                    e.then_inc(*S["s_exp"].up(now))
                for it in items:
                    act.wait_ge(*S["s_PT"].at(now, it + 1))
                    act.activation(s_PT[it].rearrange("p b k t -> p b (k t)"), bank(it, 2, 4), ACT.Copy
                                   ).then_inc(*S["s_PT_kept"].up(now))
                layernorm(own, now, 3)

            def heads_and_experts(own, now):
                keep_xT(now, 5, m_xT)
                for it in items:
                    act.wait_ge(*S["m_qkv"].at(now, it + 1))
                    for side, b in ((0, "m_bq"), (1, "m_bk")):
                        act.activation(m_parts[it][:, side, 0], bank(it, 1 + side), ACT.Identity, bias=col(b))
                        i = act.activation(m_qk[it][:, side], bank(it, 1 + side), ACT.Identity, bias=col(b))
                    i.then_inc(*S["m_qk"].up(now))
                    for t in tiles:
                        e = act.activation(m_V[it][:, t, :, 0:SD],
                                           bank(it, 3)[:, t * P:(t + 1) * P].rearrange("p (h d) -> p h d", d=SD),
                                           ACT.Copy)
                    e.then_inc(*S["m_qkv_kept"].up(now))
                for it in items:
                    act.wait_ge(*S["less_max"].at(now, ITEMS + it + 1))
                    act.activation(r_E[it], r_lg[it], ACT.Exp).then_inc(*S["gate_exp"].up(now))
                for it in items:
                    act.wait_ge(*S["m_wT"].at(now, it + 1))
                    act.activation(m_cT[it], bank(it, 3)[0:EXPERTS], ACT.Copy).then_inc(*S["m_wT_kept"].up(now))
                for it in items:
                    act.wait_ge(*S["m_mxT"].at(now, it + 1))
                    act.activation(m_row[it], bank(it, 0)[0:SH], ACT.Copy, scale=-1.0).then_inc(*S["m_row"].up(now))
                with act.Fori(0, PAIRS) as q:
                    inner = now.inner(q, PAIRS)
                    for b in range(IB):
                        for it in items:
                            act.wait_ge(*S["m_scores"].at(inner, b * ITEMS + it + 1))
                            if b:
                                act.wait_ge(*S["m_pv"].at(inner, it + 1))
                            else:
                                act.wait_ge(*S["m_pv"].at(inner, 0))
                            act.activation(m_P[it].rearrange("p h k t -> p h (k t)"), bank(it, 0, 2), ACT.Exp,
                                           scale=float(SD) ** -0.5).then_inc(*S["m_exp"].up(inner))
                layernorm(own, now, 5)

            with act.Fori(0, ROUNDS) as r:
                now = Now(r)
                own = Own(S["act_own"], now)
                linear_attention(own, now)
                if LAST > 1:
                    cross_attention(own, now, 1, 0)
                if LAST > 2:
                    experts(own, now)
                if LAST > 3:
                    self_attention(own, now)
                if LAST > 4:
                    cross_attention(own, now, 4, 1)
                if LAST > 5:
                    heads_and_experts(own, now)

        @block.vector
        def _(v):
            def stats_of(own, out_, mv_, src):
                v.bn_stats(out_, src).then_inc(*own.next())

            def normalise(own, now, s):
                for it in items:
                    for t in tiles:
                        v.bn_stats(stats[:, it, t], zs[:, it, t]).then_inc(*own.next())
                    v.wait_ge(*own.all())
                    v.memset(tick[:], 0.0)
                    for t in tiles:
                        i = v.bn_aggr(mv[:, it, t], stats[:, it, t])
                    i.then_inc(*S["var_made"].up(now))
                for it in items:
                    v.wait_ge(*S["rstd_made"].at(now, s * ITEMS + it + 1))
                    if s == 0:
                        v.wait_ge(*S["stored"].at(now, 0))
                    for t in tiles:
                        i = v.tensor_scalar(xs[:, it, t], zs[:, it, t], mv[:, it, t, 0:1], rstd[:, it, t:t + 1],
                                            ALU.subtract, ALU.mult)
                    i.then_inc(*S["x_made"].up(now))

            def layernorm(own, now, s, y_bank):
                for it in items:
                    v.wait_ge(*S["y_made"].at(now, s * ITEMS + it + 1 if s < 5 else 0))
                    x_old = x_in if s == 0 else xs
                    i = v.tensor_tensor(zs[:, it].rearrange("p t d -> p (t d)"), bank(it, y_bank),
                                        x_old[:, it].rearrange("p t d -> p (t d)"), ALU.add)
                    if s == 0:
                        i.then_inc(*S["x_free"].up(now))
                        v.wait_ge(*S["x_free"].at(now, it + 1))
                    else:
                        i.then_inc(*own.next())
                        v.wait_ge(*own.all())
                normalise(own, now, s)

            def linear_attention(own, now):
                for it in items:
                    v.wait_ge(*S["a_ss"].at(now, it + 1))
                    v.tensor_scalar(a_rn[it], bank(it, 0), 1e-24, 1e12, ALU.max, ALU.mult
                                    ).then_inc(*S["a_ss_kept"].up(now))
                for it in items:
                    v.wait_ge(*S["a_rn"].at(now, it + 1))
                    v.scalar_tensor_tensor(a_kn[it], in0=bank(it, 3), scalar=1e6, in1=a_rn[it], op0=ALU.mult,
                                           op1=ALU.mult).then_inc(*S["a_kn"].up(now))
                for it in items:
                    v.wait_ge(*S["a_e"].at(now, it + 1))
                    v.tensor_scalar(a_e1[it], a_e1[it], 1.0, None, ALU.add).then_inc(*own.next())
                    v.wait_ge(*own.all())
                    v.scalar_tensor_tensor(a_den[it], in0=a_e2[it], scalar=1.0, in1=a_e1[it], op0=ALU.add,
                                           op1=ALU.mult).then_inc(*S["a_den"].up(now))
                    v.wait_ge(*S["a_den"].at(now, it + 1))
                    v.reciprocal(a_e2[it], a_den[it]).then_inc(*own.next())
                    v.wait_ge(*own.all())
                    v.scalar_tensor_tensor(a_um[it], in0=a_e2[it], scalar=1.0, in1=a_kn[it],
                                                   op0=ALU.subtract, op1=ALU.mult).then_inc(*own.next())
                for it in items:
                    v.wait_ge(*S["a_L"].at(now, it + 1))
                    for b in range(IB):
                        v.tensor_tensor_scan(a_G[it][:, b * T:(b + 1) * T], K("ones"),
                                                     a_e1[it][:, b * T:(b + 1) * T], 0.0, ALU.mult, ALU.add).then_inc(*own.next())
                    v.wait_ge(*own.all())
                    G = a_G[it].rearrange("p (n t) -> p n t", t=P)
                    mid = G[:, :, P // 2 - 1:P // 2]
                    v.tensor_tensor(a_D[it][:, 0:4], G, mid.broadcast_to([P, 4, P]), ALU.subtract)
                    v.tensor_tensor(a_D[it][:, 4:6], G[:, 0:4:2], mid[:, 1:4:2].broadcast_to([P, 2, P]),
                                    ALU.subtract).then_inc(*S["a_D"].up(now))
                for it in items:
                    v.wait_ge(*S["a_E"].at(now, it + 1))
                    um = a_um[it].rearrange("p (n t) -> p n t", t=P)
                    v.tensor_tensor(a_UT[it][:, 0:4], a_E[it][:, 0:4], um, ALU.mult)
                    v.tensor_tensor(a_UT[it][:, 4:6], a_E[it][:, 4:6], um[:, 0:4:2], ALU.mult
                                    ).then_inc(*S["a_UT"].up(now))
                for b in range(IB):
                    for it in items:
                        v.wait_ge(*S["a_A"].at(now, b * ITEMS + it + 1))
                        v.tensor_tensor(a_Am[it][:, b], bank(it, 2, 4)[:, :, 0:3 * P], over(K("decay_mask"), 1, 2),
                                        ALU.mult).then_inc(*S["a_Am"].up(now))
                for it in items:
                    v.wait_ge(*S["a_y"].at(now, it + 1))
                    v.wait_ge(*S["a_Ep"].at(now, it + 1))
                    v.tensor_tensor(a_yT[it], bank(it, 0), a_Ep[it].rearrange("p n t -> p (n t)"), ALU.mult
                                    ).then_inc(*S["a_yT"].up(now))
                layernorm(own, now, 0, 1)

            def cross_attention(own, now, s, c):
                if c:
                    for it in items:
                        v.wait_ge(*S["x_made"].at(now, (s - 1) * ITEMS + it + 1))
                        v.wait_ge(*S["ctx_loaded"].at(now, ITEMS * 32))
                        for t in tiles:
                            v.bn_stats(stats[:, it, t], xs[:, it, t]).then_inc(*own.next())
                        v.bn_stats(stats[:, it, TILES], ctx_k[:, it]).then_inc(*own.next())
                        v.wait_ge(*own.all())
                        v.memset(tick[:], 0.0)
                        for t in range(TILES + 1):
                            i = v.bn_aggr(mv[:, it, t], stats[:, it, t])
                        i.then_inc(*S["l_var"].up(now))
                    for it in items:
                        v.wait_ge(*S["l_rstd"].at(now, it + 1))
                        for t in tiles:
                            v.tensor_scalar(x_xn[it][:, t], xs[:, it, t], mv[:, it, t, 0:1], rstd[:, it, t:t + 1],
                                            ALU.subtract, ALU.mult)
                        v.tensor_scalar(x_cn[it], ctx_k[:, it], mv[:, it, TILES, 0:1], rstd[:, it, TILES:TILES + 1],
                                        ALU.subtract, ALU.mult).then_inc(*S["l_made"].up(now))
                for it in items:
                    v.wait_ge(*S["x_kv"].at(now, c * ITEMS + it + 1))
                    for b in range(IB):
                        v.tensor_tensor(x_K[it][:, b].rearrange("p (h k) -> p h k", k=KV),
                                        over(bank(it, 1)[:, b * KV:(b + 1) * KV], 1, XH),
                                        over(K("kv_heads"), 2, KV), ALU.mult)
                    for b in range(IB):
                        i = v.tensor_tensor(x_V[it][:, b], over(bank(it, 3)[:, b * D:(b + 1) * D], 1, 4),
                                            K("v_heads").rearrange("p (a d) -> p a d", d=D), ALU.mult)
                    i.then_inc(*S["x_kv_kept"].up(now))
                for b in range(IB):
                    for it in items:
                        v.wait_ge(*S["x_scores"].at(now, (c * IB + b) * ITEMS + it + 1))
                        both = slice(HALF * b, HALF * (b + 1))
                        sc = bank(it, HALF * b, HALF * (b + 1)).rearrange("p t (h k) -> p t h k", k=KV)
                        mx = x_mx[it][:, both]
                        v.tensor_reduce(mx, sc, AX.X, ALU.max).then_inc(*own.next())
                        v.wait_ge(*own.all())
                        v.tensor_tensor(x_P[it][:, both].rearrange("p t (h k) -> p t h k", k=KV), sc,
                                        over(mx, 3, KV), ALU.subtract).then_inc(*S["x_less_max"].up(now))
                for b in range(IB):
                    for it in items:
                        v.wait_ge(*S["x_exp"].at(now, (c * IB + b) * ITEMS + it + 1))
                        both = slice(HALF * b, HALF * (b + 1))
                        v.tensor_reduce(x_sm[it][:, both],
                                                x_P[it][:, both].rearrange("p t (h k) -> p t h k", k=KV),
                                                AX.X, ALU.add).then_inc(*own.next())
                        v.wait_ge(*own.all())
                        v.reciprocal(x_rs[it][:, both], x_sm[it][:, both]).then_inc(*S["x_rs"].up(now))
                layernorm(own, now, s, 1)

            def routing(own, now, use, lg_bank, over_all):
                for it in items:
                    v.wait_ge(*S["logits"].at(now, use * ITEMS + it + 1))
                    lg = bank(it, lg_bank)[:, 0:TILES * EXPERTS].rearrange("p (t e) -> p t e", e=EXPERTS)
                    v.tensor_reduce(r_mx[it], lg, AX.X, ALU.max).then_inc(*own.next())
                    v.wait_ge(*own.all())
                    v.tensor_tensor(r_lg[it], lg, over(r_mx[it], 2, EXPERTS), ALU.subtract
                                    ).then_inc(*S["less_max"].up(now))
                    v.wait_ge(*S["less_max"].at(now, use * ITEMS + it + 1))
                    other, this = over(r_lg[it], 2, EXPERTS), over(r_lg[it], 3, EXPERTS)
                    v.tensor_tensor(r_gt[it], other, this, ALU.is_gt).then_inc(*own.next())
                    v.tensor_tensor(r_eq[it], other, this, ALU.is_equal).then_inc(*own.next())
                    v.wait_ge(*own.all())
                    v.tensor_tensor(r_eq[it], r_eq[it],
                                            over(K("tie").rearrange("p (i j) -> p i j", j=EXPERTS), 1, TILES),
                                            ALU.mult).then_inc(*own.next())
                    v.wait_ge(*own.all())
                    v.tensor_tensor(r_gt[it], r_gt[it], r_eq[it], ALU.add).then_inc(*own.next())
                    v.wait_ge(*own.all())
                    v.tensor_reduce(r_rank[it], r_gt[it], AX.X, ALU.add).then_inc(*own.next())
                    v.wait_ge(*own.all())
                    v.tensor_scalar(r_sel[it], r_rank[it], TOPK - 0.5, None, ALU.is_lt
                                    ).then_inc(*S["sel_made"].up(now))
                for it in items:
                    v.wait_ge(*S["sel_made"].at(now, use * ITEMS + it + 1))
                    v.wait_ge(*S["gate_exp"].at(now, use * ITEMS + it + 1))
                    v.tensor_tensor(r_w[it], r_E[it], r_sel[it], ALU.mult).then_inc(*own.next())
                    v.wait_ge(*own.all())
                    v.tensor_reduce(r_den[it], r_E[it] if over_all else r_w[it], AX.X, ALU.add).then_inc(*own.next())
                    v.wait_ge(*own.all())
                    v.reciprocal(r_den[it], r_den[it]).then_inc(*own.next())
                    v.wait_ge(*own.all())
                    v.tensor_tensor(r_w[it], r_w[it], over(r_den[it], 2, EXPERTS), ALU.mult
                                    ).then_inc(*S["w_made"].up(now))

            def experts(own, now):
                for it in items:
                    v.wait_ge(*S["g_rms"].at(now, it + 1))
                    v.tensor_tensor(g_xn[it], xs[:, it], over(g_r[it], 2, D), ALU.mult).then_inc(*S["g_xn"].up(now))
                routing(own, now, 0, 1, False)
                for it in items:
                    v.wait_ge(*S["g_count"].at(now, it + 1))
                    cnt = bank(it, 2)[:, 0:TILES * EXPERTS].rearrange("p (t e) -> p t e", e=EXPERTS)
                    v.tensor_scalar(g_slot[it], cnt, -1.0, float(CAP + 1), ALU.mult, ALU.add).then_inc(*own.next())
                    v.wait_ge(*own.all())
                    v.tensor_tensor(g_slot[it], g_slot[it], r_sel[it], ALU.mult).then_inc(*own.next())
                    v.wait_ge(*own.all())
                    v.tensor_scalar(g_slot[it], g_slot[it], -1.0, None, ALU.add).then_inc(*S["g_slot"].up(now))
                with v.Fori(0, EXPERTS) as e:
                    inner = now.inner(e, EXPERTS)
                    expert_step(Own(S["dve_own_experts"], inner), inner, e)
                for it in items:
                    v.wait_ge(*S["g_rms"].at(now, ITEMS + it + 1))
                    v.tensor_tensor(g_xn[it], bank(it, 0).rearrange("p (t d) -> p t d", d=D), over(g_r[it], 2, D),
                                    ALU.mult).then_inc(*S["g_on"].up(now))
                layernorm(own, now, 2, 2)

            def expert_step(own, now, e):
                for it in items:
                    v.wait_ge(*S["g_xe"].at(now, 0))
                    v.wait_ge(*S["w_made"].at(now, it + 1))
                    v.wait_ge(*S["g_slot"].at(now, it + 1))
                    for t in tiles:
                        slot, w = (a[it][:, t, bass.ds(e, 1)] for a in (g_slot, r_w))
                        v.tensor_scalar(g_Pw[it][:, t], K("slot"), slot, w, ALU.is_equal, ALU.mult)
                        i = v.tensor_scalar(g_P[it][:, t], K("slot"), slot, None, ALU.is_equal)
                    i.then_inc(*S["g_place"].up(now))
                for it in items:
                    v.wait_ge(*S["g_exp"].at(now, it + 1))
                    v.tensor_scalar(g_ln[it], g_ln[it], 1e18, None, ALU.min).then_inc(*S["g_exp_cut"].up(now))
                for it in items:
                    v.wait_ge(*S["g_ln"].at(now, it + 1))
                    v.scalar_tensor_tensor(g_sp[it], in0=bank(it, 2, 4), scalar=-1.0, in1=g_ln[it], op0=ALU.mult,
                                           op1=ALU.max).then_inc(*S["g_sp"].up(now))
                for it in items:
                    v.wait_ge(*S["g_sig"].at(now, it + 1))
                    v.tensor_tensor(g_qk[it].rearrange("p a b s -> p (a b s)"), bank(it, 2), g_eqk[it], ALU.mult
                                    ).then_inc(*S["g_qk"].up(now))
                for it in items:
                    v.wait_ge(*S["g_dec"].at(now, it + 1))
                    v.scalar_tensor_tensor(g_s[it], in0=g_s[it], scalar=1.0, in1=g_inv[it], op0=ALU.subtract,
                                           op1=ALU.mult).then_inc(*S["g_s"].up(now))
                for it in items:
                    v.wait_ge(*S["g_A"].at(now, it + 1))
                    mask_heads(it, 1.0).then_inc(*S["g_Am"].up(now))
                for it in items:
                    v.wait_ge(*S["g_ok"].at(now, it + 1))
                    v.scalar_tensor_tensor(g_ok[it], in0=bank(it, 0), scalar=-1.0, in1=g_dec[it],
                                                   op0=ALU.mult, op1=ALU.mult).then_inc(*own.next())
                    v.wait_ge(*own.all())
                    ok = g_ok[it].rearrange("p (h m) -> p h m", m=GM)
                    v.tensor_reduce(g_mx[it], ok, AX.X, ALU.max).then_inc(*own.next())
                    v.wait_ge(*own.all())
                    v.tensor_tensor(ok, ok, over(g_mx[it], 2, GM), ALU.subtract).then_inc(*S["g_less_max"].up(now))
                for it in items:
                    v.wait_ge(*S["g_p"].at(now, it + 1))
                    v.tensor_reduce(g_rs[it], g_ok[it].rearrange("p (h m) -> p h m", m=GM), AX.X, ALU.add).then_inc(*own.next())
                    v.wait_ge(*own.all())
                    v.reciprocal(g_rs[it], g_rs[it]).then_inc(*own.next())
                for it in items:
                    v.wait_ge(*S["g_T"].at(now, it + 1))
                    mask_heads(it, -1.0).then_inc(*S["g_Tm"].up(now))
                for it in items:
                    v.wait_ge(*S["g_ov"].at(now, it + 1))
                    v.wait_ge(*own.all())
                    o = g_o[it][:, bass.ds(e, 1)].rearrange("p a b (h d) -> p (a b h) d", d=GK)
                    v.tensor_tensor(o, bank(it, 0)[:, 0:IB * P].rearrange("p (h d) -> p h d", d=GK),
                                    over(g_rs[it], 2, GK), ALU.mult).then_inc(*S[f"g_o{it}"].up(now))

            def mask_heads(it, sign):
                for b in range(IB):
                    i = v.scalar_tensor_tensor(g_A[it][:, :, b], in0=bank(it, 0, 4)[:, :, b * CAP:(b + 1) * CAP],
                                               scalar=sign, in1=over(K("causal"), 1, GH), op0=ALU.mult, op1=ALU.mult)
                return i

            def self_attention(own, now):
                for it in items:
                    v.wait_ge(*S["s_qkv"].at(now, it + 1))
                    v.tensor_scalar(s_qT[it], bank(it, 1), col("s_bq"), 1.0 / D, ALU.add, ALU.mult
                                    ).then_inc(*S["s_q"].up(now))
                for it in items:
                    v.wait_ge(*S["s_scores"].at(now, it + 1))
                    v.tensor_tensor(s_S[it].rearrange("p (b t) n -> p b (t n)", b=IB), bank(it, 0, 2),
                                            over(K("no_self"), 1, IB), ALU.add).then_inc(*own.next())
                    v.wait_ge(*own.all())
                    v.tensor_reduce(s_mx[it], s_S[it], AX.X, ALU.max, negate=True).then_inc(*S["s_max"].up(now))
                for it in items:
                    v.wait_ge(*S["s_exp"].at(now, it + 1))
                    v.reciprocal(s_rs[it], s_sum[it]).then_inc(*own.next())
                for it in items:
                    v.wait_ge(*S["y_made"].at(now, 3 * ITEMS + it + 1))
                    v.wait_ge(*own.all())
                    for t in tiles:
                        v.scalar_tensor_tensor(zs[:, it, t], in0=bank(it, 0)[:, t * P:(t + 1) * P],
                                                       scalar=s_rs[it][:, t:t + 1], in1=xs[:, it, t],
                                                       op0=ALU.mult, op1=ALU.add).then_inc(*own.next())
                    v.wait_ge(*own.all())
                normalise(own, now, 3)

            def heads_and_experts(own, now):
                for it in items:
                    v.memset(m_V[it][:, :, :, SD:SD + 1], 1.0)
                for it in items:
                    v.wait_ge(*S["m_qk"].at(now, it + 1))
                    parts = m_parts[it]
                    v.tensor_tensor(m_r[it], m_qk[it], parts[:, :, 0], ALU.subtract).then_inc(*own.next())
                    v.wait_ge(*own.all())
                    v.tensor_copy(parts[:, :, 1], m_r[it]).then_inc(*own.next())
                    v.wait_ge(*own.all())
                    v.tensor_tensor(parts[:, :, 2], m_r[it], parts[:, :, 1], ALU.subtract
                                    ).then_inc(*S["m_split"].up(now))
                routing(own, now, 1, 0, True)
                for it in items:
                    v.wait_ge(*S["m_bias"].at(now, it + 1))
                    v.tensor_tensor(m_acc[it].rearrange("p t d -> p (t d)"), bank(it, 2),
                                            xs[:, it].rearrange("p t d -> p (t d)"), ALU.add).then_inc(*own.next())
                for t in tiles:
                    for it in items:
                        v.wait_ge(*S["m_moe"].at(now, t * ITEMS + it + 1))
                        for e in range(EXPERTS):
                            v.wait_ge(*own.all())
                            i = v.scalar_tensor_tensor(
                                m_acc[it][:, t], in0=bank(it, e // 4)[:, e % 4 * P:(e % 4 + 1) * P],
                                scalar=r_w[it][:, t, e:e + 1], in1=m_acc[it][:, t], op0=ALU.mult, op1=ALU.add)
                            if e < EXPERTS - 1:
                                i.then_inc(*own.next())
                        i.then_inc(*S["m_moe_read"].up(now))
                with v.Fori(0, QUADS) as q:
                    inner = now.inner(q, QUADS)
                    for t in tiles:
                        for it in items:
                            v.wait_ge(*S["m_max_scores"].at(inner, t * ITEMS + it + 1))
                            two = bank(it, 2 * (t % 2), 2 * (t % 2) + 2).rearrange("p a (h k) -> p a h k", k=T)
                            v.tensor_reduce(m_mx[it][:, t, bass.ds(q * 4, 4)], two, AX.X, ALU.max
                                            ).then_inc(*S["m_max_read"].up(inner))
                for it in items:
                    v.wait_ge(*S["m_pv"].at(now, PAIRS * IB * ITEMS))
                    for b in range(IB):
                        o = bank(it, 2 + b)[:, 0:HALF * SH * (SD + 1)].rearrange("p (t h d) -> p t h d", t=HALF, d=SD + 1)
                        v.reciprocal(m_rec[it][:, b].unsqueeze(3), o[:, :, :, SD:SD + 1]).then_inc(*own.next())
                    v.wait_ge(*own.all())
                    for b in range(IB):
                        o = bank(it, 2 + b)[:, 0:HALF * SH * (SD + 1)].rearrange("p (t h d) -> p t h d", t=HALF, d=SD + 1)
                        v.tensor_tensor(
                            zs[:, it, HALF * b:HALF * (b + 1)].rearrange("p t (h d) -> p t h d", d=SD),
                            o[:, :, :, 0:SD], over(m_rec[it][:, b], 3, SD), ALU.mult).then_inc(*own.next())
                    v.wait_ge(*own.all())
                    v.tensor_tensor(zs[:, it], zs[:, it], m_acc[it], ALU.add).then_inc(*own.next())
                    v.wait_ge(*own.all())
                normalise(own, now, 5)

            v.sem_inc(S["x_made"].sem, 1)
            v.sem_inc(S["g_o0"].sem, 1)
            v.sem_inc(S["g_o1"].sem, 1)
            v.sem_inc(S["m_max_read"].sem, 1)
            v.wait_ge(S["consts_loaded"].sem, 16 * 7)
            v.tensor_scalar(neg_cols[:], cols[:], -1.0, None, ALU.mult).then_inc(S["negated"].sem, 1)
            with v.Fori(0, ROUNDS) as r:
                now = Now(r)
                own = Own(S["dve_own"], now)
                linear_attention(own, now)
                if LAST > 1:
                    cross_attention(own, now, 1, 0)
                if LAST > 2:
                    experts(own, now)
                if LAST > 3:
                    self_attention(own, now)
                if LAST > 4:
                    cross_attention(own, now, 4, 1)
                if LAST > 5:
                    heads_and_experts(own, now)

        @block.gpsimd
        def _(pool):
            pool.wait_ge(S["consts_loaded"].sem, 16 * 7)

            def cross_attention(now, c):
                for b in range(IB):
                    for it in items:
                        pool.wait_ge(*S["x_rs"].at(now, (c * IB + b) * ITEMS + it + 1))
                        both = slice(HALF * b, HALF * (b + 1))
                        p = x_P[it][:, both].rearrange("p t (h k) -> p t h k", k=KV)
                        pool.tensor_tensor(p, p, over(x_rs[it][:, both], 3, KV), ALU.mult
                                           ).then_inc(*S["x_norm"].up(now))

            def expert_step(own, now, e):
                for it in items:
                    pool.wait_ge(*S["g_p"].at(now, it + 1))
                    pool.tensor_tensor(g_qd[it], g_ok[it], g_dec[it], ALU.mult).then_inc(*S["g_qd"].up(now))

            with pool.Fori(0, ROUNDS) as r:
                now = Now(r)
                if LAST > 1:
                    cross_attention(now, 0)
                if LAST > 2:
                    with pool.Fori(0, EXPERTS) as e:
                        inner = now.inner(e, EXPERTS)
                        expert_step(Own(S["pool_own_experts"], inner), inner, e)
                if LAST > 4:
                    cross_attention(now, 1)
        return S.rises()


def kernel(**inputs):
    import numpy as np
    import concourse.bacc as bacc
    from concourse.bass_utils import run_bass_kernel_spmd

    def of(name):
        return np.asarray(inputs[name])

    def by_expert(w):
        return np.transpose(w, (2, 0, 1)).reshape(w.shape[2], -1)

    qkv, bqkv = of("L1_ffn_W_qkv"), of("L1_ffn_b_qkv")
    w = {
        "a_wq": of("L0_attn_Wq").T, "a_wk": of("L0_attn_Wk").T, "a_wv": of("L0_attn_Wv").T, "a_wo": of("L0_attn_Wo").T,
        "x0_wq": of("L0_xattn_Wq"), "x0_wo": of("L0_xattn_Wo"),
        "g_wg": of("L0_ffn_Wg").T, "g_wq": of("L0_ffn_Wq").T, "g_wo": of("L0_ffn_Wo").T,
        "g_wk": by_expert(of("L0_ffn_Wk")), "g_wv": by_expert(of("L0_ffn_Wv")), "g_wf": by_expert(of("L0_ffn_Wf")),
        "s_wq": of("L1_attn_Wq").T, "s_wk": of("L1_attn_Wk").T, "s_wv": of("L1_attn_Wv").T,
        "x1_wq": of("L1_xattn_W_Q"), "x1_wo": of("L1_xattn_W_O"),
        "m_wq": qkv[:, 0:D], "m_wk": qkv[:, D:2 * D], "m_wv": qkv[:, 2 * D:], "m_wg": of("L1_ffn_W_gate"),
        "m_we": np.transpose(of("L1_ffn_W_experts"), (1, 0, 2)).reshape(D, -1),
    }
    c = {
        "a_wgamma": of("L0_attn_W_gamma"), "a_bgamma": of("L0_attn_b_gamma"), "a_wlambda": of("L0_attn_W_lambda"),
        "a_blambda": of("L0_attn_b_lambda"), "g_norm": of("L0_ffn_norm_w"), "g_gnorm": of("L0_ffn_gnorm_w"),
        "s_bq": of("L1_attn_bq"), "s_bk": of("L1_attn_bk"), "lat_g": of("L1_xattn_ln_lat_g"),
        "lat_b": of("L1_xattn_ln_lat_b"), "m_bq": bqkv[0:D], "m_bk": bqkv[D:2 * D],
    }
    rows = {"bo": of("L0_xattn_bo"), "s_bv": of("L1_attn_bv"), "m_bv": bqkv[2 * D:], "m_bg": of("L1_ffn_b_gate")}
    p, n = np.arange(P)[:, None], np.arange(P)[None, :]
    earlier = (p <= n).astype(np.float32)
    own = np.zeros((P, HALF, T), np.float32)
    for h in range(HALF):
        own[np.arange(P), h, h * P + np.arange(P)] = -np.finfo(np.float32).max
    k = {
        "ident": np.eye(P, dtype=np.float32), "causal": earlier,
        "decay_mask": -np.concatenate([earlier, np.ones((P, P), np.float32), earlier], 1),
        "mid_sum": earlier - (p < P // 2), "suffix": (p >= n), "ones": np.ones((P, T), np.float32),
        "head_sum": (p // 64 == n // 64), "kv_heads": (p // XD == np.arange(XH)[None, :]),
        "v_heads": (np.arange(BANK)[None, :] % D // XD == 2 * (np.arange(BANK)[None, :] // D) + p // KV),
        "slot": np.broadcast_to(n, (P, P)),
        "tie": np.broadcast_to((np.arange(EXPERTS)[None, :] < np.arange(EXPERTS)[:, None]).reshape(1, -1),
                               (P, EXPERTS * EXPERTS)),
        "no_self": own.reshape(P, -1),
    }
    ctx = of("ctx_768")
    arrays = {
        "x": of("x"),
        "ctx_tok": ctx.reshape(B * KV, CC),
        "ctx_T": np.transpose(ctx.reshape(B // IB, IB * KV, CC), (0, 2, 1)),
        "w_pack": np.concatenate([w[name] for name, _ in _WIDTHS], 1),
        "w_ctx": np.concatenate([of("L0_xattn_Wk"), of("L0_xattn_Wv"), of("L1_xattn_W_K"), of("L1_xattn_W_V")], 1),
        "col_pack": np.stack([c[name].reshape(P) for name in _COLS], 1),
        "ctx_cols": np.stack([of("L1_xattn_ln_in_g"), of("L1_xattn_ln_in_b")], 1),
        "const_pack": np.concatenate([k[name].astype(np.float32) for name, _ in _CONSTS], 1),
        "rows": np.concatenate([rows[name] for name, _ in _ROWS])[None, :],
        "b_experts": of("L1_ffn_b_experts"),
        "ones_row": np.ones((1, SH * TOK), mybir.dt.np(BF16)),
    }
    nc = bacc.Bacc("TRN2", target_bir_lowering=False, num_devices=1)
    args = {}
    for name, a in arrays.items():
        arrays[name] = a = np.ascontiguousarray(a)
        args[name] = nc.dram_tensor(name, a.shape, mybir.dt.from_np(a.dtype), kind="ExternalInput").ap()
    args["out"] = nc.dram_tensor("out", (B, T, D), F32, kind="ExternalOutput").ap()
    rises = build(nc, **args)
    assert not RISES or {k: n for k, n in rises.items() if n[0]} == RISES
    return run_bass_kernel_spmd(nc, [arrays], core_ids=[0]).results[0]["out"]
```

```python
from contextlib import ExitStack

import concourse.bass as bass
from concourse import mybir

P = 128
B, T, D = 16, 256, 128
KV, CC = 64, 96
ITEMS, IB = 2, 2
ROUNDS = B // (ITEMS * IB)
TILES = IB * T // P
TOK = IB * T
HALF = T // P
EXPERTS, TOPK, CAP = 8, 2, 128
AHEAD = 2
GH, GK, GM = 4, 32, 64
XH, XD = 8, 16
SH, SD = 16, 8
GATE_NORM = 8.0
EPS = 1e-5
BANK = 512
LAYERS = 6
LAST = LAYERS
QUADS = SH // 4
MAX_STEPS = QUADS * TILES
HEAD_STEPS = SH * IB
TERMS = 9
STACK = TERMS * SD

F32 = mybir.dt.float32
BF16 = mybir.dt.bfloat16
ALU = mybir.AluOpType
ACT = mybir.ActivationFunctionType
AX = mybir.AxisListType

_WIDTHS = [
    ("a_wq", D), ("a_wk", D), ("a_wv", D), ("a_wo", D),
    ("x0_wq", D), ("x0_wo", D),
    ("g_wg", EXPERTS), ("g_wq", D), ("g_wo", D),
    ("g_wk", EXPERTS * D), ("g_wv", EXPERTS * D), ("g_wf", EXPERTS * GH * GM),
    ("s_wq", D), ("s_wk", D), ("s_wv", D),
    ("x1_wq", D), ("x1_wo", D),
    ("m_wq", D), ("m_wk", D), ("m_wv", D), ("m_wg", EXPERTS), ("m_we", EXPERTS * D),
]
_COLS = ["a_wgamma", "a_bgamma", "a_wlambda", "a_blambda", "g_norm", "g_gnorm",
         "s_bq", "s_bk", "lat_g", "lat_b", "m_bq", "m_bk"]
_CONSTS = [("ident", P), ("causal", P), ("decay_mask", 3 * P), ("mid_sum", P), ("suffix", P), ("ones", T),
           ("head_sum", P), ("kv_heads", XH), ("v_heads", BANK), ("slot", P), ("tie", EXPERTS * EXPERTS),
           ("no_self", HALF * T)]
_ROWS = [("bo", D), ("s_bv", D), ("m_bv", D), ("m_bg", EXPERTS)]


def _places(widths):
    out, at = {}, 0
    for name, width in widths:
        out[name] = (at, at + width)
        at += width
    return out, at


W_AT, W_COLS = _places(_WIDTHS)
V_AT, V_COLS = _places([(n, 1) for n in _COLS])
C_AT, C_COLS = _places(_CONSTS)
R_AT, R_COLS = _places(_ROWS)


RISES = {
    "stored": (32, 0), "x_free": (2, 0), "x_kv": (4, 0), "m_split": (2, 0), "m_spilled0": (16, 0), "m_spilled1":
    (16, 0), "m_stacked0": (304, 0), "m_stacked1": (304, 0), "m_row": (2, 0), "m_max_spilled0": (16, 0),
    "m_max_stacked0": (16, 0), "m_max_spilled1": (16, 0), "m_max_stacked1": (16, 0), "x_made": (12, 0),
    "g_qk_made": (16, 2), "xT_made": (12, 0), "xT_kept": (12, 0), "a_qkv": (2, 0), "a_sq": (2, 0), "a_ss": (2,
    0), "a_UT": (2, 0), "a_U": (2, 0), "a_qv_kept": (2, 0), "a_A": (4, 0), "a_Am": (4, 0), "a_U_kept": (2, 0),
    "a_y": (2, 0), "a_yT": (2, 0), "y_made": (10, 0), "x_q": (4, 0), "x_q_kept": (4, 0), "x_kv_kept": (4, 0),
    "x_scores": (8, 0), "x_norm": (8, 0), "x_PT": (8, 0), "x_PT_kept": (8, 0), "x_o": (4, 0), "x_o_kept": (4,
    0), "g_xn": (2, 0), "logits": (4, 0), "sel_made": (4, 0), "g_count": (2, 0), "g_place": (20, 2), "g_xe":
    (18, 2), "g_scatter": (18, 2), "g_xe_kept": (18, 2), "g_f_made": (16, 2), "g_wk": (8, 1), "g_o0": (8, 1),
    "g_v_made": (16, 2), "g_o1": (8, 1), "g_sp": (16, 2), "g_scatter_kept": (18, 2), "g_decay": (16, 2),
    "g_dec": (16, 2), "g_qk": (16, 2), "g_A": (16, 2), "g_Am": (16, 2), "g_s": (16, 2), "g_ok": (16, 2), "g_sT":
    (16, 2), "g_qd": (16, 2), "g_qdT": (16, 2), "g_qdT_kept": (16, 2), "g_T": (16, 2), "g_Tm": (16, 2), "g_ov":
    (16, 2), "g_out": (2, 0), "g_on": (2, 0), "g_onT": (2, 0), "g_onT_kept": (2, 0), "s_qkv": (2, 0), "s_q": (2,
    0), "s_kv": (2, 0), "s_scores": (2, 0), "s_exp": (2, 0), "s_PT": (2, 0), "s_PT_kept": (2, 0), "l_made": (2,
    0), "m_qkv": (2, 0), "w_made": (4, 0), "m_qkv_kept": (2, 0), "m_wT": (2, 0), "m_wT_kept": (2, 0), "m_bias":
    (2, 0), "m_moe1": (4, 0), "m_acc": (2, 0), "m_moe_sum1": (32, 0), "m_max_scores0": (16, 0), "m_max_read0":
    (16, 0), "m_mxT": (2, 0), "m_max_scores1": (16, 0), "m_max_read1": (16, 0), "m_scores0": (32, 0), "m_exp0":
    (32, 0), "m_pv0": (32, 0), "m_attention": (2, 0), "m_moe0": (4, 0), "m_moe_sum0": (32, 0), "m_scores1": (32,
    0), "m_exp1": (32, 0), "m_pv1": (32, 0), "act_own": (36, 0), "a_ss_kept": (2, 0), "a_rn": (2, 0), "a_kn":
    (2, 0), "a_e": (2, 0), "a_den": (2, 0), "a_L": (2, 0), "a_D": (2, 0), "a_E": (2, 0), "a_Ep": (2, 0),
    "var_made": (12, 0), "rstd_made": (12, 0), "x_less_max": (8, 0), "x_exp": (8, 0), "g_rms": (4, 0),
    "less_max": (4, 0), "gate_exp": (4, 0), "g_exp_f": (16, 2), "g_exp_qk": (16, 2), "g_cut_f": (16, 2),
    "g_ln_f": (16, 2), "g_v": (16, 2), "g_cut_qk": (16, 2), "g_ln_qk": (16, 2), "g_sp_qk": (16, 2), "g_sig":
    (16, 2), "g_less_max": (16, 2), "g_p": (16, 2), "s_max": (2, 0), "l_var": (2, 0), "l_rstd": (2, 0), "m_qk":
    (2, 0), "dve_own": (156, 0), "x_rs": (8, 0), "g_slot": (2, 0), "dve_own_experts": (64, 8),
}

PRIMED = ("x_made", "stored", "g_o0", "g_o1", "g_qk_made")


class Signal:

    def __init__(self, sem, primed, per_round, per_step):
        self.primed = primed
        self.sem, self.per_round, self.per_step = sem, per_round, per_step
        self.raised_round, self.raised_step, self.frozen = 0, 0, False

    def at(self, now, n):
        value = now.round * self.per_round + (n + self.primed)
        if now.step is not None and self.per_step:
            value = value + now.step * self.per_step
        return self.sem, value

    def up(self, now, n=1):
        if self.frozen:
            return self.sem, n
        if now.step is None:
            self.raised_round += n
        else:
            self.raised_step += n
            self.raised_round += n * now.steps
        return self.sem, n


class Signals:

    def __init__(self, nc, ctx):
        self.nc, self.ctx, self.all = nc, ctx, {}

    def __getitem__(self, name):
        if name not in self.all:
            sem = self.ctx.enter_context(self.nc.semaphore(name))
            fixed = {"x_loaded0": (16, 0), "x_loaded1": (16, 0), "ctx_loaded": (ITEMS * 32, 0)}
            self.all[name] = Signal(sem, int(name in PRIMED), *fixed.get(name, RISES.get(name, (0, 0))))
        return self.all[name]

    def rises(self):
        return {k: (s.raised_round, s.raised_step) for k, s in self.all.items()}


class Now:

    def __init__(self, round_):
        self.round, self.step, self.steps = round_, None, 1

    def inner(self, step, steps):
        now = Now(self.round)
        now.step, now.steps = step, steps
        return now


class Own:

    def __init__(self, counter, now):
        self.counter, self.now, self.n = counter, now, 0

    def next(self):
        self.n += 1
        return self.counter.up(self.now)

    def all(self):
        return self.counter.at(self.now, self.n)


def build(nc, x, ctx_tok, ctx_T, w_pack, w_ctx, col_pack, ctx_cols, const_pack, rows, b_experts, ones_row, out):
    ctx = ExitStack()
    with ctx:
        S = Signals(nc, ctx)

        def sb(name, shape, dt=F32):
            return ctx.enter_context(nc.sbuf_tensor(name, shape, dt))

        weights = sb("weights", [P, W_COLS])
        wctx = sb("wctx", [CC, 4 * D])
        cols = sb("cols", [P, V_COLS])
        neg_cols = sb("neg_cols", [P, V_COLS])
        ccols = sb("ccols", [CC, 2])
        consts = sb("consts", [P, C_COLS])
        row_sb = sb("row_sb", [1, R_COLS])
        bexp = sb("bexp", [EXPERTS, D])
        x_in = sb("x_in", [P, ITEMS, TILES, D])
        ctx_k = sb("ctx_k", [P, ITEMS, CC])
        ctx_t = sb("ctx_t", [CC, ITEMS, P])
        xs = sb("xs", [P, ITEMS, TILES, D])
        zs = sb("zs", [P, ITEMS, TILES, D])
        stats = sb("stats", [P, ITEMS, TILES + 1, 6])
        mv = sb("mv", [P, ITEMS, TILES + 1, 2])
        rstd = sb("rstd", [P, ITEMS, TILES + 1])
        tick = sb("tick", [1, 1])
        wk_now = sb("wk_now", [P, D])
        PS = ctx.enter_context(nc.psum_tensor("PS", [P, 8, BANK], F32))
        ARENA = 15744
        arena = sb("arena", [P, ITEMS, ARENA])
        spill_qk = nc.dram_tensor("spill_qk", [ITEMS, P, 2, 3, TOK], BF16).ap()
        spill_max = nc.dram_tensor("spill_max", [ITEMS, SH, TOK], BF16).ap()

        class Arena:
            def __init__(self):
                self.at = 0

            def __call__(self, *shape, parts=P, dt=F32):
                n = 1
                for s in shape:
                    n *= s
                words = n if dt == F32 else n // 2
                a = self.at
                self.at += words + words % 2
                assert self.at <= ARENA, self.at
                views = []
                for it in range(ITEMS):
                    v = arena[0:parts, it, a:a + words]
                    if dt != F32:
                        v = v.bitcast(dt)
                    if len(shape) == 2:
                        v = v.rearrange("p (a b) -> p a b", b=shape[1])
                    elif len(shape) == 3:
                        v = v.rearrange("p (a b c) -> p a b c", b=shape[1], c=shape[2])
                    elif len(shape) == 4:
                        v = v.rearrange("p (a b c d) -> p a b c d", b=shape[1], c=shape[2], d=shape[3])
                    views.append(v)
                return views

        def W(name):
            a, b = W_AT[name]
            return weights[:, a:b]

        def col(name, n=P):
            return cols[0:n, V_AT[name][0]:V_AT[name][1]]

        def neg(name):
            return neg_cols[:, V_AT[name][0]:V_AT[name][1]]

        def K(name):
            a, b = C_AT[name]
            return consts[:, a:b]

        def row(name):
            a, b = R_AT[name]
            return row_sb[:, a:b]

        ident = K("ident")
        one_row = K("ones")[0:1, 0:P]

        def bank(it, n, m=None):
            return PS[:, 4 * it + n, :] if m is None else PS[:, 4 * it + n:4 * it + m, :]

        def over(ap, dim, n):
            v = ap.unsqueeze(dim)
            shape = list(v.shape)
            shape[dim] = n
            return v.broadcast_to(shape)

        items = range(ITEMS)
        tiles = range(TILES)

        al = Arena()
        a_xT, a_qT, a_vT, a_sq, a_rn, a_kn, a_e1, a_e2, a_den, a_G, a_um = (al(TOK) for _ in range(11))
        a_D = al(6, P)
        a_E = al(6, P)
        a_Ep = al(4, P)
        a_UT = al(6, P)
        a_U = al(6, P)
        a_Am = al(IB, 2, 3 * P)
        a_yT = al(TOK)
        al = Arena()
        x_xn = al(TILES, D)
        x_cn = al(CC)
        x_xT = al(TOK)
        x_cT = al(P, parts=CC)
        x_qT = al(TOK)
        x_K = al(IB, BANK)
        x_V = al(IB, 4, P)
        x_P = al(TILES, BANK)
        x_mx = al(TILES, XH)
        x_sm = al(TILES, XH)
        x_rs = al(TILES, XH)
        x_PT = al(IB, 4, T)
        x_yT = al(TOK)
        al = Arena()
        g_xn = al(TILES, D)
        g_ss = al(TILES)
        g_r = al(TILES)
        r_mx = al(TILES)
        r_lg = al(TILES, EXPERTS)
        r_E = al(TILES, EXPERTS)
        r_gt = al(TILES, EXPERTS, EXPERTS)
        r_eq = al(TILES, EXPERTS, EXPERTS)
        r_rank = al(TILES, EXPERTS)
        r_sel = al(TILES, EXPERTS)
        r_den = al(TILES)
        r_w = al(TILES, EXPERTS)
        r_end = al.at
        g_slot = al(TILES, EXPERTS + AHEAD)
        g_w = al(TILES, EXPERTS + AHEAD)
        g_P = al(TILES, CAP)
        g_Pw = al(TILES, CAP)
        g_PwT = al(EXPERTS + 1, TOK)
        g_o = al(EXPERTS, IB, P)
        g_xe = al(IB, CAP)
        g_v = al(IB, P)
        g_qk = al(2, IB, CAP)
        g_ln = al(2, BANK)
        g_sp = al(2, BANK)
        g_eqk = [a[:, 0] for a in g_ln]
        g_s = al(BANK)
        g_dec = al(BANK)
        g_inv = al(BANK)
        g_A = al(GH, IB, CAP)
        g_ok = g_eqk
        g_mx = al(IB * GH)
        g_rs = al(IB * GH)
        g_sT = al(IB, 2, CAP)
        g_qd = g_inv
        g_qT = al(IB, 2, CAP)
        g_xT = [a[:, 0] for a in g_sp]
        g_onT = [a[:, 0] for a in g_sp]
        al = Arena()
        s_xT, s_qT, s_kT = al(TOK), al(TOK), al(TOK)
        s_v = al(TILES, D)
        s_S = al(TILES, T)
        s_mx = al(TILES)
        s_sum = al(TILES)
        s_rs = al(TILES)
        s_PT = al(IB, 2, T)
        al = Arena()
        al.at = r_end
        m_xT = al(TOK)
        m_qk = al(2, TOK)
        r_at = al.at
        m_r = al(2, TOK)
        m_parts = al(2, 3, TOK, dt=BF16)
        m_Q = al(SH, TOK, parts=STACK + 1, dt=BF16)
        m_K = al(SH, TOK, parts=STACK + 1, dt=BF16)
        m_V = al(TILES, SH, SD + 1)
        m_acc = al(TILES, D)
        m_acc2 = [a[:, 0].rearrange("p (t d) -> p t d", d=D) for a in m_qk]
        m_mx = al(TILES, SH)
        row_at = al.at
        m_cT = al(TOK, parts=EXPERTS)
        m_rec = al(IB, HALF, SH)
        al.at = row_at
        m_row = al(TOK, parts=SH, dt=BF16)
        al.at = r_at
        m_P = al(2, 2, T)

        block = ctx.enter_context(nc.Block())

        @block.sync
        def _(sp):
            sp.sem_inc(S["stored"].sem, 1)
            for dst, src in ((weights[:], w_pack), (wctx[:], w_ctx), (cols[:], col_pack), (ccols[:], ctx_cols),
                             (consts[:], const_pack), (row_sb[:], rows), (bexp[:], b_experts)):
                sp.dma_start(dst, src).then_inc(S["consts_loaded"].sem, 16)

            def load_x(now, r):
                for it in items:
                    sp.dma_start(x_in[:, it].rearrange("p (b h) d -> p b h d", b=IB),
                                 x[bass.ds(r * (ITEMS * IB) + it * IB, IB)].rearrange("b (h p) d -> p b h d", p=P)
                                 ).then_inc(S[f"x_loaded{it}"].sem, 16)

            def load_context(now, r):
                for it in items:
                    sp.dma_start(ctx_k[:, it], ctx_tok[bass.ds(r * (ITEMS * P) + it * P, P)]
                                 ).then_inc(S["ctx_loaded"].sem, 16)
                    sp.dma_start(ctx_t[:, it], ctx_T[bass.ds(r * ITEMS + it, 1)].rearrange("a c n -> (a c) n")
                                 ).then_inc(S["ctx_loaded"].sem, 16)

            def one_round(now, ahead):
                if ahead:
                    sp.wait_ge(*S["x_free"].at(now, ITEMS))
                    load_x(now, now.round + 1)
                    if LAST > 1:
                        sp.wait_ge(*S["x_kv"].at(now, (2 if LAST > 4 else 1) * ITEMS))
                    load_context(now, now.round + 1)
                if LAST > 5:
                    for it in items:
                        sp.wait_ge(*S["m_split"].at(now, it + 1))
                        sp.dma_start(spill_qk[it], m_parts[it]).then_inc(*S[f"m_spilled{it}"].up(now, 16))
                    for it in items:
                        sp.wait_ge(*S[f"m_spilled{it}"].at(now, 16))
                        for t in range(TERMS):
                            for side, part, stack in ((0, t // 3, m_Q), (1, t % 3, m_K)):
                                src = spill_qk[it, :, side, part, :].rearrange("(h d) n -> d h n", d=SD)
                                sp.dma_start(stack[it][SD * t:SD * t + SD], src
                                             ).then_inc(*S[f"m_stacked{it}"].up(now, 16))
                        sp.dma_start(m_K[it][STACK:STACK + 1], ones_row.rearrange("a (h n) -> a h n", h=SH)
                                     ).then_inc(*S[f"m_stacked{it}"].up(now, 16))
                    for it in items:
                        sp.wait_ge(*S["m_row"].at(now, it + 1))
                        sp.dma_start(spill_max[it], m_row[it]).then_inc(*S[f"m_max_spilled{it}"].up(now, 16))
                        sp.wait_ge(*S[f"m_max_spilled{it}"].at(now, 16))
                        sp.dma_start(m_Q[it][STACK:STACK + 1], spill_max[it].rearrange("(a h) n -> a h n", a=1)
                                     ).then_inc(*S[f"m_max_stacked{it}"].up(now, 16))
                for it in items:
                    sp.wait_ge(*S["x_made"].at(now, (LAST - 1) * ITEMS + it + 1))
                    sp.dma_start(out[bass.ds(now.round * (ITEMS * IB) + it * IB, IB)].rearrange("b (h p) d -> p b h d", p=P),
                                 xs[:, it].rearrange("p (b h) d -> p b h d", b=IB)
                                 ).then_inc(*S["stored"].up(now, 16))

            load_x(None, 0)
            load_context(None, 0)
            if ROUNDS > 1:
                with sp.Fori(0, ROUNDS - 1) as r:
                    one_round(Now(r), True)
                for s_ in S.all.values():
                    s_.frozen = True
            one_round(Now(ROUNDS - 1), False)
            sp.wait_ge(S["stored"].sem, 1 + ROUNDS * ITEMS * 16)
            for s_ in S.all.values():
                s_.frozen = False

        @block.tensor
        def _(pe):
            def transpose4(it, src, dst_bank):
                for t in tiles:
                    mm = pe.transpose(bank(it, dst_bank)[:, t * P:(t + 1) * P], src[:, t, :], ident)
                return mm

            def tokens_out(it, dst_bank, lhs, w, bias=None):
                for t in tiles:
                    o = bank(it, dst_bank)[:, t * P:(t + 1) * P]
                    mm = pe.matmul(o, lhsT=lhs[:, t * P:(t + 1) * P], rhs=w, start=True, stop=bias is None)
                    if bias is not None:
                        mm = pe.matmul(o, lhsT=one_row, rhs=bias, start=False, stop=True)
                return mm

            def linear_attention(now):
                for it in items:
                    pe.wait_ge(*S[f"x_loaded{it}"].at(now, 16))
                    pe.wait_ge(*S["x_made"].at(now, 0))
                    transpose4(it, x_in[:, it], 0).then_inc(*S["xT_made"].up(now))
                for it in items:
                    pe.wait_ge(*S["xT_kept"].at(now, it + 1))
                    for n, w in ((1, "a_wq"), (2, "a_wv"), (3, "a_wk")):
                        mm = pe.matmul(bank(it, n), lhsT=W(w), rhs=a_xT[it], start=True, stop=True)
                    mm.then_inc(*S["a_qkv"].up(now))
                for it in items:
                    pe.wait_ge(*S["a_sq"].at(now, it + 1))
                    pe.matmul(bank(it, 0), lhsT=K("head_sum"), rhs=a_sq[it], start=True, stop=True
                              ).then_inc(*S["a_ss"].up(now))
                for it in items:
                    pe.wait_ge(*S["a_UT"].at(now, it + 1))
                    for n in range(6):
                        mm = pe.transpose(bank(it, n // 4)[:, n % 4 * P:(n % 4 + 1) * P], a_UT[it][:, n], ident)
                    mm.then_inc(*S["a_U"].up(now))
                for b in range(IB):
                    for it in items:
                        if b:
                            pe.wait_ge(*S["a_Am"].at(now, it + 1))
                        else:
                            pe.wait_ge(*S["a_qv_kept"].at(now, it + 1))
                        for part, (s0, t0, n) in enumerate(((0, 0, 2), (1, 1, 1))):
                            for h in range(2):
                                lanes = slice(64 * h, 64 * h + 64)
                                s = (b * HALF + s0) * P
                                t = (b * HALF + t0) * P
                                mm = pe.matmul(bank(it, 2 + h)[:, 256 * part:256 * part + n * P],
                                               lhsT=a_vT[it][lanes, s:s + P], rhs=a_qT[it][lanes, t:t + n * P],
                                               start=True, stop=True)
                        mm.then_inc(*S["a_A"].up(now))
                for it in items:
                    pe.wait_ge(*S["a_U_kept"].at(now, it + 1))
                    pe.wait_ge(*S["a_Am"].at(now, ITEMS + it + 1))
                    for b in range(IB):
                        for h in range(2):
                            lanes = slice(64 * h, 64 * h + 64)
                            A = a_Am[it][:, b, h]

                            def U(n):
                                return a_U[it][:, n, lanes]
                            first = bank(it, 0)[lanes, b * T:b * T + P]
                            second = bank(it, 0)[lanes, b * T + P:(b + 1) * T]
                            pe.matmul(first, lhsT=U(2 * b), rhs=A[:, 0:P], start=True, stop=True)
                            pe.matmul(second, lhsT=U(4 + b), rhs=A[:, P:2 * P], start=True, stop=False)
                            mm = pe.matmul(second, lhsT=U(2 * b + 1), rhs=A[:, 2 * P:], start=False, stop=True)
                    mm.then_inc(*S["a_y"].up(now))
                for it in items:
                    pe.wait_ge(*S["a_yT"].at(now, it + 1))
                    tokens_out(it, 1, a_yT[it], W("a_wo")).then_inc(*S["y_made"].up(now))

            def cross_attention(now, s, c):
                for it in items:
                    if c:
                        pe.wait_ge(*S["l_made"].at(now, it + 1))
                        transpose4(it, x_xn[it], 0)
                        pe.transpose(bank(it, 1)[0:CC, 0:P], x_cn[it], ident).then_inc(*S["xT_made"].up(now))
                    else:
                        pe.wait_ge(*S["x_made"].at(now, (s - 1) * ITEMS + it + 1))
                        transpose4(it, xs[:, it], 0).then_inc(*S["xT_made"].up(now))
                wk, wv = (wctx[:, (2 * c + n) * D:(2 * c + n + 1) * D] for n in range(2))
                pe.wait_ge(*S["ctx_loaded"].at(now, ITEMS * 32))
                for it in items:
                    cT = x_cT[it] if c else ctx_t[:, it]
                    pe.wait_ge(*S["xT_kept"].at(now, s * ITEMS + it + 1))
                    pe.matmul(bank(it, 1)[:, 0:P], lhsT=wk, rhs=cT, start=True, stop=True)
                    for b in range(IB):
                        for half in range(2):
                            mm = pe.matmul(bank(it, 3)[64 * half:64 * half + 64, b * D:(b + 1) * D],
                                           lhsT=cT[:, b * KV:(b + 1) * KV], rhs=wv, start=True, stop=True)
                    mm.then_inc(*S["x_kv"].up(now))
                    pe.matmul(bank(it, 2), lhsT=W(f"x{c}_wq"), rhs=x_xT[it], start=True, stop=True
                              ).then_inc(*S["x_q"].up(now))
                for b in range(IB):
                    for it in items:
                        pe.wait_ge(*S["x_q_kept"].at(now, c * ITEMS + it + 1))
                        pe.wait_ge(*S["x_kv_kept"].at(now, c * ITEMS + it + 1))
                        for t in range(HALF * b, HALF * b + HALF):
                            mm = pe.matmul(bank(it, t), lhsT=x_qT[it][:, t * P:(t + 1) * P], rhs=x_K[it][:, b],
                                           start=True, stop=True)
                        mm.then_inc(*S["x_scores"].up(now))
                for b in range(IB):
                    for it in items:
                        pe.wait_ge(*S["x_norm"].at(now, (c * IB + b) * ITEMS + it + 1))
                        for h in range(4):
                            for t in range(HALF):
                                o = bank(it, 2 * b + h // 2)[:, h % 2 * T + t * P:h % 2 * T + (t + 1) * P]
                                mm = pe.transpose(o, x_P[it][:, HALF * b + t, h * P:(h + 1) * P], ident)
                        mm.then_inc(*S["x_PT"].up(now))
                for it in items:
                    for b in range(IB):
                        pe.wait_ge(*S["x_PT_kept"].at(now, (c * IB + b) * ITEMS + it + 1))
                        for h in range(4):
                            mm = pe.matmul(bank(it, 0)[:, b * T:(b + 1) * T], lhsT=x_V[it][:, b, h],
                                           rhs=x_PT[it][:, b, h], start=(h == 0), stop=(h == 3))
                    mm.then_inc(*S["x_o"].up(now))
                for it in items:
                    pe.wait_ge(*S["x_o_kept"].at(now, c * ITEMS + it + 1))
                    tokens_out(it, 1, x_yT[it], W(f"x{c}_wo"), None if c else row("bo")).then_inc(*S["y_made"].up(now))

            def experts(now):
                for it in items:
                    pe.wait_ge(*S["g_xn"].at(now, it + 1))
                    transpose4(it, g_xn[it], 0).then_inc(*S["xT_made"].up(now))
                for it in items:
                    pe.wait_ge(*S["xT_kept"].at(now, 2 * ITEMS + it + 1))
                    for t in tiles:
                        mm = pe.matmul(bank(it, 1)[:, t * EXPERTS:(t + 1) * EXPERTS],
                                       lhsT=g_xT[it][:, t * P:(t + 1) * P], rhs=W("g_wg"), start=True, stop=True)
                    mm.then_inc(*S["logits"].up(now))
                for it in items:
                    pe.wait_ge(*S["sel_made"].at(now, it + 1))
                    for t in tiles:
                        o = bank(it, 2)[:, t * EXPERTS:(t + 1) * EXPERTS]
                        mm = pe.matmul(o, lhsT=K("suffix"), rhs=r_sel[it][:, t], start=True, stop=t % 2 == 1)
                        if t % 2 == 0:
                            mm = pe.matmul(o, lhsT=K("ones")[:, 0:P], rhs=r_sel[it][:, t + 1], start=False, stop=True)
                    mm.then_inc(*S["g_count"].up(now))
                gather(now, 0)
                with pe.Fori(0, EXPERTS) as e:
                    expert_step(now.inner(e, EXPERTS), e)
                for it in items:
                    pe.wait_ge(*S[f"g_o{it}"].at(now, EXPERTS))
                    for t in tiles:
                        for e in range(EXPERTS):
                            mm = pe.matmul(bank(it, 0)[:, t * P:(t + 1) * P],
                                           lhsT=g_PwT[it][:, e, t * P:(t + 1) * P], rhs=g_o[it][:, e, t // HALF],
                                           start=(e == 0), stop=(e == EXPERTS - 1))
                    mm.then_inc(*S["g_out"].up(now))
                for it in items:
                    pe.wait_ge(*S["g_on"].at(now, it + 1))
                    transpose4(it, g_xn[it], 1).then_inc(*S["g_onT"].up(now))
                for it in items:
                    pe.wait_ge(*S["g_onT_kept"].at(now, it + 1))
                    tokens_out(it, 2, g_onT[it], W("g_wo")).then_inc(*S["y_made"].up(now))

            def gather(now, done):
                for it in items:
                    pe.wait_ge(*S["g_place"].at(now, done + it + 1))
                    for b in range(IB):
                        for t in range(HALF):
                            mm = pe.matmul(bank(it, 3)[:, b * CAP:(b + 1) * CAP], lhsT=g_xn[it][:, HALF * b + t],
                                           rhs=g_P[it][:, HALF * b + t], start=(t == 0), stop=(t == HALF - 1))
                    mm.then_inc(*S["g_xe"].up(now))
                for it in items:
                    if now.step is not None:
                        pe.wait_ge(*S["g_sT"].at(now, it + 1))
                    for t in tiles:
                        mm = pe.transpose(bank(it, 1)[:, t * P:(t + 1) * P], g_Pw[it][:, t], ident)
                    mm.then_inc(*S["g_scatter"].up(now))

            def expert_step(now, e):
                for it in items:
                    pe.wait_ge(*S["g_xe_kept"].at(now, it + 1))
                    for b in range(IB):
                        mm = pe.matmul(bank(it, 3)[:, b * GH * GM:(b + 1) * GH * GM], lhsT=g_xe[it][:, b],
                                       rhs=W("g_wf")[:, bass.ds(e * (GH * GM), GH * GM)], start=True, stop=True)
                    mm.then_inc(*S["g_f_made"].up(now))
                    if it == 0:
                        pe.wait_ge(*S["g_wk"].at(now, 1))
                    xe = g_xe[it].rearrange("p b s -> p (b s)")
                    pe.matmul(bank(it, 2)[:, 0:IB * CAP], lhsT=W("g_wq"), rhs=xe, start=True, stop=True)
                    pe.matmul(bank(it, 2)[:, IB * CAP:], lhsT=wk_now[:], rhs=xe, start=True, stop=True
                              ).then_inc(*S["g_qk_made"].up(now))
                for it in items:
                    pe.wait_ge(*S[f"g_o{it}"].at(now, 0))
                    for b in range(IB):
                        mm = pe.matmul(bank(it, 0)[:, b * P:(b + 1) * P], lhsT=g_xe[it][:, b],
                                       rhs=W("g_wv")[:, bass.ds(e * D, D)], start=True, stop=True)
                    mm.then_inc(*S["g_v_made"].up(now))
                for it in items:
                    pe.wait_ge(*S["g_sp"].at(now, it + 1))
                    if it == 0:
                        pe.wait_ge(*S["g_scatter_kept"].at(now, ITEMS))
                    pe.matmul(bank(it, 1), lhsT=K("mid_sum"), rhs=g_sp[it][:, 1], start=True, stop=True
                              ).then_inc(*S["g_decay"].up(now))
                for it in items:
                    pe.wait_ge(*S["g_dec"].at(now, it + 1))
                    pe.wait_ge(*S["g_qk"].at(now, it + 1))
                    for b in range(IB):
                        for h in range(GH):
                            lanes = slice(GK * h, GK * h + GK)
                            mm = pe.matmul(bank(it, h)[:, b * CAP:(b + 1) * CAP], lhsT=g_qk[it][lanes, 1, b],
                                           rhs=g_qk[it][lanes, 0, b], start=True, stop=True)
                    mm.then_inc(*S["g_A"].up(now))
                for it in items:
                    pe.wait_ge(*S["g_Am"].at(now, it + 1))
                    pe.wait_ge(*S["g_s"].at(now, it + 1))
                    for b in range(IB):
                        for h in range(GH):
                            at = (b * GH + h) * GM
                            pe.matmul(bank(it, 0)[:, at:at + GM], lhsT=g_A[it][:, h, b], rhs=g_s[it][:, at:at + GM],
                                      start=True, stop=True)
                    for n in range(4):
                        mm = pe.transpose(bank(it, 1)[:, n * P:(n + 1) * P], g_s[it][:, n * P:(n + 1) * P], ident)
                    mm.then_inc(*S["g_ok"].up(now))
                gather(now, ITEMS)
                for it in items:
                    pe.wait_ge(*S["g_qd"].at(now, it + 1))
                    for n in range(4):
                        mm = pe.transpose(bank(it, 2)[:, n * P:(n + 1) * P], g_qd[it][:, n * P:(n + 1) * P], ident)
                    mm.then_inc(*S["g_qdT"].up(now))
                for it in items:
                    pe.wait_ge(*S["g_qdT_kept"].at(now, it + 1))
                    for b in range(IB):
                        for h in range(GH):
                            lanes = slice(64 * (h % 2), 64 * (h % 2) + 64)
                            mm = pe.matmul(bank(it, h)[:, b * CAP:(b + 1) * CAP], lhsT=g_sT[it][lanes, b, h // 2],
                                           rhs=g_qT[it][lanes, b, h // 2], start=True, stop=True)
                    mm.then_inc(*S["g_T"].up(now))
                for it in items:
                    pe.wait_ge(*S["g_Tm"].at(now, it + 1))
                    for b in range(IB):
                        for h in range(GH):
                            at = b * P + h * GK
                            mm = pe.matmul(bank(it, 0)[:, at:at + GK], lhsT=g_A[it][:, h, b],
                                           rhs=g_v[it][:, b, h * GK:(h + 1) * GK], start=True, stop=True)
                    mm.then_inc(*S["g_ov"].up(now))

            def self_attention(now):
                for it in items:
                    pe.wait_ge(*S["x_made"].at(now, 2 * ITEMS + it + 1))
                    transpose4(it, xs[:, it], 0).then_inc(*S["xT_made"].up(now))
                for it in items:
                    pe.wait_ge(*S["xT_kept"].at(now, 3 * ITEMS + it + 1))
                    for n, w in ((1, "s_wq"), (2, "s_wk")):
                        pe.matmul(bank(it, n), lhsT=W(w), rhs=s_xT[it], start=True, stop=True)
                    tokens_out(it, 3, s_xT[it], W("s_wv"), row("s_bv")).then_inc(*S["s_qkv"].up(now))
                for it in items:
                    pe.wait_ge(*S["s_q"].at(now, it + 1))
                    pe.wait_ge(*S["s_kv"].at(now, it + 1))
                    for t in tiles:
                        b = t // HALF
                        mm = pe.matmul(bank(it, b)[:, t % HALF * T:(t % HALF + 1) * T],
                                       lhsT=s_qT[it][:, t * P:(t + 1) * P], rhs=s_kT[it][:, b * T:(b + 1) * T],
                                       start=True, stop=True)
                    mm.then_inc(*S["s_scores"].up(now))
                for it in items:
                    pe.wait_ge(*S["s_exp"].at(now, it + 1))
                    for t in tiles:
                        b = t // HALF
                        for k in range(HALF):
                            o = bank(it, 2 + b)[:, k * T + t % HALF * P:k * T + (t % HALF + 1) * P]
                            mm = pe.transpose(o, s_S[it][:, t, k * P:(k + 1) * P], ident)
                    mm.then_inc(*S["s_PT"].up(now))
                for it in items:
                    pe.wait_ge(*S["s_PT_kept"].at(now, it + 1))
                    for t in tiles:
                        b = t // HALF
                        for k in range(HALF):
                            mm = pe.matmul(bank(it, 0)[:, t * P:(t + 1) * P],
                                           lhsT=s_PT[it][:, b, k, t % HALF * P:(t % HALF + 1) * P],
                                           rhs=s_v[it][:, HALF * b + k], start=(k == 0), stop=(k == HALF - 1))
                    mm.then_inc(*S["y_made"].up(now))

            def heads_and_experts(now):
                for it in items:
                    pe.wait_ge(*S["x_made"].at(now, 4 * ITEMS + it + 1))
                    transpose4(it, xs[:, it], 0).then_inc(*S["xT_made"].up(now))
                for it in items:
                    pe.wait_ge(*S["xT_kept"].at(now, 5 * ITEMS + it + 1))
                    for n, w in ((1, "m_wq"), (2, "m_wk")):
                        pe.matmul(bank(it, n), lhsT=W(w), rhs=m_xT[it], start=True, stop=True)
                    tokens_out(it, 3, m_xT[it], W("m_wv"), row("m_bv")).then_inc(*S["m_qkv"].up(now))
                    for t in tiles:
                        o = bank(it, 0)[:, t * EXPERTS:(t + 1) * EXPERTS]
                        pe.matmul(o, lhsT=m_xT[it][:, t * P:(t + 1) * P], rhs=W("m_wg"), start=True, stop=False)
                        mm = pe.matmul(o, lhsT=one_row, rhs=row("m_bg"), start=False, stop=True)
                    mm.then_inc(*S["logits"].up(now))
                for it in items:
                    pe.wait_ge(*S["w_made"].at(now, ITEMS + it + 1))
                    pe.wait_ge(*S["m_qkv_kept"].at(now, it + 1))
                    for t in tiles:
                        mm = pe.transpose(bank(it, 3)[0:EXPERTS, t * P:(t + 1) * P], r_w[it][:, t], ident)
                    mm.then_inc(*S["m_wT"].up(now))
                for it in items:
                    pe.wait_ge(*S["m_wT_kept"].at(now, it + 1))
                    tokens_out(it, 2, m_cT[it], bexp[:]).then_inc(*S["m_bias"].up(now))
                for t in tiles:
                    moe_step(now, 1, t)
                for n in range(MAX_STEPS):
                    max_step(now, 0, n)
                rows_of_maxima(now, 0)
                ahead = MAX_STEPS // 2
                for n in range(ahead):
                    max_step(now, 1, n)
                head_steps(now, 0, 0, 1)
                for n in range(ahead, MAX_STEPS):
                    max_step(now, 1, n)
                    at = (n - ahead) * 3
                    head_steps(now, 0, at + 1, at + 4)
                rows_of_maxima(now, 1)
                head_steps(now, 0, (MAX_STEPS - ahead) * 3 + 1, HEAD_STEPS + 2)
                for t in tiles:
                    moe_step(now, 0, t)
                head_steps(now, 1, 0, HEAD_STEPS + 2)

            def moe_step(now, it, t):
                if t >= 2:
                    pe.wait_ge(*S[f"m_moe_sum{it}"].at(now, (t - 1) * EXPERTS))
                elif it == 0:
                    pe.wait_ge(*S["m_attention"].at(now, 1))
                elif t == 1:
                    pe.wait_ge(*S["m_acc"].at(now, it + 1))
                for n in range(2):
                    mm = pe.matmul(bank(it, 2 * (t % 2) + n), lhsT=m_xT[it][:, t * P:(t + 1) * P],
                                   rhs=W("m_we")[:, n * BANK:(n + 1) * BANK], start=True, stop=True)
                mm.then_inc(*S[f"m_moe{it}"].up(now))

            def max_step(now, it, n):
                q, t = n // TILES, n % TILES
                if n == 0:
                    pe.wait_ge(*S[f"m_stacked{it}"].at(now, 16 * (2 * TERMS + 1)))
                if n >= 2:
                    pe.wait_ge(*S[f"m_max_read{it}"].at(now, n - 1))
                elif it == 1:
                    pe.wait_ge(*S["m_moe_sum1"].at(now, TILES * EXPERTS))
                elif n == 1:
                    pe.wait_ge(*S["m_acc"].at(now, it + 1))
                b = t // HALF
                for h in range(4):
                    mm = pe.matmul(bank(it, 2 * (n % 2) + h // 2)[:, h % 2 * T:(h % 2 + 1) * T],
                                   lhsT=m_Q[it][0:STACK, 4 * q + h, t * P:(t + 1) * P],
                                   rhs=m_K[it][0:STACK, 4 * q + h, b * T:(b + 1) * T], start=True, stop=True)
                mm.then_inc(*S[f"m_max_scores{it}"].up(now))

            def rows_of_maxima(now, it):
                pe.wait_ge(*S[f"m_max_read{it}"].at(now, MAX_STEPS))
                for t in tiles:
                    mm = pe.transpose(bank(it, 0)[0:SH, t * P:(t + 1) * P], m_mx[it][:, t], ident)
                mm.then_inc(*S["m_mxT"].up(now))

            def head_steps(now, it, first, end):
                for n in range(first, end):
                    if n == 0:
                        pe.wait_ge(*S[f"m_max_stacked{it}"].at(now, 16))
                    if n >= 2:
                        g = n - 2
                        pe.wait_ge(*S[f"m_exp{it}"].at(now, g + 1))
                        h, b = g // IB, g % IB
                        for t in range(HALF):
                            at = (t * SH + h) * (SD + 1)
                            for k in range(HALF):
                                mm = pe.matmul(bank(it, 2 + b)[:, at:at + SD + 1],
                                               lhsT=m_P[it][:, g % 2, k, t * P:(t + 1) * P],
                                               rhs=m_V[it][:, HALF * b + k, h, :], start=(k == 0), stop=(k == HALF - 1))
                        mm.then_inc(*S[f"m_pv{it}"].up(now))
                    if n < HEAD_STEPS:
                        h, b = n // IB, n % IB
                        for k in range(HALF):
                            at = b * T + k * P
                            mm = pe.matmul(bank(it, n % 2)[:, k * T:(k + 1) * T], lhsT=m_K[it][:, h, at:at + P],
                                           rhs=m_Q[it][:, h, b * T:(b + 1) * T], start=True, stop=True)
                        mm.then_inc(*S[f"m_scores{it}"].up(now))

            pe.sem_inc(S["g_qk_made"].sem, 1)
            pe.wait_ge(S["consts_loaded"].sem, 16 * 7)
            with pe.Fori(0, ROUNDS) as r:
                now = Now(r)
                linear_attention(now)
                if LAST > 1:
                    cross_attention(now, 1, 0)
                if LAST > 2:
                    experts(now)
                if LAST > 3:
                    self_attention(now)
                if LAST > 4:
                    cross_attention(now, 4, 1)
                if LAST > 5:
                    heads_and_experts(now)

        @block.scalar
        def _(act):
            act.preload_act_table_set("natural_log_exp_and_others")
            act.wait_ge(S["consts_loaded"].sem, 16 * 7)

            def power(own, out_, in_, scale, bias):
                act.activation(out_, in_, ACT.Ln, scale=scale, bias=bias).then_inc(*own.next())
                act.wait_ge(*own.all())
                return act.activation(out_, out_, ACT.Exp, scale=-0.5)

            def layernorm(own, now, s):
                for it in items:
                    act.wait_ge(*S["var_made"].at(now, s * ITEMS + it + 1))
                    power(own, rstd[:, it, 0:TILES], mv[:, it, 0:TILES, 1], 1.0, EPS
                          ).then_inc(*S["rstd_made"].up(now))

            def keep_xT(now, s, dst, scale=1.0, bias=0.0):
                for it in items:
                    act.wait_ge(*S["xT_made"].at(now, s * ITEMS + it + 1))
                    act.activation(dst[it], bank(it, 0), ACT.Identity, scale=scale, bias=bias
                                   ).then_inc(*S["xT_kept"].up(now))

            def linear_attention(own, now):
                keep_xT(now, 0, a_xT)
                for it in items:
                    act.wait_ge(*S["a_qkv"].at(now, it + 1))
                    act.activation(a_sq[it], bank(it, 3), ACT.Square).then_inc(*S["a_sq"].up(now))
                    act.activation(a_qT[it], bank(it, 1), ACT.Copy)
                    act.activation(a_vT[it], bank(it, 2), ACT.Copy).then_inc(*S["a_qv_kept"].up(now))
                for it in items:
                    act.wait_ge(*S["a_ss_kept"].at(now, it + 1))
                    act.activation(a_rn[it], a_rn[it], ACT.Ln).then_inc(*own.next())
                    act.wait_ge(*own.all())
                    act.activation(a_rn[it], a_rn[it], ACT.Exp, scale=-0.5).then_inc(*S["a_rn"].up(now))
                for it in items:
                    act.wait_ge(*S["a_kn"].at(now, it + 1))
                    act.activation(a_e1[it], a_kn[it], ACT.Exp, scale=neg("a_wgamma"), bias=neg("a_bgamma"))
                    act.activation(a_e2[it], a_kn[it], ACT.Exp, scale=col("a_wlambda"), bias=col("a_blambda")
                                   ).then_inc(*S["a_e"].up(now))
                for it in items:
                    act.wait_ge(*S["a_den"].at(now, it + 1))
                    act.activation(a_e1[it], a_den[it], ACT.Ln).then_inc(*S["a_L"].up(now))
                for it in items:
                    act.wait_ge(*S["a_D"].at(now, it + 1))
                    act.activation(a_E[it], a_D[it], ACT.Exp).then_inc(*S["a_E"].up(now))
                    act.activation(a_Ep[it], a_D[it][:, 0:4], ACT.Exp, scale=-1.0).then_inc(*S["a_Ep"].up(now))
                for it in items:
                    act.wait_ge(*S["a_U"].at(now, it + 1))
                    act.activation(a_U[it][:, 0:4], bank(it, 0).rearrange("p (a b) -> p a b", b=P), ACT.Copy)
                    act.activation(a_U[it][:, 4:6], bank(it, 1)[:, 0:2 * P].rearrange("p (a b) -> p a b", b=P), ACT.Copy
                                   ).then_inc(*S["a_U_kept"].up(now))
                layernorm(own, now, 0)

            def cross_attention(own, now, s, c):
                if c:
                    for it in items:
                        act.wait_ge(*S["l_var"].at(now, it + 1))
                        power(own, rstd[:, it], mv[:, it, :, 1], 1.0, EPS).then_inc(*S["l_rstd"].up(now))
                    for it in items:
                        act.wait_ge(*S["xT_made"].at(now, s * ITEMS + it + 1))
                        act.activation(x_cT[it], bank(it, 1)[0:CC, 0:P], ACT.Identity, scale=ccols[:, 0:1],
                                       bias=ccols[:, 1:2])
                        act.activation(x_xT[it], bank(it, 0), ACT.Identity, scale=col("lat_g"), bias=col("lat_b")
                                       ).then_inc(*S["xT_kept"].up(now))
                else:
                    keep_xT(now, s, x_xT)
                for it in items:
                    act.wait_ge(*S["x_q"].at(now, c * ITEMS + it + 1))
                    act.activation(x_qT[it], bank(it, 2), ACT.Copy).then_inc(*S["x_q_kept"].up(now))
                for b in range(IB):
                    for it in items:
                        act.wait_ge(*S["x_less_max"].at(now, (c * IB + b) * ITEMS + it + 1))
                        p = x_P[it][:, HALF * b:HALF * (b + 1)]
                        act.activation(p, p, ACT.Exp, scale=float(XD) ** -0.5).then_inc(*S["x_exp"].up(now))
                for b in range(IB):
                    for it in items:
                        act.wait_ge(*S["x_PT"].at(now, (c * IB + b) * ITEMS + it + 1))
                        act.activation(x_PT[it][:, b].rearrange("p (a h) t -> p a (h t)", a=2),
                                       bank(it, 2 * b, 2 * b + 2), ACT.Copy).then_inc(*S["x_PT_kept"].up(now))
                for it in items:
                    act.wait_ge(*S["x_o"].at(now, c * ITEMS + it + 1))
                    act.activation(x_yT[it], bank(it, 0), ACT.Copy).then_inc(*S["x_o_kept"].up(now))
                layernorm(own, now, s)

            def rms(own, now, it, src, done):
                for t in tiles:
                    act.activation(g_s[it][:, t * P:(t + 1) * P], src[:, t * P:(t + 1) * P], ACT.Square,
                                           accum_out=g_ss[it][:, t:t + 1]).then_inc(*own.next())
                act.wait_ge(*own.all())
                power(own, g_r[it], g_ss[it], 1.0 / D, EPS).then_inc(*S[done].up(now))

            def experts(own, now):
                for it in items:
                    act.wait_ge(*S["x_made"].at(now, ITEMS + it + 1))
                    rms(own, now, it, xs[:, it].rearrange("p t d -> p (t d)"), "g_rms")
                keep_xT(now, 2, g_xT, scale=col("g_norm"))
                for it in items:
                    act.wait_ge(*S["less_max"].at(now, it + 1))
                    act.activation(r_E[it], r_lg[it], ACT.Exp).then_inc(*S["gate_exp"].up(now))
                keep_tokens(now, 0)
                keep_scatter(now, 0, 0)
                with act.Fori(0, EXPERTS) as e:
                    expert_step(now.inner(e, EXPERTS), e)
                for it in items:
                    act.wait_ge(*S["g_out"].at(now, it + 1))
                    rms(own, now, it, bank(it, 0), "g_rms")
                for it in items:
                    act.wait_ge(*S["g_onT"].at(now, it + 1))
                    act.activation(g_onT[it], bank(it, 1), ACT.Copy, scale=col("g_gnorm")
                                   ).then_inc(*S["g_onT_kept"].up(now))
                layernorm(own, now, 2)

            def keep_tokens(now, done):
                for it in items:
                    act.wait_ge(*S["g_xe"].at(now, done + it + 1))
                    act.activation(g_xe[it].rearrange("p b s -> p (b s)"), bank(it, 3)[:, 0:IB * CAP], ACT.Copy,
                                   scale=col("g_norm")).then_inc(*S["g_xe_kept"].up(now))

            def keep_scatter(now, done, e):
                for it in items:
                    act.wait_ge(*S["g_scatter"].at(now, done + it + 1))
                    act.activation(g_PwT[it][:, bass.ds(e, 1)].rearrange("p a n -> p (a n)"), bank(it, 1), ACT.Copy
                                   ).then_inc(*S["g_scatter_kept"].up(now))

            def expert_step(now, e):
                act.wait_ge(*S["g_qk_made"].at(now, 0))
                act.activation(wk_now[:], W("g_wk")[:, bass.ds(e * D, D)], ACT.Copy).then_inc(*S["g_wk"].up(now))
                for it in items:
                    act.wait_ge(*S["g_f_made"].at(now, it + 1))
                    act.activation(g_ln[it][:, 1], bank(it, 3), ACT.Exp, scale=-1.0).then_inc(*S["g_exp_f"].up(now))
                for it in items:
                    act.wait_ge(*S["g_qk_made"].at(now, it + 1))
                    act.activation(g_ln[it][:, 0], bank(it, 2), ACT.Exp, scale=-1.0).then_inc(*S["g_exp_qk"].up(now))
                    act.wait_ge(*S["g_cut_f"].at(now, it + 1))
                    act.activation(g_ln[it][:, 1], g_ln[it][:, 1], ACT.Ln, bias=1.0).then_inc(*S["g_ln_f"].up(now))
                for it in items:
                    act.wait_ge(*S["g_v_made"].at(now, it + 1))
                    act.activation(g_v[it].rearrange("p b d -> p (b d)"), bank(it, 0)[:, 0:IB * P], ACT.Copy
                                   ).then_inc(*S["g_v"].up(now))
                    act.wait_ge(*S["g_cut_qk"].at(now, it + 1))
                    act.activation(g_ln[it][:, 0], g_ln[it][:, 0], ACT.Ln, bias=1.0).then_inc(*S["g_ln_qk"].up(now))
                    act.wait_ge(*S["g_sp"].at(now, it + 1))
                    act.activation(g_s[it], g_sp[it][:, 1], ACT.Exp, scale=-1.0 / GATE_NORM)
                for it in items:
                    act.wait_ge(*S["g_sp_qk"].at(now, it + 1))
                    act.activation(g_eqk[it], g_sp[it][:, 0], ACT.Exp, scale=-1.0).then_inc(*S["g_sig"].up(now))
                    act.wait_ge(*S["g_decay"].at(now, it + 1))
                    act.activation(g_inv[it], bank(it, 1), ACT.Exp, scale=1.0 / GATE_NORM)
                    act.activation(g_dec[it], bank(it, 1), ACT.Exp, scale=-1.0 / GATE_NORM
                                   ).then_inc(*S["g_dec"].up(now))
                for it in items:
                    act.wait_ge(*S["g_ok"].at(now, it + 1))
                    act.activation(g_sT[it].rearrange("p b a n -> p (b a n)"), bank(it, 1), ACT.Copy
                                   ).then_inc(*S["g_sT"].up(now))
                keep_tokens(now, ITEMS)
                for it in items:
                    act.wait_ge(*S["g_less_max"].at(now, it + 1))
                    act.activation(g_ok[it], g_ok[it], ACT.Exp).then_inc(*S["g_p"].up(now))
                keep_scatter(now, ITEMS, e + 1)
                for it in items:
                    act.wait_ge(*S["g_qdT"].at(now, it + 1))
                    act.activation(g_qT[it].rearrange("p b a n -> p (b a n)"), bank(it, 2), ACT.Copy
                                   ).then_inc(*S["g_qdT_kept"].up(now))

            def self_attention(own, now):
                keep_xT(now, 3, s_xT)
                for it in items:
                    act.wait_ge(*S["s_qkv"].at(now, it + 1))
                    act.activation(s_kT[it], bank(it, 2), ACT.Identity, bias=col("s_bk"))
                    act.activation(s_v[it].rearrange("p t d -> p (t d)"), bank(it, 3), ACT.Copy
                                   ).then_inc(*S["s_kv"].up(now))
                for it in items:
                    act.wait_ge(*S["s_max"].at(now, it + 1))
                    for t in tiles:
                        e = act.activation(s_S[it][:, t], s_S[it][:, t], ACT.Exp, bias=s_mx[it][:, t:t + 1],
                                           accum_out=s_sum[it][:, t:t + 1])
                    e.then_inc(*S["s_exp"].up(now))
                for it in items:
                    act.wait_ge(*S["s_PT"].at(now, it + 1))
                    act.activation(s_PT[it].rearrange("p b k t -> p b (k t)"), bank(it, 2, 4), ACT.Copy
                                   ).then_inc(*S["s_PT_kept"].up(now))
                layernorm(own, now, 3)

            def heads_and_experts(own, now):
                keep_xT(now, 5, m_xT)
                for it in items:
                    act.wait_ge(*S["m_qkv"].at(now, it + 1))
                    for side, b in ((0, "m_bq"), (1, "m_bk")):
                        act.activation(m_parts[it][:, side, 0], bank(it, 1 + side), ACT.Identity, bias=col(b))
                        i = act.activation(m_qk[it][:, side], bank(it, 1 + side), ACT.Identity, bias=col(b))
                    i.then_inc(*S["m_qk"].up(now))
                    for t in tiles:
                        e = act.activation(m_V[it][:, t, :, 0:SD],
                                           bank(it, 3)[:, t * P:(t + 1) * P].rearrange("p (h d) -> p h d", d=SD),
                                           ACT.Copy)
                    e.then_inc(*S["m_qkv_kept"].up(now))
                for it in items:
                    act.wait_ge(*S["less_max"].at(now, ITEMS + it + 1))
                    act.activation(r_E[it], r_lg[it], ACT.Exp).then_inc(*S["gate_exp"].up(now))
                for it in items:
                    act.wait_ge(*S["m_wT"].at(now, it + 1))
                    act.activation(m_cT[it], bank(it, 3)[0:EXPERTS], ACT.Copy).then_inc(*S["m_wT_kept"].up(now))
                for it in items:
                    act.wait_ge(*S["m_mxT"].at(now, it + 1))
                    act.activation(m_row[it], bank(it, 0)[0:SH], ACT.Copy, scale=-1.0).then_inc(*S["m_row"].up(now))
                    for n in range(HEAD_STEPS):
                        act.wait_ge(*S[f"m_scores{it}"].at(now, n + 1))
                        if n >= 2:
                            act.wait_ge(*S[f"m_pv{it}"].at(now, n - 1))
                        act.activation(m_P[it][:, n % 2].rearrange("p k t -> p (k t)"), bank(it, n % 2), ACT.Exp,
                                       scale=float(SD) ** -0.5).then_inc(*S[f"m_exp{it}"].up(now))
                layernorm(own, now, 5)

            with act.Fori(0, ROUNDS) as r:
                now = Now(r)
                own = Own(S["act_own"], now)
                linear_attention(own, now)
                if LAST > 1:
                    cross_attention(own, now, 1, 0)
                if LAST > 2:
                    experts(own, now)
                if LAST > 3:
                    self_attention(own, now)
                if LAST > 4:
                    cross_attention(own, now, 4, 1)
                if LAST > 5:
                    heads_and_experts(own, now)

        @block.vector
        def _(v):
            def stats_of(own, out_, mv_, src):
                v.bn_stats(out_, src).then_inc(*own.next())

            def normalise(own, now, s):
                for it in items:
                    for t in tiles:
                        v.bn_stats(stats[:, it, t], zs[:, it, t]).then_inc(*own.next())
                    v.wait_ge(*own.all())
                    v.memset(tick[:], 0.0)
                    for t in tiles:
                        i = v.bn_aggr(mv[:, it, t], stats[:, it, t])
                    i.then_inc(*S["var_made"].up(now))
                for it in items:
                    v.wait_ge(*S["rstd_made"].at(now, s * ITEMS + it + 1))
                    if s == 0:
                        v.wait_ge(*S["stored"].at(now, 0))
                    for t in tiles:
                        i = v.tensor_scalar(xs[:, it, t], zs[:, it, t], mv[:, it, t, 0:1], rstd[:, it, t:t + 1],
                                            ALU.subtract, ALU.mult)
                    i.then_inc(*S["x_made"].up(now))

            def layernorm(own, now, s, y_bank):
                for it in items:
                    v.wait_ge(*S["y_made"].at(now, s * ITEMS + it + 1 if s < 5 else 0))
                    x_old = x_in if s == 0 else xs
                    i = v.tensor_tensor(zs[:, it].rearrange("p t d -> p (t d)"), bank(it, y_bank),
                                        x_old[:, it].rearrange("p t d -> p (t d)"), ALU.add)
                    if s == 0:
                        i.then_inc(*S["x_free"].up(now))
                        v.wait_ge(*S["x_free"].at(now, it + 1))
                    else:
                        i.then_inc(*own.next())
                        v.wait_ge(*own.all())
                normalise(own, now, s)

            def linear_attention(own, now):
                for it in items:
                    v.wait_ge(*S["a_ss"].at(now, it + 1))
                    v.tensor_scalar(a_rn[it], bank(it, 0), 1e-24, 1e12, ALU.max, ALU.mult
                                    ).then_inc(*S["a_ss_kept"].up(now))
                for it in items:
                    v.wait_ge(*S["a_rn"].at(now, it + 1))
                    v.scalar_tensor_tensor(a_kn[it], in0=bank(it, 3), scalar=1e6, in1=a_rn[it], op0=ALU.mult,
                                           op1=ALU.mult).then_inc(*S["a_kn"].up(now))
                for it in items:
                    v.wait_ge(*S["a_e"].at(now, it + 1))
                    v.tensor_scalar(a_e1[it], a_e1[it], 1.0, None, ALU.add).then_inc(*own.next())
                    v.wait_ge(*own.all())
                    v.scalar_tensor_tensor(a_den[it], in0=a_e2[it], scalar=1.0, in1=a_e1[it], op0=ALU.add,
                                           op1=ALU.mult).then_inc(*S["a_den"].up(now))
                    v.wait_ge(*S["a_den"].at(now, it + 1))
                    v.reciprocal(a_e2[it], a_den[it]).then_inc(*own.next())
                    v.wait_ge(*own.all())
                    v.scalar_tensor_tensor(a_um[it], in0=a_e2[it], scalar=1.0, in1=a_kn[it],
                                                   op0=ALU.subtract, op1=ALU.mult).then_inc(*own.next())
                for it in items:
                    v.wait_ge(*S["a_L"].at(now, it + 1))
                    for b in range(IB):
                        v.tensor_tensor_scan(a_G[it][:, b * T:(b + 1) * T], K("ones"),
                                                     a_e1[it][:, b * T:(b + 1) * T], 0.0, ALU.mult, ALU.add).then_inc(*own.next())
                    v.wait_ge(*own.all())
                    G = a_G[it].rearrange("p (n t) -> p n t", t=P)
                    mid = G[:, :, P // 2 - 1:P // 2]
                    v.tensor_tensor(a_D[it][:, 0:4], G, mid.broadcast_to([P, 4, P]), ALU.subtract)
                    v.tensor_tensor(a_D[it][:, 4:6], G[:, 0:4:2], mid[:, 1:4:2].broadcast_to([P, 2, P]),
                                    ALU.subtract).then_inc(*S["a_D"].up(now))
                for it in items:
                    v.wait_ge(*S["a_E"].at(now, it + 1))
                    um = a_um[it].rearrange("p (n t) -> p n t", t=P)
                    v.tensor_tensor(a_UT[it][:, 0:4], a_E[it][:, 0:4], um, ALU.mult)
                    v.tensor_tensor(a_UT[it][:, 4:6], a_E[it][:, 4:6], um[:, 0:4:2], ALU.mult
                                    ).then_inc(*S["a_UT"].up(now))
                for b in range(IB):
                    for it in items:
                        v.wait_ge(*S["a_A"].at(now, b * ITEMS + it + 1))
                        v.tensor_tensor(a_Am[it][:, b], bank(it, 2, 4)[:, :, 0:3 * P], over(K("decay_mask"), 1, 2),
                                        ALU.mult).then_inc(*S["a_Am"].up(now))
                for it in items:
                    v.wait_ge(*S["a_y"].at(now, it + 1))
                    v.wait_ge(*S["a_Ep"].at(now, it + 1))
                    v.tensor_tensor(a_yT[it], bank(it, 0), a_Ep[it].rearrange("p n t -> p (n t)"), ALU.mult
                                    ).then_inc(*S["a_yT"].up(now))
                layernorm(own, now, 0, 1)

            def cross_attention(own, now, s, c):
                if c:
                    for it in items:
                        v.wait_ge(*S["x_made"].at(now, (s - 1) * ITEMS + it + 1))
                        v.wait_ge(*S["ctx_loaded"].at(now, ITEMS * 32))
                        for t in tiles:
                            v.bn_stats(stats[:, it, t], xs[:, it, t]).then_inc(*own.next())
                        v.bn_stats(stats[:, it, TILES], ctx_k[:, it]).then_inc(*own.next())
                        v.wait_ge(*own.all())
                        v.memset(tick[:], 0.0)
                        for t in range(TILES + 1):
                            i = v.bn_aggr(mv[:, it, t], stats[:, it, t])
                        i.then_inc(*S["l_var"].up(now))
                    for it in items:
                        v.wait_ge(*S["l_rstd"].at(now, it + 1))
                        for t in tiles:
                            v.tensor_scalar(x_xn[it][:, t], xs[:, it, t], mv[:, it, t, 0:1], rstd[:, it, t:t + 1],
                                            ALU.subtract, ALU.mult)
                        v.tensor_scalar(x_cn[it], ctx_k[:, it], mv[:, it, TILES, 0:1], rstd[:, it, TILES:TILES + 1],
                                        ALU.subtract, ALU.mult).then_inc(*S["l_made"].up(now))
                for it in items:
                    v.wait_ge(*S["x_kv"].at(now, c * ITEMS + it + 1))
                    for b in range(IB):
                        v.tensor_tensor(x_K[it][:, b].rearrange("p (h k) -> p h k", k=KV),
                                        over(bank(it, 1)[:, b * KV:(b + 1) * KV], 1, XH),
                                        over(K("kv_heads"), 2, KV), ALU.mult)
                    for b in range(IB):
                        i = v.tensor_tensor(x_V[it][:, b], over(bank(it, 3)[:, b * D:(b + 1) * D], 1, 4),
                                            K("v_heads").rearrange("p (a d) -> p a d", d=D), ALU.mult)
                    i.then_inc(*S["x_kv_kept"].up(now))
                for b in range(IB):
                    for it in items:
                        v.wait_ge(*S["x_scores"].at(now, (c * IB + b) * ITEMS + it + 1))
                        both = slice(HALF * b, HALF * (b + 1))
                        sc = bank(it, HALF * b, HALF * (b + 1)).rearrange("p t (h k) -> p t h k", k=KV)
                        mx = x_mx[it][:, both]
                        v.tensor_reduce(mx, sc, AX.X, ALU.max).then_inc(*own.next())
                        v.wait_ge(*own.all())
                        v.tensor_tensor(x_P[it][:, both].rearrange("p t (h k) -> p t h k", k=KV), sc,
                                        over(mx, 3, KV), ALU.subtract).then_inc(*S["x_less_max"].up(now))
                for b in range(IB):
                    for it in items:
                        v.wait_ge(*S["x_exp"].at(now, (c * IB + b) * ITEMS + it + 1))
                        both = slice(HALF * b, HALF * (b + 1))
                        v.tensor_reduce(x_sm[it][:, both],
                                                x_P[it][:, both].rearrange("p t (h k) -> p t h k", k=KV),
                                                AX.X, ALU.add).then_inc(*own.next())
                        v.wait_ge(*own.all())
                        v.reciprocal(x_rs[it][:, both], x_sm[it][:, both]).then_inc(*S["x_rs"].up(now))
                layernorm(own, now, s, 1)

            def routing(own, now, use, lg_bank, over_all):
                for it in items:
                    v.wait_ge(*S["logits"].at(now, use * ITEMS + it + 1))
                    lg = bank(it, lg_bank)[:, 0:TILES * EXPERTS].rearrange("p (t e) -> p t e", e=EXPERTS)
                    v.tensor_reduce(r_mx[it], lg, AX.X, ALU.max).then_inc(*own.next())
                    v.wait_ge(*own.all())
                    v.tensor_tensor(r_lg[it], lg, over(r_mx[it], 2, EXPERTS), ALU.subtract
                                    ).then_inc(*S["less_max"].up(now))
                    v.wait_ge(*S["less_max"].at(now, use * ITEMS + it + 1))
                    other, this = over(r_lg[it], 2, EXPERTS), over(r_lg[it], 3, EXPERTS)
                    v.tensor_tensor(r_gt[it], other, this, ALU.is_gt).then_inc(*own.next())
                    v.tensor_tensor(r_eq[it], other, this, ALU.is_equal).then_inc(*own.next())
                    v.wait_ge(*own.all())
                    v.tensor_tensor(r_eq[it], r_eq[it],
                                            over(K("tie").rearrange("p (i j) -> p i j", j=EXPERTS), 1, TILES),
                                            ALU.mult).then_inc(*own.next())
                    v.wait_ge(*own.all())
                    v.tensor_tensor(r_gt[it], r_gt[it], r_eq[it], ALU.add).then_inc(*own.next())
                    v.wait_ge(*own.all())
                    v.tensor_reduce(r_rank[it], r_gt[it], AX.X, ALU.add).then_inc(*own.next())
                    v.wait_ge(*own.all())
                    v.tensor_scalar(r_sel[it], r_rank[it], TOPK - 0.5, None, ALU.is_lt
                                    ).then_inc(*S["sel_made"].up(now))
                for it in items:
                    v.wait_ge(*S["sel_made"].at(now, use * ITEMS + it + 1))
                    v.wait_ge(*S["gate_exp"].at(now, use * ITEMS + it + 1))
                    v.tensor_tensor(r_w[it], r_E[it], r_sel[it], ALU.mult).then_inc(*own.next())
                    v.wait_ge(*own.all())
                    v.tensor_reduce(r_den[it], r_E[it] if over_all else r_w[it], AX.X, ALU.add).then_inc(*own.next())
                    v.wait_ge(*own.all())
                    v.reciprocal(r_den[it], r_den[it]).then_inc(*own.next())
                    v.wait_ge(*own.all())
                    v.tensor_tensor(r_w[it], r_w[it], over(r_den[it], 2, EXPERTS), ALU.mult
                                    ).then_inc(*S["w_made"].up(now))

            def experts(own, now):
                for it in items:
                    v.wait_ge(*S["g_rms"].at(now, it + 1))
                    v.tensor_tensor(g_xn[it], xs[:, it], over(g_r[it], 2, D), ALU.mult).then_inc(*S["g_xn"].up(now))
                routing(own, now, 0, 1, False)
                for it in items:
                    v.wait_ge(*S["g_count"].at(now, it + 1))
                    cnt = bank(it, 2)[:, 0:TILES * EXPERTS].rearrange("p (t e) -> p t e", e=EXPERTS)
                    real = g_slot[it][:, :, 0:EXPERTS]
                    v.memset(g_slot[it][:, :, EXPERTS:], 0.0)
                    v.memset(g_w[it][:, :, EXPERTS:], 0.0)
                    v.tensor_scalar(real, cnt, -1.0, float(CAP + 1), ALU.mult, ALU.add).then_inc(*own.next())
                    v.wait_ge(*own.all())
                    v.tensor_tensor(real, real, r_sel[it], ALU.mult).then_inc(*own.next())
                    v.wait_ge(*S["w_made"].at(now, it + 1))
                    v.tensor_copy(g_w[it][:, :, 0:EXPERTS], r_w[it]).then_inc(*own.next())
                    v.wait_ge(*own.all())
                    v.tensor_scalar(g_slot[it], g_slot[it], -1.0, None, ALU.add).then_inc(*S["g_slot"].up(now))
                for it in items:
                    v.wait_ge(*S["g_slot"].at(now, it + 1))
                    place(it, 0).then_inc(*S["g_place"].up(now))
                for it in items:
                    v.wait_ge(*S["g_scatter"].at(now, it + 1))
                    place(it, 1).then_inc(*S["g_place"].up(now))
                with v.Fori(0, EXPERTS) as e:
                    inner = now.inner(e, EXPERTS)
                    expert_step(Own(S["dve_own_experts"], inner), inner, e)
                for it in items:
                    v.wait_ge(*S["g_rms"].at(now, ITEMS + it + 1))
                    v.tensor_tensor(g_xn[it], bank(it, 0).rearrange("p (t d) -> p t d", d=D), over(g_r[it], 2, D),
                                    ALU.mult).then_inc(*S["g_on"].up(now))
                layernorm(own, now, 2, 2)

            def place(it, e):
                for t in tiles:
                    slot, w = (a[it][:, t, bass.ds(e, 1)] for a in (g_slot, g_w))
                    v.tensor_scalar(g_Pw[it][:, t], K("slot"), slot, w, ALU.is_equal, ALU.mult)
                    i = v.tensor_scalar(g_P[it][:, t], K("slot"), slot, None, ALU.is_equal)
                return i

            def expert_step(own, now, e):
                for it in items:
                    v.wait_ge(*S["g_exp_f"].at(now, it + 1))
                    v.tensor_scalar(g_ln[it][:, 1], g_ln[it][:, 1], 1e18, None, ALU.min).then_inc(*S["g_cut_f"].up(now))
                for it in items:
                    v.wait_ge(*S["g_exp_qk"].at(now, it + 1))
                    v.tensor_scalar(g_ln[it][:, 0], g_ln[it][:, 0], 1e18, None, ALU.min).then_inc(*S["g_cut_qk"].up(now))
                    v.wait_ge(*S["g_ln_f"].at(now, it + 1))
                    v.scalar_tensor_tensor(g_sp[it][:, 1], in0=bank(it, 3), scalar=-1.0, in1=g_ln[it][:, 1],
                                           op0=ALU.mult, op1=ALU.max).then_inc(*S["g_sp"].up(now))
                for it in items:
                    v.wait_ge(*S["g_ln_qk"].at(now, it + 1))
                    v.scalar_tensor_tensor(g_sp[it][:, 0], in0=bank(it, 2), scalar=-1.0, in1=g_ln[it][:, 0],
                                           op0=ALU.mult, op1=ALU.max).then_inc(*S["g_sp_qk"].up(now))
                for it in items:
                    v.wait_ge(*S["g_sig"].at(now, it + 1))
                    v.tensor_tensor(g_qk[it].rearrange("p a b s -> p (a b s)"), bank(it, 2), g_eqk[it], ALU.mult
                                    ).then_inc(*S["g_qk"].up(now))
                for it in items:
                    v.wait_ge(*S["g_dec"].at(now, it + 1))
                    v.scalar_tensor_tensor(g_s[it], in0=g_s[it], scalar=1.0, in1=g_inv[it], op0=ALU.subtract,
                                           op1=ALU.mult).then_inc(*S["g_s"].up(now))
                for it in items:
                    v.wait_ge(*S["g_A"].at(now, it + 1))
                    mask_heads(it, 1.0).then_inc(*S["g_Am"].up(now))
                for it in items:
                    v.wait_ge(*S["g_ok"].at(now, it + 1))
                    v.scalar_tensor_tensor(g_ok[it], in0=bank(it, 0), scalar=-1.0, in1=g_dec[it],
                                                   op0=ALU.mult, op1=ALU.mult).then_inc(*own.next())
                    v.wait_ge(*own.all())
                    ok = g_ok[it].rearrange("p (h m) -> p h m", m=GM)
                    v.tensor_reduce(g_mx[it], ok, AX.X, ALU.max).then_inc(*own.next())
                    v.wait_ge(*own.all())
                    v.tensor_tensor(ok, ok, over(g_mx[it], 2, GM), ALU.subtract).then_inc(*S["g_less_max"].up(now))
                for it in items:
                    v.wait_ge(*S["g_p"].at(now, it + 1))
                    v.tensor_tensor(g_qd[it], g_ok[it], g_dec[it], ALU.mult).then_inc(*S["g_qd"].up(now))
                for it in items:
                    v.tensor_reduce(g_rs[it], g_ok[it].rearrange("p (h m) -> p h m", m=GM), AX.X, ALU.add
                                    ).then_inc(*own.next())
                    v.wait_ge(*own.all())
                    v.reciprocal(g_rs[it], g_rs[it]).then_inc(*own.next())
                for it in items:
                    v.wait_ge(*S["g_T"].at(now, it + 1))
                    mask_heads(it, -1.0).then_inc(*S["g_Tm"].up(now))
                v.wait_ge(*own.all())
                for it in items:
                    v.wait_ge(*S["g_scatter"].at(now, ITEMS + it + 1))
                    place(it, e + AHEAD).then_inc(*S["g_place"].up(now))
                    v.wait_ge(*S["g_ov"].at(now, it + 1))
                    o = g_o[it][:, bass.ds(e, 1)].rearrange("p a b (h d) -> p (a b h) d", d=GK)
                    v.tensor_tensor(o, bank(it, 0)[:, 0:IB * P].rearrange("p (h d) -> p h d", d=GK),
                                    over(g_rs[it], 2, GK), ALU.mult).then_inc(*S[f"g_o{it}"].up(now))

            def mask_heads(it, sign):
                for b in range(IB):
                    i = v.scalar_tensor_tensor(g_A[it][:, :, b], in0=bank(it, 0, 4)[:, :, b * CAP:(b + 1) * CAP],
                                               scalar=sign, in1=over(K("causal"), 1, GH), op0=ALU.mult, op1=ALU.mult)
                return i

            def self_attention(own, now):
                for it in items:
                    v.wait_ge(*S["s_qkv"].at(now, it + 1))
                    v.tensor_scalar(s_qT[it], bank(it, 1), col("s_bq"), 1.0 / D, ALU.add, ALU.mult
                                    ).then_inc(*S["s_q"].up(now))
                for it in items:
                    v.wait_ge(*S["s_scores"].at(now, it + 1))
                    v.tensor_tensor(s_S[it].rearrange("p (b t) n -> p b (t n)", b=IB), bank(it, 0, 2),
                                            over(K("no_self"), 1, IB), ALU.add).then_inc(*own.next())
                    v.wait_ge(*own.all())
                    v.tensor_reduce(s_mx[it], s_S[it], AX.X, ALU.max, negate=True).then_inc(*S["s_max"].up(now))
                for it in items:
                    v.wait_ge(*S["s_exp"].at(now, it + 1))
                    v.reciprocal(s_rs[it], s_sum[it]).then_inc(*own.next())
                for it in items:
                    v.wait_ge(*S["y_made"].at(now, 3 * ITEMS + it + 1))
                    v.wait_ge(*own.all())
                    for t in tiles:
                        v.scalar_tensor_tensor(zs[:, it, t], in0=bank(it, 0)[:, t * P:(t + 1) * P],
                                                       scalar=s_rs[it][:, t:t + 1], in1=xs[:, it, t],
                                                       op0=ALU.mult, op1=ALU.add).then_inc(*own.next())
                    v.wait_ge(*own.all())
                normalise(own, now, 3)

            def heads_and_experts(own, now):
                for it in items:
                    v.memset(m_V[it][:, :, :, SD:SD + 1], 1.0)
                for it in items:
                    v.wait_ge(*S["m_qk"].at(now, it + 1))
                    parts = m_parts[it]
                    v.tensor_tensor(m_r[it], m_qk[it], parts[:, :, 0], ALU.subtract).then_inc(*own.next())
                    v.wait_ge(*own.all())
                    v.tensor_copy(parts[:, :, 1], m_r[it]).then_inc(*own.next())
                    v.wait_ge(*own.all())
                    v.tensor_tensor(parts[:, :, 2], m_r[it], parts[:, :, 1], ALU.subtract
                                    ).then_inc(*S["m_split"].up(now))
                routing(own, now, 1, 0, True)
                for it in items:
                    v.wait_ge(*S["m_bias"].at(now, it + 1))
                    v.tensor_tensor(m_acc[it].rearrange("p t d -> p (t d)"), bank(it, 2),
                                    xs[:, it].rearrange("p t d -> p (t d)"), ALU.add).then_inc(*S["m_acc"].up(now))
                moe_sum(now, 1)
                for it in items:
                    for n in range(MAX_STEPS):
                        v.wait_ge(*S[f"m_max_scores{it}"].at(now, n + 1))
                        two = bank(it, 2 * (n % 2), 2 * (n % 2) + 2).rearrange("p a (h k) -> p a h k", k=T)
                        v.tensor_reduce(m_mx[it][:, n % TILES, n // TILES * 4:n // TILES * 4 + 4], two, AX.X, ALU.max
                                        ).then_inc(*S[f"m_max_read{it}"].up(now))
                for it in items:
                    v.wait_ge(*S[f"m_pv{it}"].at(now, HEAD_STEPS))
                    for b in range(IB):
                        o = bank(it, 2 + b)[:, 0:HALF * SH * (SD + 1)].rearrange("p (t h d) -> p t h d", t=HALF, d=SD + 1)
                        v.reciprocal(m_rec[it][:, b].unsqueeze(3), o[:, :, :, SD:SD + 1]).then_inc(*own.next())
                    v.wait_ge(*own.all())
                    for b in range(IB):
                        o = bank(it, 2 + b)[:, 0:HALF * SH * (SD + 1)].rearrange("p (t h d) -> p t h d", t=HALF, d=SD + 1)
                        i = v.tensor_tensor(zs[:, it, HALF * b:HALF * (b + 1)].rearrange("p t (h d) -> p t h d", d=SD),
                                            o[:, :, :, 0:SD], over(m_rec[it][:, b], 3, SD), ALU.mult)
                    i.then_inc(*S["m_attention"].up(now))
                    if it == 0:
                        moe_sum(now, 0)
                    v.wait_ge(*S["m_attention"].at(now, it + 1))
                    v.wait_ge(*S[f"m_moe_sum{it}"].at(now, TILES * EXPERTS))
                    v.tensor_tensor(zs[:, it], zs[:, it], m_acc[it], ALU.add).then_inc(*own.next())
                    v.wait_ge(*own.all())
                    v.tensor_tensor(zs[:, it], zs[:, it], m_acc2[it], ALU.add).then_inc(*own.next())
                v.wait_ge(*own.all())
                normalise(own, now, 5)

            def moe_sum(now, it):
                for t in tiles:
                    v.wait_ge(*S[f"m_moe{it}"].at(now, t + 1))
                    for e in range(EXPERTS):
                        acc = (m_acc, m_acc2)[e % 2][it][:, t]
                        product, weight = bank(it, 2 * (t % 2) + e // 4)[:, e % 4 * P:(e % 4 + 1) * P], r_w[it][:, t, e:e + 1]
                        if e == 0:
                            v.wait_ge(*S["m_acc"].at(now, it + 1))
                        elif e > 1:
                            v.wait_ge(*S[f"m_moe_sum{it}"].at(now, t * EXPERTS + e - 1))
                        if e == 1:
                            i = v.tensor_scalar(acc, product, weight, None, ALU.mult)
                        else:
                            i = v.scalar_tensor_tensor(acc, in0=product, scalar=weight, in1=acc, op0=ALU.mult, op1=ALU.add)
                        i.then_inc(*S[f"m_moe_sum{it}"].up(now))

            v.sem_inc(S["x_made"].sem, 1)
            v.sem_inc(S["g_o0"].sem, 1)
            v.sem_inc(S["g_o1"].sem, 1)
            v.wait_ge(S["consts_loaded"].sem, 16 * 7)
            v.tensor_scalar(neg_cols[:], cols[:], -1.0, None, ALU.mult).then_inc(S["negated"].sem, 1)
            with v.Fori(0, ROUNDS) as r:
                now = Now(r)
                own = Own(S["dve_own"], now)
                linear_attention(own, now)
                if LAST > 1:
                    cross_attention(own, now, 1, 0)
                if LAST > 2:
                    experts(own, now)
                if LAST > 3:
                    self_attention(own, now)
                if LAST > 4:
                    cross_attention(own, now, 4, 1)
                if LAST > 5:
                    heads_and_experts(own, now)

        @block.gpsimd
        def _(pool):
            pool.wait_ge(S["consts_loaded"].sem, 16 * 7)

            def cross_attention(now, c):
                for b in range(IB):
                    for it in items:
                        pool.wait_ge(*S["x_rs"].at(now, (c * IB + b) * ITEMS + it + 1))
                        both = slice(HALF * b, HALF * (b + 1))
                        p = x_P[it][:, both].rearrange("p t (h k) -> p t h k", k=KV)
                        pool.tensor_tensor(p, p, over(x_rs[it][:, both], 3, KV), ALU.mult
                                           ).then_inc(*S["x_norm"].up(now))

            with pool.Fori(0, ROUNDS) as r:
                now = Now(r)
                if LAST > 1:
                    cross_attention(now, 0)
                if LAST > 4:
                    cross_attention(now, 1)
        return S.rises()


def kernel(**inputs):
    import numpy as np
    import concourse.bacc as bacc
    from concourse.bass_utils import run_bass_kernel_spmd

    def of(name):
        return np.asarray(inputs[name])

    def by_expert(w):
        return np.transpose(w, (2, 0, 1)).reshape(w.shape[2], -1)

    qkv, bqkv = of("L1_ffn_W_qkv"), of("L1_ffn_b_qkv")
    w = {
        "a_wq": of("L0_attn_Wq").T, "a_wk": of("L0_attn_Wk").T, "a_wv": of("L0_attn_Wv").T, "a_wo": of("L0_attn_Wo").T,
        "x0_wq": of("L0_xattn_Wq"), "x0_wo": of("L0_xattn_Wo"),
        "g_wg": of("L0_ffn_Wg").T, "g_wq": of("L0_ffn_Wq").T, "g_wo": of("L0_ffn_Wo").T,
        "g_wk": by_expert(of("L0_ffn_Wk")), "g_wv": by_expert(of("L0_ffn_Wv")), "g_wf": by_expert(of("L0_ffn_Wf")),
        "s_wq": of("L1_attn_Wq").T, "s_wk": of("L1_attn_Wk").T, "s_wv": of("L1_attn_Wv").T,
        "x1_wq": of("L1_xattn_W_Q"), "x1_wo": of("L1_xattn_W_O"),
        "m_wq": qkv[:, 0:D], "m_wk": qkv[:, D:2 * D], "m_wv": qkv[:, 2 * D:], "m_wg": of("L1_ffn_W_gate"),
        "m_we": np.transpose(of("L1_ffn_W_experts"), (1, 0, 2)).reshape(D, -1),
    }
    c = {
        "a_wgamma": of("L0_attn_W_gamma"), "a_bgamma": of("L0_attn_b_gamma"), "a_wlambda": of("L0_attn_W_lambda"),
        "a_blambda": of("L0_attn_b_lambda"), "g_norm": of("L0_ffn_norm_w"), "g_gnorm": of("L0_ffn_gnorm_w"),
        "s_bq": of("L1_attn_bq"), "s_bk": of("L1_attn_bk"), "lat_g": of("L1_xattn_ln_lat_g"),
        "lat_b": of("L1_xattn_ln_lat_b"), "m_bq": bqkv[0:D], "m_bk": bqkv[D:2 * D],
    }
    rows = {"bo": of("L0_xattn_bo"), "s_bv": of("L1_attn_bv"), "m_bv": bqkv[2 * D:], "m_bg": of("L1_ffn_b_gate")}
    p, n = np.arange(P)[:, None], np.arange(P)[None, :]
    earlier = (p <= n).astype(np.float32)
    own = np.zeros((P, HALF, T), np.float32)
    for h in range(HALF):
        own[np.arange(P), h, h * P + np.arange(P)] = -np.finfo(np.float32).max
    k = {
        "ident": np.eye(P, dtype=np.float32), "causal": earlier,
        "decay_mask": -np.concatenate([earlier, np.ones((P, P), np.float32), earlier], 1),
        "mid_sum": earlier - (p < P // 2), "suffix": (p >= n), "ones": np.ones((P, T), np.float32),
        "head_sum": (p // 64 == n // 64), "kv_heads": (p // XD == np.arange(XH)[None, :]),
        "v_heads": (np.arange(BANK)[None, :] % D // XD == 2 * (np.arange(BANK)[None, :] // D) + p // KV),
        "slot": np.broadcast_to(n, (P, P)),
        "tie": np.broadcast_to((np.arange(EXPERTS)[None, :] < np.arange(EXPERTS)[:, None]).reshape(1, -1),
                               (P, EXPERTS * EXPERTS)),
        "no_self": own.reshape(P, -1),
    }
    ctx = of("ctx_768")
    arrays = {
        "x": of("x"),
        "ctx_tok": ctx.reshape(B * KV, CC),
        "ctx_T": np.transpose(ctx.reshape(B // IB, IB * KV, CC), (0, 2, 1)),
        "w_pack": np.concatenate([w[name] for name, _ in _WIDTHS], 1),
        "w_ctx": np.concatenate([of("L0_xattn_Wk"), of("L0_xattn_Wv"), of("L1_xattn_W_K"), of("L1_xattn_W_V")], 1),
        "col_pack": np.stack([c[name].reshape(P) for name in _COLS], 1),
        "ctx_cols": np.stack([of("L1_xattn_ln_in_g"), of("L1_xattn_ln_in_b")], 1),
        "const_pack": np.concatenate([k[name].astype(np.float32) for name, _ in _CONSTS], 1),
        "rows": np.concatenate([rows[name] for name, _ in _ROWS])[None, :],
        "b_experts": of("L1_ffn_b_experts"),
        "ones_row": np.ones((1, SH * TOK), mybir.dt.np(BF16)),
    }
    nc = bacc.Bacc("TRN2", target_bir_lowering=False, num_devices=1)
    args = {}
    for name, a in arrays.items():
        arrays[name] = a = np.ascontiguousarray(a)
        args[name] = nc.dram_tensor(name, a.shape, mybir.dt.from_np(a.dtype), kind="ExternalInput").ap()
    args["out"] = nc.dram_tensor("out", (B, T, D), F32, kind="ExternalOutput").ap()
    rises = build(nc, **args)
    assert not RISES or {k: n for k, n in rises.items() if n[0]} == RISES
    return run_bass_kernel_spmd(nc, [arrays], core_ids=[0]).results[0]["out"]
```

```python
from contextlib import ExitStack

import concourse.bass as bass
from concourse import mybir

P = 128
B, T, D = 16, 256, 128
KV, CC = 64, 96
ITEMS, IB = 2, 2
ROUNDS = B // (ITEMS * IB)
TILES = IB * T // P
TOK = IB * T
HALF = T // P
EXPERTS, TOPK, CAP = 8, 2, 128
AHEAD = 2
GH, GK, GM = 4, 32, 64
XH, XD = 8, 16
SH, SD = 16, 8
GATE_NORM = 8.0
EPS = 1e-5
BANK = 512
LAYERS = 6
QUADS = SH // 4
MAX_STEPS = QUADS * TILES
HEAD_STEPS = SH * IB
MAX_AHEAD = 6
HEAD_PAIRS = HEAD_STEPS // 2
ROW_AT = MAX_STEPS - MAX_AHEAD + 4
TERMS = 9
STACK = TERMS * SD
LANES = 32

F32 = mybir.dt.float32
BF16 = mybir.dt.bfloat16
ALU = mybir.AluOpType
ACT = mybir.ActivationFunctionType
AX = mybir.AxisListType

_WIDTHS = [
    ("a_wq", D), ("a_wk", D), ("a_wv", D), ("a_wo", D),
    ("x0_wq", D), ("x0_wo", D),
    ("g_wg", EXPERTS), ("g_wq", D), ("g_wo", D),
    ("g_wk", EXPERTS * D), ("g_wv", EXPERTS * D), ("g_wf", EXPERTS * GH * GM),
    ("s_wq", D), ("s_wk", D), ("s_wv", D),
    ("x1_wq", D), ("x1_wo", D),
    ("m_wq", D), ("m_wk", D), ("m_wv", D), ("m_wg", EXPERTS), ("m_we", EXPERTS * D),
]
_COLS = ["a_wgamma", "a_bgamma", "a_wlambda", "a_blambda", "g_norm", "g_gnorm",
         "s_bq", "s_bk", "lat_g", "lat_b", "m_bq", "m_bk"]
_CONSTS = [("ident", P), ("causal", P), ("decay_mask", 3 * P), ("mid_sum", P), ("suffix", P), ("ones", T),
           ("head_sum", P), ("kv_heads", XH), ("v_heads", BANK), ("slot", P), ("tie", EXPERTS * EXPERTS),
           ("no_self", HALF * T)]
_ROWS = [("bo", D), ("s_bv", D), ("m_bv", D), ("m_bg", EXPERTS)]


def _places(widths):
    out, at = {}, 0
    for name, width in widths:
        out[name] = (at, at + width)
        at += width
    return out, at


W_AT, W_COLS = _places(_WIDTHS)
V_AT, V_COLS = _places([(n, 1) for n in _COLS])
C_AT, C_COLS = _places(_CONSTS)
R_AT, R_COLS = _places(_ROWS)


RISES = {
    "stored": (32, 0), "x_free": (2, 0), "x_kv": (4, 0), "m_split": (2, 0), "m_spilled0": (16, 0), "m_spilled1":
    (16, 0), "m_stacked0": (304, 0), "m_stacked1": (304, 0), "m_row": (2, 0), "m_max_spilled0": (16, 0),
    "m_max_stacked0": (16, 0), "m_max_spilled1": (16, 0), "m_max_stacked1": (16, 0), "x_made": (12, 0),
    "g_qk_made": (16, 2), "xT_made": (12, 0), "xT_kept": (12, 0), "a_qkv": (2, 0), "a_sq": (2, 0), "a_ss": (2,
    0), "a_UT": (2, 0), "a_U": (2, 0), "a_qv_kept": (2, 0), "a_A": (4, 0), "a_Am": (4, 0), "a_U_kept": (2, 0),
    "a_y": (2, 0), "a_yT": (2, 0), "y_made": (10, 0), "x_q": (4, 0), "x_q_kept": (4, 0), "x_K": (4, 0),
    "x_scores": (8, 0), "x_v": (4, 0), "x_norm": (8, 0), "x_PT": (8, 0), "x_V": (4, 0), "x_PT_kept": (8, 0),
    "x_o": (4, 0), "x_o_kept": (4, 0), "g_xn": (2, 0), "logits": (4, 0), "sel_made": (4, 0), "g_count": (2, 0),
    "g_place": (20, 2), "g_xe": (18, 2), "g_weighted": (20, 2), "g_scatter": (18, 2), "g_xe_kept": (18, 2),
    "g_f_made": (16, 2), "g_wk": (8, 1), "g_sp": (16, 2), "g_scatter_kept": (18, 2), "g_decay": (16, 2), "g_o0":
    (8, 1), "g_v_made": (16, 2), "g_o1": (8, 1), "g_v": (16, 2), "g_qk": (16, 2), "g_A": (16, 2), "g_Am": (16,
    2), "g_s": (16, 2), "g_ok": (16, 2), "g_combined": (18, 2), "g_sT": (16, 2), "g_qd": (16, 2), "g_qdT": (16,
    2), "g_qdT_kept": (16, 2), "g_sum": (18, 2), "g_T": (16, 2), "g_Tm": (16, 2), "g_ov": (16, 2), "g_out_sq":
    (2, 0), "g_out_ss": (2, 0), "g_onT": (2, 0), "s_qkv": (2, 0), "s_q": (2, 0), "s_kv": (2, 0), "s_scores": (2,
    0), "s_exp": (2, 0), "s_PT": (2, 0), "s_PT_kept": (2, 0), "l_made": (2, 0), "m_qk_made": (2, 0), "m_v_made":
    (2, 0), "w_made": (4, 0), "m_qkv_kept": (2, 0), "m_wT": (2, 0), "m_wT_kept": (2, 0), "m_bias": (2, 0),
    "m_max_scores0": (16, 0), "m_acc": (2, 0), "m_max_read0": (16, 0), "m_mxT": (2, 0), "m_moe1": (4, 0),
    "m_moe_sum1": (32, 0), "m_max_scores1": (16, 0), "m_max_read1": (16, 0), "m_scores0": (32, 0), "m_exp0":
    (32, 0), "m_pv0": (16, 0), "m_quad_kept0": (4, 0), "m_heads": (2, 0), "m_scores1": (32, 0), "m_exp1": (32,
    0), "m_pv1": (16, 0), "m_attention": (2, 0), "m_moe0": (4, 0), "m_moe_sum0": (32, 0), "m_quad_kept1": (4,
    0), "act_own": (28, 0), "a_ss_kept": (2, 0), "a_rn": (2, 0), "a_kn": (2, 0), "a_e": (2, 0), "a_den": (2, 0),
    "a_L": (2, 0), "a_rho": (2, 0), "a_D": (2, 0), "a_E": (2, 0), "a_Ep": (2, 0), "var_made": (12, 0),
    "rstd_made": (12, 0), "x_less_max": (8, 0), "x_exp": (8, 0), "g_rms": (2, 0), "less_max": (4, 0),
    "gate_exp": (4, 0), "g_exp_f": (16, 2), "g_cut_f": (16, 2), "g_ln_f": (16, 2), "g_exp_qk": (16, 2),
    "g_cut_qk": (16, 2), "g_ln_qk": (16, 2), "g_sp_qk": (16, 2), "g_sig": (16, 2), "g_eg": (16, 2),
    "g_less_max": (16, 2), "g_p": (16, 2), "g_out_rms": (2, 0), "s_max": (2, 0), "l_var": (2, 0), "l_rstd": (2,
    0), "m_qk": (2, 0), "dve_own": (152, 0), "x_rs": (8, 0), "g_slot": (2, 0), "dve_own_experts": (64, 8),
}

PRIMED = ("x_made", "stored", "g_o0", "g_o1", "g_qk_made")


class Signal:

    def __init__(self, sem, primed, per_round, per_step):
        self.primed = primed
        self.sem, self.per_round, self.per_step = sem, per_round, per_step
        self.raised_round, self.raised_step, self.frozen = 0, 0, False

    def at(self, now, n):
        value = now.round * self.per_round + (n + self.primed)
        if now.step is not None and self.per_step:
            value = value + now.step * self.per_step
        return self.sem, value

    def up(self, now, n=1):
        if self.frozen:
            return self.sem, n
        if now.step is None:
            self.raised_round += n
        else:
            self.raised_step += n
            self.raised_round += n * now.steps
        return self.sem, n


class Signals:

    def __init__(self, nc, ctx):
        self.nc, self.ctx, self.all = nc, ctx, {}

    def __getitem__(self, name):
        if name not in self.all:
            sem = self.ctx.enter_context(self.nc.semaphore(name))
            fixed = {"x_loaded0": (16, 0), "x_loaded1": (16, 0), "ctx_loaded": (ITEMS * 32, 0)}
            self.all[name] = Signal(sem, int(name in PRIMED), *fixed.get(name, RISES.get(name, (0, 0))))
        return self.all[name]

    def rises(self):
        return {k: (s.raised_round, s.raised_step) for k, s in self.all.items()}


class Now:

    def __init__(self, round_):
        self.round, self.step, self.steps = round_, None, 1

    def inner(self, step, steps):
        now = Now(self.round)
        now.step, now.steps = step, steps
        return now


class Own:

    def __init__(self, counter, now):
        self.counter, self.now, self.n = counter, now, 0

    def next(self):
        self.n += 1
        return self.counter.up(self.now)

    def all(self):
        return self.counter.at(self.now, self.n)


def build(nc, x, ctx_tok, ctx_T, w_pack, w_ctx, col_pack, ctx_cols, const_pack, rows, b_experts, ones_row, out):
    ctx = ExitStack()
    with ctx:
        S = Signals(nc, ctx)

        def sb(name, shape, dt=F32):
            return ctx.enter_context(nc.sbuf_tensor(name, shape, dt))

        weights = sb("weights", [P, W_COLS])
        wctx = sb("wctx", [CC, 4 * D])
        cols = sb("cols", [P, V_COLS])
        neg_cols = sb("neg_cols", [P, V_COLS])
        ccols = sb("ccols", [CC, 2])
        consts = sb("consts", [P, C_COLS])
        row_sb = sb("row_sb", [1, R_COLS])
        bexp = sb("bexp", [EXPERTS, D])
        x_in = sb("x_in", [P, ITEMS, TILES, D])
        ctx_k = sb("ctx_k", [P, ITEMS, CC])
        ctx_t = sb("ctx_t", [CC, ITEMS, P])
        xs = sb("xs", [P, ITEMS, TILES, D])
        zs = sb("zs", [P, ITEMS, TILES, D])
        stats = sb("stats", [P, ITEMS, TILES + 1, 6])
        mv = sb("mv", [P, ITEMS, TILES + 1, 2])
        rstd = sb("rstd", [P, ITEMS, TILES + 1])
        tick = sb("tick", [1, 1])
        wk_now = sb("wk_now", [P, D])
        PS = ctx.enter_context(nc.psum_tensor("PS", [P, 8, BANK], F32))
        ARENA = 17456
        arena = sb("arena", [P, ITEMS, ARENA])
        spill_qk = nc.dram_tensor("spill_qk", [ITEMS, P, 2, 3, TOK], BF16).ap()
        spill_max = nc.dram_tensor("spill_max", [ITEMS, SH, TOK], BF16).ap()

        class Arena:
            def __init__(self):
                self.at = 0

            def __call__(self, *shape, parts=P, dt=F32):
                n = 1
                for s in shape:
                    n *= s
                words = n if dt == F32 else n // 2
                a = self.at
                self.at += words + words % 2
                assert self.at <= ARENA, self.at
                views = []
                for it in range(ITEMS):
                    v = arena[0:parts, it, a:a + words]
                    if dt != F32:
                        v = v.bitcast(dt)
                    if len(shape) == 2:
                        v = v.rearrange("p (a b) -> p a b", b=shape[1])
                    elif len(shape) == 3:
                        v = v.rearrange("p (a b c) -> p a b c", b=shape[1], c=shape[2])
                    elif len(shape) == 4:
                        v = v.rearrange("p (a b c d) -> p a b c d", b=shape[1], c=shape[2], d=shape[3])
                    views.append(v)
                return views

        def W(name):
            a, b = W_AT[name]
            return weights[:, a:b]

        def col(name, n=P):
            return cols[0:n, V_AT[name][0]:V_AT[name][1]]

        def neg(name):
            return neg_cols[:, V_AT[name][0]:V_AT[name][1]]

        def K(name):
            a, b = C_AT[name]
            return consts[:, a:b]

        def row(name):
            a, b = R_AT[name]
            return row_sb[:, a:b]

        ident = K("ident")
        one_row = K("ones")[0:1, 0:P]

        def bank(it, n, m=None):
            return PS[:, 4 * it + n, :] if m is None else PS[:, 4 * it + n:4 * it + m, :]

        def over(ap, dim, n):
            v = ap.unsqueeze(dim)
            shape = list(v.shape)
            shape[dim] = n
            return v.broadcast_to(shape)

        def head_of(n):
            return n // (4 * IB), n // 4 % IB, n // (4 * IB) * 4 + n % 4

        items = range(ITEMS)
        tiles = range(TILES)

        al = Arena()
        a_xT, a_qT, a_vT, a_sq, a_rn, a_kn, a_e1, a_e2, a_den, a_G, a_um = (al(TOK) for _ in range(11))
        a_D = al(6, P)
        a_E = al(6, P)
        a_Ep = al(4, P)
        a_UT = al(6, P)
        a_U = al(6, P)
        a_Am = al(IB, 2, 3 * P)
        a_yT = al(TOK)
        al = Arena()
        x_xn = al(TILES, D)
        x_cn = al(CC)
        x_xT = al(TOK)
        x_cT = al(P, parts=CC)
        x_qT = al(TOK)
        x_K = al(IB, BANK)
        x_v = al(IB, D)
        x_V = al(IB, 4, P)
        x_P = al(TILES, BANK)
        x_mx = al(TILES, XH)
        x_sm = al(TILES, XH)
        x_rs = al(TILES, XH)
        x_PT = al(IB, 4, T)
        x_yT = al(TOK)
        al = Arena()
        g_xn = al(TILES, D)
        g_ss = al(TILES)
        g_r = al(TILES)
        r_mx = al(TILES)
        r_lg = al(TILES, EXPERTS)
        r_E = al(TILES, EXPERTS)
        r_gt = al(TILES, EXPERTS, EXPERTS)
        r_eq = al(TILES, EXPERTS, EXPERTS)
        r_rank = al(TILES, EXPERTS)
        r_sel = al(TILES, EXPERTS)
        r_den = al(TILES)
        r_w = al(TILES, EXPERTS)
        r_end = al.at
        g_slot = al(TILES, EXPERTS + AHEAD)
        g_w = al(TILES, EXPERTS + AHEAD)
        g_P = al(TILES, CAP)
        g_Pw = al(TILES, CAP)
        g_PwT = al(EXPERTS + 2, TOK)
        g_o = al(IB, P)
        g_acc = al(TOK)
        g_xe = al(IB, CAP)
        g_v = al(IB, P)
        g_qk = al(2, IB, CAP)
        g_ln = al(2, BANK)
        g_sp = al(2, BANK)
        g_sig = [a[:, 0] for a in g_ln]
        g_s = al(BANK)
        g_dec = al(BANK)
        g_inv = al(BANK)
        g_A = al(GH, IB, CAP)
        g_ok = g_sig
        g_mx = al(IB * GH)
        g_rs = al(IB * GH)
        g_sT = al(IB, 2, CAP)
        g_qd = g_inv
        g_qT = al(IB, 2, CAP)
        g_xT = [a[:, 0] for a in g_sp]
        g_onT = [a[:, 0] for a in g_sp]
        g_sq = [a[:, 1] for a in g_sp]
        al = Arena()
        s_xT, s_qT, s_kT = al(TOK), al(TOK), al(TOK)
        s_v = al(TILES, D)
        s_S = al(TILES, T)
        s_mx = al(TILES)
        s_sum = al(TILES)
        s_rs = al(TILES)
        s_PT = al(IB, 2, T)
        al = Arena()
        al.at = r_end
        m_xT = al(TOK)
        m_qk = al(2, TOK)
        qk_at = al.at
        m_r = al(2, TOK)
        m_parts = al(2, 3, TOK, dt=BF16)
        al(2 * TOK)
        m_Q = al(SH, TOK, parts=STACK + 1, dt=BF16)
        m_K = al(SH, TOK, parts=STACK + 1, dt=BF16)
        m_V = al(TILES, SH, LANES)
        m_acc = al(TILES, D)
        m_acc2 = [a[:, 0].rearrange("p (t d) -> p t d", d=D) for a in m_qk]
        m_mx = al(TILES, SH)
        m_cT = [a.rearrange("p t d -> p (t d)")[0:EXPERTS] for a in m_acc]
        m_rec = al(TILES, SH)
        m_row = al(TOK, parts=SH, dt=BF16)
        al.at = qk_at - TOK
        m_P = al(4, 2, T)
        m_oT = al(QUADS, TOK)

        block = ctx.enter_context(nc.Block())

        @block.sync
        def _(sp):
            sp.sem_inc(S["stored"].sem, 1)
            for dst, src in ((weights[:], w_pack), (wctx[:], w_ctx), (cols[:], col_pack), (ccols[:], ctx_cols),
                             (consts[:], const_pack), (row_sb[:], rows), (bexp[:], b_experts)):
                sp.dma_start(dst, src).then_inc(S["consts_loaded"].sem, 16)

            def load_x(now, r):
                for it in items:
                    sp.dma_start(x_in[:, it].rearrange("p (b h) d -> p b h d", b=IB),
                                 x[bass.ds(r * (ITEMS * IB) + it * IB, IB)].rearrange("b (h p) d -> p b h d", p=P)
                                 ).then_inc(S[f"x_loaded{it}"].sem, 16)

            def load_context(now, r):
                for it in items:
                    sp.dma_start(ctx_k[:, it], ctx_tok[bass.ds(r * (ITEMS * P) + it * P, P)]
                                 ).then_inc(S["ctx_loaded"].sem, 16)
                    sp.dma_start(ctx_t[:, it], ctx_T[bass.ds(r * ITEMS + it, 1)].rearrange("a c n -> (a c) n")
                                 ).then_inc(S["ctx_loaded"].sem, 16)

            def one_round(now, ahead):
                if ahead:
                    sp.wait_ge(*S["x_free"].at(now, ITEMS))
                    load_x(now, now.round + 1)
                    sp.wait_ge(*S["x_kv"].at(now, 2 * ITEMS))
                    load_context(now, now.round + 1)
                for it in items:
                    sp.wait_ge(*S["m_split"].at(now, it + 1))
                    sp.dma_start(spill_qk[it], m_parts[it]).then_inc(*S[f"m_spilled{it}"].up(now, 16))
                for it in items:
                    sp.wait_ge(*S[f"m_spilled{it}"].at(now, 16))
                    for t in range(TERMS):
                        for side, part, stack in ((0, t // 3, m_Q), (1, t % 3, m_K)):
                            src = spill_qk[it, :, side, part, :].rearrange("(h d) n -> d h n", d=SD)
                            sp.dma_start(stack[it][SD * t:SD * t + SD], src
                                         ).then_inc(*S[f"m_stacked{it}"].up(now, 16))
                    sp.dma_start(m_K[it][STACK:STACK + 1], ones_row.rearrange("a (h n) -> a h n", h=SH)
                                 ).then_inc(*S[f"m_stacked{it}"].up(now, 16))
                for it in items:
                    sp.wait_ge(*S["m_row"].at(now, it + 1))
                    sp.dma_start(spill_max[it], m_row[it]).then_inc(*S[f"m_max_spilled{it}"].up(now, 16))
                    sp.wait_ge(*S[f"m_max_spilled{it}"].at(now, 16))
                    sp.dma_start(m_Q[it][STACK:STACK + 1], spill_max[it].rearrange("(a h) n -> a h n", a=1)
                                 ).then_inc(*S[f"m_max_stacked{it}"].up(now, 16))
                for it in items:
                    sp.wait_ge(*S["x_made"].at(now, (LAYERS - 1) * ITEMS + it + 1))
                    sp.dma_start(out[bass.ds(now.round * (ITEMS * IB) + it * IB, IB)].rearrange("b (h p) d -> p b h d", p=P),
                                 xs[:, it].rearrange("p (b h) d -> p b h d", b=IB)
                                 ).then_inc(*S["stored"].up(now, 16))

            load_x(None, 0)
            load_context(None, 0)
            if ROUNDS > 1:
                with sp.Fori(0, ROUNDS - 1) as r:
                    one_round(Now(r), True)
                for s_ in S.all.values():
                    s_.frozen = True
            one_round(Now(ROUNDS - 1), False)
            sp.wait_ge(S["stored"].sem, 1 + ROUNDS * ITEMS * 16)
            for s_ in S.all.values():
                s_.frozen = False

        @block.tensor
        def _(pe):
            def transpose4(it, src, dst_bank):
                for t in tiles:
                    mm = pe.transpose(bank(it, dst_bank)[:, t * P:(t + 1) * P], src[:, t, :], ident)
                return mm

            def tokens_out(it, dst_bank, lhs, w, bias=None):
                for t in tiles:
                    o = bank(it, dst_bank)[:, t * P:(t + 1) * P]
                    mm = pe.matmul(o, lhsT=lhs[:, t * P:(t + 1) * P], rhs=w, start=True, stop=bias is None)
                    if bias is not None:
                        mm = pe.matmul(o, lhsT=one_row, rhs=bias, start=False, stop=True)
                return mm

            def linear_attention(now):
                for it in items:
                    pe.wait_ge(*S[f"x_loaded{it}"].at(now, 16))
                    pe.wait_ge(*S["x_made"].at(now, 0))
                    transpose4(it, x_in[:, it], 0).then_inc(*S["xT_made"].up(now))
                for it in items:
                    pe.wait_ge(*S["xT_kept"].at(now, it + 1))
                    for n, w in ((1, "a_wq"), (2, "a_wv"), (3, "a_wk")):
                        mm = pe.matmul(bank(it, n), lhsT=W(w), rhs=a_xT[it], start=True, stop=True)
                    mm.then_inc(*S["a_qkv"].up(now))
                for it in items:
                    pe.wait_ge(*S["a_sq"].at(now, it + 1))
                    pe.matmul(bank(it, 0), lhsT=K("head_sum"), rhs=a_sq[it], start=True, stop=True
                              ).then_inc(*S["a_ss"].up(now))
                for it in items:
                    pe.wait_ge(*S["a_UT"].at(now, it + 1))
                    for n in range(6):
                        mm = pe.transpose(bank(it, n // 4)[:, n % 4 * P:(n % 4 + 1) * P], a_UT[it][:, n], ident)
                    mm.then_inc(*S["a_U"].up(now))
                for b in range(IB):
                    for it in items:
                        if b:
                            pe.wait_ge(*S["a_Am"].at(now, it + 1))
                        else:
                            pe.wait_ge(*S["a_qv_kept"].at(now, it + 1))
                        for part, (s0, t0, n) in enumerate(((0, 0, 2), (1, 1, 1))):
                            for h in range(2):
                                lanes = slice(64 * h, 64 * h + 64)
                                s = (b * HALF + s0) * P
                                t = (b * HALF + t0) * P
                                mm = pe.matmul(bank(it, 2 + h)[:, 256 * part:256 * part + n * P],
                                               lhsT=a_vT[it][lanes, s:s + P], rhs=a_qT[it][lanes, t:t + n * P],
                                               start=True, stop=True)
                        mm.then_inc(*S["a_A"].up(now))
                for it in items:
                    pe.wait_ge(*S["a_U_kept"].at(now, it + 1))
                    pe.wait_ge(*S["a_Am"].at(now, ITEMS + it + 1))
                    for b in range(IB):
                        for h in range(2):
                            lanes = slice(64 * h, 64 * h + 64)
                            A = a_Am[it][:, b, h]

                            def U(n):
                                return a_U[it][:, n, lanes]
                            first = bank(it, 0)[lanes, b * T:b * T + P]
                            second = bank(it, 0)[lanes, b * T + P:(b + 1) * T]
                            pe.matmul(first, lhsT=U(2 * b), rhs=A[:, 0:P], start=True, stop=True)
                            pe.matmul(second, lhsT=U(4 + b), rhs=A[:, P:2 * P], start=True, stop=False)
                            mm = pe.matmul(second, lhsT=U(2 * b + 1), rhs=A[:, 2 * P:], start=False, stop=True)
                    mm.then_inc(*S["a_y"].up(now))
                for it in items:
                    pe.wait_ge(*S["a_yT"].at(now, it + 1))
                    tokens_out(it, 1, a_yT[it], W("a_wo")).then_inc(*S["y_made"].up(now))

            def cross_attention(now, s, c):
                for it in items:
                    if c:
                        pe.wait_ge(*S["l_made"].at(now, it + 1))
                        transpose4(it, x_xn[it], 0)
                        pe.transpose(bank(it, 1)[0:CC, 0:P], x_cn[it], ident).then_inc(*S["xT_made"].up(now))
                    else:
                        pe.wait_ge(*S["x_made"].at(now, (s - 1) * ITEMS + it + 1))
                        transpose4(it, xs[:, it], 0).then_inc(*S["xT_made"].up(now))
                wk, wv = (wctx[:, (2 * c + n) * D:(2 * c + n + 1) * D] for n in range(2))
                pe.wait_ge(*S["ctx_loaded"].at(now, ITEMS * 32))
                for it in items:
                    cT = x_cT[it] if c else ctx_t[:, it]
                    pe.wait_ge(*S["xT_kept"].at(now, s * ITEMS + it + 1))
                    pe.matmul(bank(it, 1)[:, 0:P], lhsT=wk, rhs=cT, start=True, stop=True)
                    for b in range(IB):
                        for half in range(2):
                            mm = pe.matmul(bank(it, 3)[64 * half:64 * half + 64, b * D:(b + 1) * D],
                                           lhsT=cT[:, b * KV:(b + 1) * KV], rhs=wv, start=True, stop=True)
                    mm.then_inc(*S["x_kv"].up(now))
                    pe.matmul(bank(it, 2), lhsT=W(f"x{c}_wq"), rhs=x_xT[it], start=True, stop=True
                              ).then_inc(*S["x_q"].up(now))
                for b in range(IB):
                    for it in items:
                        pe.wait_ge(*S["x_q_kept"].at(now, c * ITEMS + it + 1))
                        pe.wait_ge(*S["x_K"].at(now, c * ITEMS + it + 1))
                        if b:
                            pe.wait_ge(*S["x_v"].at(now, c * ITEMS + it + 1))
                        for t in range(HALF * b, HALF * b + HALF):
                            mm = pe.matmul(bank(it, t), lhsT=x_qT[it][:, t * P:(t + 1) * P], rhs=x_K[it][:, b],
                                           start=True, stop=True)
                        mm.then_inc(*S["x_scores"].up(now))
                for b in range(IB):
                    for it in items:
                        pe.wait_ge(*S["x_norm"].at(now, (c * IB + b) * ITEMS + it + 1))
                        for h in range(4):
                            for t in range(HALF):
                                o = bank(it, 2 * b + h // 2)[:, h % 2 * T + t * P:h % 2 * T + (t + 1) * P]
                                mm = pe.transpose(o, x_P[it][:, HALF * b + t, h * P:(h + 1) * P], ident)
                        mm.then_inc(*S["x_PT"].up(now))
                for it in items:
                    pe.wait_ge(*S["x_V"].at(now, c * ITEMS + it + 1))
                    for b in range(IB):
                        pe.wait_ge(*S["x_PT_kept"].at(now, (c * IB + b) * ITEMS + it + 1))
                        for h in range(4):
                            mm = pe.matmul(bank(it, 0)[:, b * T:(b + 1) * T], lhsT=x_V[it][:, b, h],
                                           rhs=x_PT[it][:, b, h], start=(h == 0), stop=(h == 3))
                    mm.then_inc(*S["x_o"].up(now))
                for it in items:
                    pe.wait_ge(*S["x_o_kept"].at(now, c * ITEMS + it + 1))
                    tokens_out(it, 1, x_yT[it], W(f"x{c}_wo"), None if c else row("bo")).then_inc(*S["y_made"].up(now))

            def experts(now):
                for it in items:
                    pe.wait_ge(*S["g_xn"].at(now, it + 1))
                    transpose4(it, g_xn[it], 0).then_inc(*S["xT_made"].up(now))
                for it in items:
                    pe.wait_ge(*S["xT_kept"].at(now, 2 * ITEMS + it + 1))
                    for t in tiles:
                        mm = pe.matmul(bank(it, 1)[:, t * EXPERTS:(t + 1) * EXPERTS],
                                       lhsT=g_xT[it][:, t * P:(t + 1) * P], rhs=W("g_wg"), start=True, stop=True)
                    mm.then_inc(*S["logits"].up(now))
                for it in items:
                    pe.wait_ge(*S["sel_made"].at(now, it + 1))
                    for t in tiles:
                        o = bank(it, 2)[:, t * EXPERTS:(t + 1) * EXPERTS]
                        mm = pe.matmul(o, lhsT=K("suffix"), rhs=r_sel[it][:, t], start=True, stop=t % 2 == 1)
                        if t % 2 == 0:
                            mm = pe.matmul(o, lhsT=K("ones")[:, 0:P], rhs=r_sel[it][:, t + 1], start=False, stop=True)
                    mm.then_inc(*S["g_count"].up(now))
                gather(now, 0)
                scatter(now, 0)
                with pe.Fori(0, EXPERTS) as e:
                    expert_step(now.inner(e, EXPERTS), e)
                for it in items:
                    pe.wait_ge(*S[f"g_o{it}"].at(now, EXPERTS))
                    combine(now, it, EXPERTS)
                for it in items:
                    pe.wait_ge(*S["g_out_sq"].at(now, it + 1))
                    pe.matmul(bank(it, 0), lhsT=K("ones")[:, 0:P], rhs=g_sq[it], start=True, stop=True
                              ).then_inc(*S["g_out_ss"].up(now))
                for it in items:
                    pe.wait_ge(*S["g_onT"].at(now, it + 1))
                    tokens_out(it, 2, g_onT[it], W("g_wo")).then_inc(*S["y_made"].up(now))

            def gather(now, done):
                for it in items:
                    pe.wait_ge(*S["g_place"].at(now, done + it + 1))
                    for b in range(IB):
                        for t in range(HALF):
                            mm = pe.matmul(bank(it, 3)[:, b * CAP:(b + 1) * CAP], lhsT=g_xn[it][:, HALF * b + t],
                                           rhs=g_P[it][:, HALF * b + t], start=(t == 0), stop=(t == HALF - 1))
                    mm.then_inc(*S["g_xe"].up(now))

            def scatter(now, done):
                for it in items:
                    if now.step is not None:
                        pe.wait_ge(*S["g_sT"].at(now, it + 1))
                    pe.wait_ge(*S["g_weighted"].at(now, done + it + 1))
                    for t in tiles:
                        mm = pe.transpose(bank(it, 1)[:, t * P:(t + 1) * P], g_Pw[it][:, t], ident)
                    mm.then_inc(*S["g_scatter"].up(now))

            def combine(now, it, e):
                for b in range(IB):
                    mm = pe.matmul(bank(it, 3)[:, b * T:(b + 1) * T], lhsT=g_o[it][:, b],
                                   rhs=g_PwT[it][:, bass.ds(e, 1), b * T:(b + 1) * T].rearrange("p a n -> p (a n)"),
                                   start=True, stop=True)
                mm.then_inc(*S["g_combined"].up(now))

            def expert_step(now, e):
                for it in items:
                    pe.wait_ge(*S["g_xe_kept"].at(now, it + 1))
                    for b in range(IB):
                        mm = pe.matmul(bank(it, 3)[:, b * GH * GM:(b + 1) * GH * GM], lhsT=g_xe[it][:, b],
                                       rhs=W("g_wf")[:, bass.ds(e * (GH * GM), GH * GM)], start=True, stop=True)
                    mm.then_inc(*S["g_f_made"].up(now))
                for it in items:
                    if it == 0:
                        pe.wait_ge(*S["g_wk"].at(now, 1))
                    xe = g_xe[it].rearrange("p b s -> p (b s)")
                    pe.matmul(bank(it, 2)[:, 0:IB * CAP], lhsT=W("g_wq"), rhs=xe, start=True, stop=True)
                    pe.matmul(bank(it, 2)[:, IB * CAP:], lhsT=wk_now[:], rhs=xe, start=True, stop=True
                              ).then_inc(*S["g_qk_made"].up(now))
                for it in items:
                    pe.wait_ge(*S["g_sp"].at(now, it + 1))
                    if it == 0:
                        pe.wait_ge(*S["g_scatter_kept"].at(now, ITEMS))
                    pe.matmul(bank(it, 1), lhsT=K("mid_sum"), rhs=g_sp[it][:, 1], start=True, stop=True
                              ).then_inc(*S["g_decay"].up(now))
                for it in items:
                    pe.wait_ge(*S[f"g_o{it}"].at(now, 0))
                    for b in range(IB):
                        mm = pe.matmul(bank(it, 0)[:, b * P:(b + 1) * P], lhsT=g_xe[it][:, b],
                                       rhs=W("g_wv")[:, bass.ds(e * D, D)], start=True, stop=True)
                    mm.then_inc(*S["g_v_made"].up(now))
                gather(now, ITEMS)
                for it in items:
                    pe.wait_ge(*S["g_v"].at(now, it + 1))
                    pe.wait_ge(*S["g_xe_kept"].at(now, ITEMS + it + 1))
                    pe.wait_ge(*S["g_qk"].at(now, it + 1))
                    for b in range(IB):
                        for h in range(GH):
                            lanes = slice(GK * h, GK * h + GK)
                            mm = pe.matmul(bank(it, h)[:, b * CAP:(b + 1) * CAP], lhsT=g_qk[it][lanes, 1, b],
                                           rhs=g_qk[it][lanes, 0, b], start=True, stop=True)
                    mm.then_inc(*S["g_A"].up(now))
                for it in items:
                    pe.wait_ge(*S["g_Am"].at(now, it + 1))
                    pe.wait_ge(*S["g_s"].at(now, it + 1))
                    for b in range(IB):
                        for h in range(GH):
                            at = (b * GH + h) * GM
                            end = min(at + 2 * GM, IB * GH * GM)
                            pe.matmul(bank(it, 0)[:, at:end], lhsT=g_A[it][:, h, b], rhs=g_s[it][:, at:end],
                                      start=True, stop=True)
                    for n in range(4):
                        mm = pe.transpose(bank(it, 1)[:, n * P:(n + 1) * P], g_s[it][:, n * P:(n + 1) * P], ident)
                    mm.then_inc(*S["g_ok"].up(now))
                for it in items:
                    combine(now, it, e)
                scatter(now, ITEMS)
                for it in items:
                    pe.wait_ge(*S["g_qd"].at(now, it + 1))
                    for n in range(4):
                        mm = pe.transpose(bank(it, 2)[:, n * P:(n + 1) * P], g_qd[it][:, n * P:(n + 1) * P], ident)
                    mm.then_inc(*S["g_qdT"].up(now))
                for it in items:
                    pe.wait_ge(*S["g_qdT_kept"].at(now, it + 1))
                    pe.wait_ge(*S["g_sum"].at(now, it + 1))
                    for b in range(IB):
                        for h in range(GH):
                            lanes = slice(64 * (h % 2), 64 * (h % 2) + 64)
                            mm = pe.matmul(bank(it, h)[:, b * CAP:(b + 1) * CAP], lhsT=g_sT[it][lanes, b, h // 2],
                                           rhs=g_qT[it][lanes, b, h // 2], start=True, stop=True)
                    mm.then_inc(*S["g_T"].up(now))
                for it in items:
                    pe.wait_ge(*S["g_Tm"].at(now, it + 1))
                    for b in range(IB):
                        for h in range(GH):
                            at = b * P + h * GK
                            mm = pe.matmul(bank(it, 0)[:, at:(b + 1) * P], lhsT=g_A[it][:, h, b],
                                           rhs=g_v[it][:, b, h * GK:], start=True, stop=True)
                    mm.then_inc(*S["g_ov"].up(now))

            def self_attention(now):
                for it in items:
                    pe.wait_ge(*S["x_made"].at(now, 2 * ITEMS + it + 1))
                    transpose4(it, xs[:, it], 0).then_inc(*S["xT_made"].up(now))
                for it in items:
                    pe.wait_ge(*S["xT_kept"].at(now, 3 * ITEMS + it + 1))
                    for n, w in ((1, "s_wq"), (2, "s_wk")):
                        pe.matmul(bank(it, n), lhsT=W(w), rhs=s_xT[it], start=True, stop=True)
                    tokens_out(it, 3, s_xT[it], W("s_wv"), row("s_bv")).then_inc(*S["s_qkv"].up(now))
                for it in items:
                    pe.wait_ge(*S["s_q"].at(now, it + 1))
                    pe.wait_ge(*S["s_kv"].at(now, it + 1))
                    for t in tiles:
                        b = t // HALF
                        mm = pe.matmul(bank(it, b)[:, t % HALF * T:(t % HALF + 1) * T],
                                       lhsT=s_qT[it][:, t * P:(t + 1) * P], rhs=s_kT[it][:, b * T:(b + 1) * T],
                                       start=True, stop=True)
                    mm.then_inc(*S["s_scores"].up(now))
                for it in items:
                    pe.wait_ge(*S["s_exp"].at(now, it + 1))
                    for t in tiles:
                        b = t // HALF
                        for k in range(HALF):
                            o = bank(it, 2 + b)[:, k * T + t % HALF * P:k * T + (t % HALF + 1) * P]
                            mm = pe.transpose(o, s_S[it][:, t, k * P:(k + 1) * P], ident)
                    mm.then_inc(*S["s_PT"].up(now))
                for it in items:
                    pe.wait_ge(*S["s_PT_kept"].at(now, it + 1))
                    for t in tiles:
                        b = t // HALF
                        for k in range(HALF):
                            mm = pe.matmul(bank(it, 0)[:, t * P:(t + 1) * P],
                                           lhsT=s_PT[it][:, b, k, t % HALF * P:(t % HALF + 1) * P],
                                           rhs=s_v[it][:, HALF * b + k], start=(k == 0), stop=(k == HALF - 1))
                    mm.then_inc(*S["y_made"].up(now))

            def heads_and_experts(now):
                for it in items:
                    pe.wait_ge(*S["x_made"].at(now, 4 * ITEMS + it + 1))
                    transpose4(it, xs[:, it], 0).then_inc(*S["xT_made"].up(now))
                for it in items:
                    pe.wait_ge(*S["xT_kept"].at(now, 5 * ITEMS + it + 1))
                    for n, w in ((1, "m_wq"), (2, "m_wk")):
                        mm = pe.matmul(bank(it, n), lhsT=W(w), rhs=m_xT[it], start=True, stop=True)
                    mm.then_inc(*S["m_qk_made"].up(now))
                for it in items:
                    tokens_out(it, 3, m_xT[it], W("m_wv"), row("m_bv")).then_inc(*S["m_v_made"].up(now))
                    for t in tiles:
                        o = bank(it, 0)[:, t * EXPERTS:(t + 1) * EXPERTS]
                        pe.matmul(o, lhsT=m_xT[it][:, t * P:(t + 1) * P], rhs=W("m_wg"), start=True, stop=False)
                        mm = pe.matmul(o, lhsT=one_row, rhs=row("m_bg"), start=False, stop=True)
                    mm.then_inc(*S["logits"].up(now))
                for it in items:
                    pe.wait_ge(*S["w_made"].at(now, ITEMS + it + 1))
                    pe.wait_ge(*S["m_qkv_kept"].at(now, it + 1))
                    for t in tiles:
                        mm = pe.transpose(bank(it, 3)[0:EXPERTS, t * P:(t + 1) * P], r_w[it][:, t], ident)
                    mm.then_inc(*S["m_wT"].up(now))
                for it in items:
                    pe.wait_ge(*S["m_wT_kept"].at(now, it + 1))
                    tokens_out(it, 2, m_cT[it], bexp[:]).then_inc(*S["m_bias"].up(now))
                for n in range(MAX_STEPS):
                    max_step(now, 0, n)
                rows_of_maxima(now, 0)
                for t in tiles:
                    moe_step(now, 1, t)
                for n in range(MAX_AHEAD):
                    max_step(now, 1, n)
                head_pairs(now, 0, 0, 1)
                for n in range(MAX_AHEAD, MAX_STEPS, 2):
                    max_step(now, 1, n)
                    max_step(now, 1, n + 1)
                    at = (n - MAX_AHEAD) // 2 + 1
                    head_pairs(now, 0, at, at + 1)
                rows_of_maxima(now, 1)
                head_pairs(now, 0, (MAX_STEPS - MAX_AHEAD) // 2 + 1, HEAD_PAIRS + 1)
                tokens_first(now, 0)
                for t in tiles:
                    head_pairs(now, 1, 2 * t, 2 * t + 2)
                    moe_step(now, 0, t)
                head_pairs(now, 1, 2 * TILES, HEAD_PAIRS + 1)
                tokens_first(now, 1)

            def moe_step(now, it, t):
                if t >= 2:
                    pe.wait_ge(*S[f"m_moe_sum{it}"].at(now, (t - 1) * EXPERTS))
                elif it == 0:
                    pe.wait_ge(*S["m_attention"].at(now, 1))
                elif t == 1:
                    pe.wait_ge(*S["m_acc"].at(now, it + 1))
                for n in range(2):
                    mm = pe.matmul(bank(it, 2 * (t % 2) + n), lhsT=m_xT[it][:, t * P:(t + 1) * P],
                                   rhs=W("m_we")[:, n * BANK:(n + 1) * BANK], start=True, stop=True)
                mm.then_inc(*S[f"m_moe{it}"].up(now))

            def max_step(now, it, n):
                q, t = n // TILES, n % TILES
                if n == 0:
                    pe.wait_ge(*S[f"m_stacked{it}"].at(now, 16 * (2 * TERMS + 1)))
                if n >= 2:
                    pe.wait_ge(*S[f"m_max_read{it}"].at(now, n - 1))
                elif it == 1:
                    pe.wait_ge(*S["m_moe_sum1"].at(now, (TILES - 1 + n) * EXPERTS))
                elif n == 1:
                    pe.wait_ge(*S["m_acc"].at(now, it + 1))
                b = t // HALF
                for h in range(4):
                    mm = pe.matmul(bank(it, 2 * (n % 2) + h // 2)[:, h % 2 * T:(h % 2 + 1) * T],
                                   lhsT=m_Q[it][0:STACK, 4 * q + h, t * P:(t + 1) * P],
                                   rhs=m_K[it][0:STACK, 4 * q + h, b * T:(b + 1) * T], start=True, stop=True)
                mm.then_inc(*S[f"m_max_scores{it}"].up(now))

            def rows_of_maxima(now, it):
                pe.wait_ge(*S[f"m_max_read{it}"].at(now, MAX_STEPS))
                for t in tiles:
                    mm = pe.transpose(bank(it, 0)[0:SH, t * P:(t + 1) * P], m_mx[it][:, t], ident)
                mm.then_inc(*S["m_mxT"].up(now))

            def head_pairs(now, it, first, end):
                for pair in range(first, end):
                    if pair == 0:
                        pe.wait_ge(*S[f"m_max_stacked{it}"].at(now, 16))
                    if pair < HEAD_PAIRS:
                        for n in (2 * pair, 2 * pair + 1):
                            q, b, h = head_of(n)
                            if n >= 2:
                                pe.wait_ge(*S[f"m_exp{it}"].at(now, n - 1))
                            for k in range(HALF):
                                at = b * T + k * P
                                mm = pe.matmul(bank(it, n % 2)[:, k * T:(k + 1) * T], lhsT=m_K[it][:, h, at:at + P],
                                               rhs=m_Q[it][:, h, b * T:(b + 1) * T], start=True, stop=True)
                            mm.then_inc(*S[f"m_scores{it}"].up(now))
                    if pair > 0:
                        g = 2 * (pair - 1)
                        q, b, h = head_of(g)
                        if q >= 2 and g % 8 == 0:
                            pe.wait_ge(*S[f"m_quad_kept{it}"].at(now, q - 1))
                        pe.wait_ge(*S[f"m_exp{it}"].at(now, g + 2))
                        for k in range(HALF):
                            for i in range(2):
                                lanes = slice(LANES * (h % 4 + i), LANES * (h % 4 + i + 1))
                                mm = pe.matmul(bank(it, 2 + q % 2)[lanes, b * T:(b + 1) * T],
                                               lhsT=m_V[it][:, HALF * b + k, h + i], rhs=m_P[it][:, (g + i) % 4, k],
                                               start=(k == 0), stop=(k == HALF - 1))
                        mm.then_inc(*S[f"m_pv{it}"].up(now))

            def tokens_first(now, it):
                pe.wait_ge(*S[f"m_quad_kept{it}"].at(now, QUADS))
                for t in tiles:
                    for q in range(QUADS):
                        mm = pe.transpose(bank(it, t)[:, q * P:(q + 1) * P], m_oT[it][:, q, t * P:(t + 1) * P], ident)
                mm.then_inc(*S["m_heads"].up(now))

            pe.sem_inc(S["g_qk_made"].sem, 1)
            pe.wait_ge(S["consts_loaded"].sem, 16 * 7)
            with pe.Fori(0, ROUNDS) as r:
                now = Now(r)
                linear_attention(now)
                cross_attention(now, 1, 0)
                experts(now)
                self_attention(now)
                cross_attention(now, 4, 1)
                heads_and_experts(now)

        @block.scalar
        def _(act):
            act.preload_act_table_set("natural_log_exp_and_others")
            act.wait_ge(S["consts_loaded"].sem, 16 * 7)

            def power(own, out_, in_, scale, bias):
                act.activation(out_, in_, ACT.Ln, scale=scale, bias=bias).then_inc(*own.next())
                act.wait_ge(*own.all())
                return act.activation(out_, out_, ACT.Exp, scale=-0.5)

            def layernorm(own, now, s):
                for it in items:
                    act.wait_ge(*S["var_made"].at(now, s * ITEMS + it + 1))
                    power(own, rstd[:, it, 0:TILES], mv[:, it, 0:TILES, 1], 1.0, EPS
                          ).then_inc(*S["rstd_made"].up(now))

            def keep_xT(now, s, dst, scale=1.0, bias=0.0):
                for it in items:
                    act.wait_ge(*S["xT_made"].at(now, s * ITEMS + it + 1))
                    act.activation(dst[it], bank(it, 0), ACT.Identity, scale=scale, bias=bias
                                   ).then_inc(*S["xT_kept"].up(now))

            def linear_attention(own, now):
                keep_xT(now, 0, a_xT)
                for it in items:
                    act.wait_ge(*S["a_qkv"].at(now, it + 1))
                    act.activation(a_sq[it], bank(it, 3), ACT.Square).then_inc(*S["a_sq"].up(now))
                    act.activation(a_qT[it], bank(it, 1), ACT.Copy)
                    act.activation(a_vT[it], bank(it, 2), ACT.Copy).then_inc(*S["a_qv_kept"].up(now))
                for it in items:
                    act.wait_ge(*S["a_ss_kept"].at(now, it + 1))
                    act.activation(a_rn[it], a_rn[it], ACT.Ln).then_inc(*own.next())
                    act.wait_ge(*own.all())
                    act.activation(a_rn[it], a_rn[it], ACT.Exp, scale=-0.5).then_inc(*S["a_rn"].up(now))
                for it in items:
                    act.wait_ge(*S["a_kn"].at(now, it + 1))
                    act.activation(a_e1[it], a_kn[it], ACT.Exp, scale=neg("a_wgamma"), bias=neg("a_bgamma"))
                    act.activation(a_e2[it], a_kn[it], ACT.Exp, scale=col("a_wlambda"), bias=col("a_blambda")
                                   ).then_inc(*S["a_e"].up(now))
                for it in items:
                    act.wait_ge(*S["a_den"].at(now, it + 1))
                    act.activation(a_e1[it], a_den[it], ACT.Ln).then_inc(*S["a_L"].up(now))
                for it in items:
                    act.wait_ge(*S["a_L"].at(now, it + 1))
                    act.activation(a_e2[it], a_e1[it], ACT.Exp, scale=-1.0).then_inc(*S["a_rho"].up(now))
                for it in items:
                    act.wait_ge(*S["a_D"].at(now, it + 1))
                    act.activation(a_E[it], a_D[it], ACT.Exp).then_inc(*S["a_E"].up(now))
                    act.activation(a_Ep[it], a_D[it][:, 0:4], ACT.Exp, scale=-1.0).then_inc(*S["a_Ep"].up(now))
                for it in items:
                    act.wait_ge(*S["a_U"].at(now, it + 1))
                    act.activation(a_U[it][:, 0:4], bank(it, 0).rearrange("p (a b) -> p a b", b=P), ACT.Copy)
                    act.activation(a_U[it][:, 4:6], bank(it, 1)[:, 0:2 * P].rearrange("p (a b) -> p a b", b=P), ACT.Copy
                                   ).then_inc(*S["a_U_kept"].up(now))
                layernorm(own, now, 0)

            def cross_attention(own, now, s, c):
                if c:
                    for it in items:
                        act.wait_ge(*S["l_var"].at(now, it + 1))
                        power(own, rstd[:, it], mv[:, it, :, 1], 1.0, EPS).then_inc(*S["l_rstd"].up(now))
                    for it in items:
                        act.wait_ge(*S["xT_made"].at(now, s * ITEMS + it + 1))
                        act.activation(x_cT[it], bank(it, 1)[0:CC, 0:P], ACT.Identity, scale=ccols[:, 0:1],
                                       bias=ccols[:, 1:2])
                        act.activation(x_xT[it], bank(it, 0), ACT.Identity, scale=col("lat_g"), bias=col("lat_b")
                                       ).then_inc(*S["xT_kept"].up(now))
                else:
                    keep_xT(now, s, x_xT)
                for it in items:
                    act.wait_ge(*S["x_q"].at(now, c * ITEMS + it + 1))
                    act.activation(x_qT[it], bank(it, 2), ACT.Copy).then_inc(*S["x_q_kept"].up(now))
                    act.activation(x_v[it].rearrange("p b d -> p (b d)"), bank(it, 3)[:, 0:IB * D], ACT.Copy
                                   ).then_inc(*S["x_v"].up(now))
                for b in range(IB):
                    for it in items:
                        act.wait_ge(*S["x_less_max"].at(now, (c * IB + b) * ITEMS + it + 1))
                        p = x_P[it][:, HALF * b:HALF * (b + 1)]
                        act.activation(p, p, ACT.Exp, scale=float(XD) ** -0.5).then_inc(*S["x_exp"].up(now))
                for b in range(IB):
                    for it in items:
                        act.wait_ge(*S["x_PT"].at(now, (c * IB + b) * ITEMS + it + 1))
                        act.activation(x_PT[it][:, b].rearrange("p (a h) t -> p a (h t)", a=2),
                                       bank(it, 2 * b, 2 * b + 2), ACT.Copy).then_inc(*S["x_PT_kept"].up(now))
                for it in items:
                    act.wait_ge(*S["x_o"].at(now, c * ITEMS + it + 1))
                    act.activation(x_yT[it], bank(it, 0), ACT.Copy).then_inc(*S["x_o_kept"].up(now))
                layernorm(own, now, s)

            def rms(own, now, it, src, done):
                for t in tiles:
                    act.activation(g_s[it][:, t * P:(t + 1) * P], src[:, t * P:(t + 1) * P], ACT.Square,
                                           accum_out=g_ss[it][:, t:t + 1]).then_inc(*own.next())
                act.wait_ge(*own.all())
                power(own, g_r[it], g_ss[it], 1.0 / D, EPS).then_inc(*S[done].up(now))

            def experts(own, now):
                for it in items:
                    act.wait_ge(*S["x_made"].at(now, ITEMS + it + 1))
                    rms(own, now, it, xs[:, it].rearrange("p t d -> p (t d)"), "g_rms")
                keep_xT(now, 2, g_xT, scale=col("g_norm"))
                for it in items:
                    act.wait_ge(*S["less_max"].at(now, it + 1))
                    act.activation(r_E[it], r_lg[it], ACT.Exp).then_inc(*S["gate_exp"].up(now))
                keep_scatter(now, 0, 1)
                with act.Fori(0, EXPERTS) as e:
                    expert_step(now.inner(e, EXPERTS), e)
                for it in items:
                    act.wait_ge(*S["g_sum"].at(now, ITEMS * EXPERTS + it + 1))
                    act.activation(g_sq[it], g_acc[it], ACT.Square).then_inc(*S["g_out_sq"].up(now))
                for it in items:
                    act.wait_ge(*S["g_out_ss"].at(now, it + 1))
                    power(own, g_sq[it], bank(it, 0), 1.0 / D, EPS).then_inc(*S["g_out_rms"].up(now))
                layernorm(own, now, 2)

            def keep_scatter(now, done, e):
                for it in items:
                    act.wait_ge(*S["g_scatter"].at(now, done + it + 1))
                    act.activation(g_PwT[it][:, bass.ds(e, 1)].rearrange("p a n -> p (a n)"), bank(it, 1), ACT.Copy
                                   ).then_inc(*S["g_scatter_kept"].up(now))

            def expert_step(now, e):
                act.wait_ge(*S["g_qk_made"].at(now, 0))
                act.activation(wk_now[:], W("g_wk")[:, bass.ds(e * D, D)], ACT.Copy).then_inc(*S["g_wk"].up(now))
                for it in items:
                    act.wait_ge(*S["g_f_made"].at(now, it + 1))
                    act.activation(g_ln[it][:, 1], bank(it, 3), ACT.Exp, scale=-1.0).then_inc(*S["g_exp_f"].up(now))
                def ln_f(it):
                    act.wait_ge(*S["g_cut_f"].at(now, it + 1))
                    act.activation(g_ln[it][:, 1], g_ln[it][:, 1], ACT.Ln, bias=1.0).then_inc(*S["g_ln_f"].up(now))

                def exp_qk(it):
                    act.wait_ge(*S["g_qk_made"].at(now, it + 1))
                    act.activation(g_ln[it][:, 0], bank(it, 2), ACT.Exp, scale=-1.0).then_inc(*S["g_exp_qk"].up(now))

                def ln_qk(it):
                    act.wait_ge(*S["g_cut_qk"].at(now, it + 1))
                    act.activation(g_ln[it][:, 0], g_ln[it][:, 0], ACT.Ln, bias=1.0).then_inc(*S["g_ln_qk"].up(now))

                def decays(it):
                    act.wait_ge(*S["g_decay"].at(now, it + 1))
                    act.activation(g_inv[it], bank(it, 1), ACT.Exp, scale=1.0 / GATE_NORM)
                    act.activation(g_dec[it], bank(it, 1), ACT.Exp, scale=-1.0 / GATE_NORM)

                def sigmoid_and_values(it):
                    act.wait_ge(*S["g_sp_qk"].at(now, it + 1))
                    act.activation(g_sig[it], g_sp[it][:, 0], ACT.Exp, scale=-1.0).then_inc(*S["g_sig"].up(now))
                    act.wait_ge(*S["g_v_made"].at(now, it + 1))
                    act.activation(g_v[it].rearrange("p b d -> p (b d)"), bank(it, 0)[:, 0:IB * P], ACT.Copy
                                   ).then_inc(*S["g_v"].up(now))

                ln_f(0)
                exp_qk(0)
                ln_f(1)
                ln_qk(0)
                exp_qk(1)
                decays(0)
                ln_qk(1)
                sigmoid_and_values(0)
                decays(1)
                sigmoid_and_values(1)
                for it in items:
                    act.activation(g_s[it], g_sp[it][:, 1], ACT.Exp, scale=-1.0 / GATE_NORM).then_inc(*S["g_eg"].up(now))
                for it in items:
                    act.wait_ge(*S["g_ok"].at(now, it + 1))
                    act.activation(g_sT[it].rearrange("p b a n -> p (b a n)"), bank(it, 1), ACT.Copy
                                   ).then_inc(*S["g_sT"].up(now))
                for it in items:
                    act.wait_ge(*S["g_less_max"].at(now, it + 1))
                    act.activation(g_ok[it], g_ok[it], ACT.Exp).then_inc(*S["g_p"].up(now))
                keep_scatter(now, ITEMS, e + 2)
                for it in items:
                    act.wait_ge(*S["g_qdT"].at(now, it + 1))
                    act.activation(g_qT[it].rearrange("p b a n -> p (b a n)"), bank(it, 2), ACT.Copy
                                   ).then_inc(*S["g_qdT_kept"].up(now))

            def self_attention(own, now):
                keep_xT(now, 3, s_xT)
                for it in items:
                    act.wait_ge(*S["s_qkv"].at(now, it + 1))
                    act.activation(s_kT[it], bank(it, 2), ACT.Identity, bias=col("s_bk"))
                    act.activation(s_v[it].rearrange("p t d -> p (t d)"), bank(it, 3), ACT.Copy
                                   ).then_inc(*S["s_kv"].up(now))
                for it in items:
                    act.wait_ge(*S["s_max"].at(now, it + 1))
                    for t in tiles:
                        e = act.activation(s_S[it][:, t], s_S[it][:, t], ACT.Exp, bias=s_mx[it][:, t:t + 1],
                                           accum_out=s_sum[it][:, t:t + 1])
                    e.then_inc(*S["s_exp"].up(now))
                for it in items:
                    act.wait_ge(*S["s_PT"].at(now, it + 1))
                    act.activation(s_PT[it].rearrange("p b k t -> p b (k t)"), bank(it, 2, 4), ACT.Copy
                                   ).then_inc(*S["s_PT_kept"].up(now))
                layernorm(own, now, 3)

            def heads_and_experts(own, now):
                keep_xT(now, 5, m_xT)
                for it in items:
                    act.wait_ge(*S["m_qk_made"].at(now, it + 1))
                    for side, b in ((0, "m_bq"), (1, "m_bk")):
                        act.activation(m_parts[it][:, side, 0], bank(it, 1 + side), ACT.Identity, bias=col(b))
                        i = act.activation(m_qk[it][:, side], bank(it, 1 + side), ACT.Identity, bias=col(b))
                    i.then_inc(*S["m_qk"].up(now))
                for it in items:
                    act.wait_ge(*S["m_v_made"].at(now, it + 1))
                    for t in tiles:
                        e = act.activation(m_V[it][:, t, :, 0:SD],
                                           bank(it, 3)[:, t * P:(t + 1) * P].rearrange("p (h d) -> p h d", d=SD),
                                           ACT.Copy)
                    e.then_inc(*S["m_qkv_kept"].up(now))
                for it in items:
                    act.wait_ge(*S["less_max"].at(now, ITEMS + it + 1))
                    act.activation(r_E[it], r_lg[it], ACT.Exp).then_inc(*S["gate_exp"].up(now))
                for it in items:
                    act.wait_ge(*S["m_wT"].at(now, it + 1))
                    act.activation(m_cT[it], bank(it, 3)[0:EXPERTS], ACT.Copy).then_inc(*S["m_wT_kept"].up(now))
                def keep_row(it):
                    act.wait_ge(*S["m_mxT"].at(now, it + 1))
                    act.activation(m_row[it], bank(it, 0)[0:SH], ACT.Copy, scale=-1.0).then_inc(*S["m_row"].up(now))

                def keep_quad(it, q):
                    act.wait_ge(*S[f"m_pv{it}"].at(now, (q + 1) * 2 * IB))
                    act.activation(m_oT[it][:, q], bank(it, 2 + q % 2), ACT.Copy).then_inc(*S[f"m_quad_kept{it}"].up(now))

                keep_row(0)
                for it in items:
                    for n in range(HEAD_STEPS):
                        act.wait_ge(*S[f"m_scores{it}"].at(now, n + 1))
                        if n >= 4:
                            act.wait_ge(*S[f"m_pv{it}"].at(now, (n - 4) // 2 + 1))
                        act.activation(m_P[it][:, n % 4].rearrange("p k t -> p (k t)"), bank(it, n % 2), ACT.Exp,
                                       scale=float(SD) ** -0.5).then_inc(*S[f"m_exp{it}"].up(now))
                        if it == 0 and n == ROW_AT:
                            keep_row(1)
                        if n % (4 * IB) == 1 and n > 1:
                            keep_quad(it, n // (4 * IB) - 1)
                    keep_quad(it, QUADS - 1)
                layernorm(own, now, 5)

            with act.Fori(0, ROUNDS) as r:
                now = Now(r)
                own = Own(S["act_own"], now)
                linear_attention(own, now)
                cross_attention(own, now, 1, 0)
                experts(own, now)
                self_attention(own, now)
                cross_attention(own, now, 4, 1)
                heads_and_experts(own, now)

        @block.vector
        def _(v):
            def variance(own, now, it):
                for t in tiles:
                    v.bn_stats(stats[:, it, t], zs[:, it, t]).then_inc(*own.next())
                v.wait_ge(*own.all())
                v.memset(tick[:], 0.0)
                for t in tiles:
                    i = v.bn_aggr(mv[:, it, t], stats[:, it, t])
                i.then_inc(*S["var_made"].up(now))

            def normalise(own, now, s):
                for it in items:
                    v.wait_ge(*S["rstd_made"].at(now, s * ITEMS + it + 1))
                    if s == 0:
                        v.wait_ge(*S["stored"].at(now, 0))
                    for t in tiles:
                        i = v.tensor_scalar(xs[:, it, t], zs[:, it, t], mv[:, it, t, 0:1], rstd[:, it, t:t + 1],
                                            ALU.subtract, ALU.mult)
                    i.then_inc(*S["x_made"].up(now))

            def layernorm(own, now, s, y_bank):
                for it in items:
                    v.wait_ge(*S["y_made"].at(now, s * ITEMS + it + 1))
                    x_old = x_in if s == 0 else xs
                    i = v.tensor_tensor(zs[:, it].rearrange("p t d -> p (t d)"), bank(it, y_bank),
                                        x_old[:, it].rearrange("p t d -> p (t d)"), ALU.add)
                    if s == 0:
                        i.then_inc(*S["x_free"].up(now))
                        v.wait_ge(*S["x_free"].at(now, it + 1))
                    else:
                        i.then_inc(*own.next())
                        v.wait_ge(*own.all())
                    variance(own, now, it)
                normalise(own, now, s)

            def linear_attention(own, now):
                for it in items:
                    v.wait_ge(*S["a_ss"].at(now, it + 1))
                    v.tensor_scalar(a_rn[it], bank(it, 0), 1e-24, 1e12, ALU.max, ALU.mult
                                    ).then_inc(*S["a_ss_kept"].up(now))
                for it in items:
                    v.wait_ge(*S["a_rn"].at(now, it + 1))
                    v.scalar_tensor_tensor(a_kn[it], in0=bank(it, 3), scalar=1e6, in1=a_rn[it], op0=ALU.mult,
                                           op1=ALU.mult).then_inc(*S["a_kn"].up(now))
                for it in items:
                    v.wait_ge(*S["a_e"].at(now, it + 1))
                    v.tensor_scalar(a_e1[it], a_e1[it], 1.0, None, ALU.add).then_inc(*own.next())
                    v.wait_ge(*own.all())
                    v.scalar_tensor_tensor(a_den[it], in0=a_e2[it], scalar=1.0, in1=a_e1[it], op0=ALU.add,
                                           op1=ALU.mult).then_inc(*S["a_den"].up(now))
                for it in items:
                    v.wait_ge(*S["a_L"].at(now, it + 1))
                    for b in range(IB):
                        v.tensor_tensor_scan(a_G[it][:, b * T:(b + 1) * T], K("ones"),
                                                     a_e1[it][:, b * T:(b + 1) * T], 0.0, ALU.mult, ALU.add).then_inc(*own.next())
                    v.wait_ge(*own.all())
                    G = a_G[it].rearrange("p (n t) -> p n t", t=P)
                    mid = G[:, :, P // 2 - 1:P // 2]
                    v.tensor_tensor(a_D[it][:, 0:4], G, mid.broadcast_to([P, 4, P]), ALU.subtract)
                    v.tensor_tensor(a_D[it][:, 4:6], G[:, 0:4:2], mid[:, 1:4:2].broadcast_to([P, 2, P]),
                                    ALU.subtract).then_inc(*S["a_D"].up(now))
                for it in items:
                    v.wait_ge(*S["a_rho"].at(now, it + 1))
                    v.scalar_tensor_tensor(a_um[it], in0=a_e2[it], scalar=1.0, in1=a_kn[it], op0=ALU.subtract,
                                           op1=ALU.mult).then_inc(*own.next())
                v.wait_ge(*own.all())
                for it in items:
                    v.wait_ge(*S["a_E"].at(now, it + 1))
                    um = a_um[it].rearrange("p (n t) -> p n t", t=P)
                    v.tensor_tensor(a_UT[it][:, 0:4], a_E[it][:, 0:4], um, ALU.mult)
                    v.tensor_tensor(a_UT[it][:, 4:6], a_E[it][:, 4:6], um[:, 0:4:2], ALU.mult
                                    ).then_inc(*S["a_UT"].up(now))
                for b in range(IB):
                    for it in items:
                        v.wait_ge(*S["a_A"].at(now, b * ITEMS + it + 1))
                        v.tensor_tensor(a_Am[it][:, b], bank(it, 2, 4)[:, :, 0:3 * P], over(K("decay_mask"), 1, 2),
                                        ALU.mult).then_inc(*S["a_Am"].up(now))
                for it in items:
                    v.wait_ge(*S["a_y"].at(now, it + 1))
                    v.wait_ge(*S["a_Ep"].at(now, it + 1))
                    v.tensor_tensor(a_yT[it], bank(it, 0), a_Ep[it].rearrange("p n t -> p (n t)"), ALU.mult
                                    ).then_inc(*S["a_yT"].up(now))
                layernorm(own, now, 0, 1)

            def cross_attention(own, now, s, c):
                if c:
                    for it in items:
                        v.wait_ge(*S["x_made"].at(now, (s - 1) * ITEMS + it + 1))
                        v.wait_ge(*S["ctx_loaded"].at(now, ITEMS * 32))
                        for t in tiles:
                            v.bn_stats(stats[:, it, t], xs[:, it, t]).then_inc(*own.next())
                        v.bn_stats(stats[:, it, TILES], ctx_k[:, it]).then_inc(*own.next())
                        v.wait_ge(*own.all())
                        v.memset(tick[:], 0.0)
                        for t in range(TILES + 1):
                            i = v.bn_aggr(mv[:, it, t], stats[:, it, t])
                        i.then_inc(*S["l_var"].up(now))
                    for it in items:
                        v.wait_ge(*S["l_rstd"].at(now, it + 1))
                        for t in tiles:
                            v.tensor_scalar(x_xn[it][:, t], xs[:, it, t], mv[:, it, t, 0:1], rstd[:, it, t:t + 1],
                                            ALU.subtract, ALU.mult)
                        v.tensor_scalar(x_cn[it], ctx_k[:, it], mv[:, it, TILES, 0:1], rstd[:, it, TILES:TILES + 1],
                                        ALU.subtract, ALU.mult).then_inc(*S["l_made"].up(now))
                for it in items:
                    v.wait_ge(*S["x_kv"].at(now, c * ITEMS + it + 1))
                    for b in range(IB):
                        i = v.tensor_tensor(x_K[it][:, b].rearrange("p (h k) -> p h k", k=KV),
                                            over(bank(it, 1)[:, b * KV:(b + 1) * KV], 1, XH),
                                            over(K("kv_heads"), 2, KV), ALU.mult)
                    i.then_inc(*S["x_K"].up(now))
                for b in range(IB):
                    for it in items:
                        v.wait_ge(*S["x_scores"].at(now, (c * IB + b) * ITEMS + it + 1))
                        both = slice(HALF * b, HALF * (b + 1))
                        sc = bank(it, HALF * b, HALF * (b + 1)).rearrange("p t (h k) -> p t h k", k=KV)
                        mx = x_mx[it][:, both]
                        v.tensor_reduce(mx, sc, AX.X, ALU.max).then_inc(*own.next())
                        v.wait_ge(*own.all())
                        v.tensor_tensor(x_P[it][:, both].rearrange("p t (h k) -> p t h k", k=KV), sc,
                                        over(mx, 3, KV), ALU.subtract).then_inc(*S["x_less_max"].up(now))
                for b in range(IB):
                    for it in items:
                        v.wait_ge(*S["x_exp"].at(now, (c * IB + b) * ITEMS + it + 1))
                        both = slice(HALF * b, HALF * (b + 1))
                        v.tensor_reduce(x_sm[it][:, both],
                                                x_P[it][:, both].rearrange("p t (h k) -> p t h k", k=KV),
                                                AX.X, ALU.add).then_inc(*own.next())
                        v.wait_ge(*own.all())
                        v.reciprocal(x_rs[it][:, both], x_sm[it][:, both]).then_inc(*S["x_rs"].up(now))
                layernorm(own, now, s, 1)

            def routing(own, now, use, lg_bank, over_all):
                for it in items:
                    v.wait_ge(*S["logits"].at(now, use * ITEMS + it + 1))
                    lg = bank(it, lg_bank)[:, 0:TILES * EXPERTS].rearrange("p (t e) -> p t e", e=EXPERTS)
                    v.tensor_reduce(r_mx[it], lg, AX.X, ALU.max).then_inc(*own.next())
                    v.wait_ge(*own.all())
                    v.tensor_tensor(r_lg[it], lg, over(r_mx[it], 2, EXPERTS), ALU.subtract
                                    ).then_inc(*S["less_max"].up(now))
                    v.wait_ge(*S["less_max"].at(now, use * ITEMS + it + 1))
                    other, this = over(r_lg[it], 2, EXPERTS), over(r_lg[it], 3, EXPERTS)
                    v.tensor_tensor(r_gt[it], other, this, ALU.is_gt).then_inc(*own.next())
                    v.tensor_tensor(r_eq[it], other, this, ALU.is_equal).then_inc(*own.next())
                    v.wait_ge(*own.all())
                    v.tensor_tensor(r_eq[it], r_eq[it],
                                            over(K("tie").rearrange("p (i j) -> p i j", j=EXPERTS), 1, TILES),
                                            ALU.mult).then_inc(*own.next())
                    v.wait_ge(*own.all())
                    v.tensor_tensor(r_gt[it], r_gt[it], r_eq[it], ALU.add).then_inc(*own.next())
                    v.wait_ge(*own.all())
                    v.tensor_reduce(r_rank[it], r_gt[it], AX.X, ALU.add).then_inc(*own.next())
                    v.wait_ge(*own.all())
                    v.tensor_scalar(r_sel[it], r_rank[it], TOPK - 0.5, None, ALU.is_lt
                                    ).then_inc(*S["sel_made"].up(now))
                for it in items:
                    v.wait_ge(*S["sel_made"].at(now, use * ITEMS + it + 1))
                    v.wait_ge(*S["gate_exp"].at(now, use * ITEMS + it + 1))
                    v.tensor_tensor(r_w[it], r_E[it], r_sel[it], ALU.mult).then_inc(*own.next())
                    v.wait_ge(*own.all())
                    v.tensor_reduce(r_den[it], r_E[it] if over_all else r_w[it], AX.X, ALU.add).then_inc(*own.next())
                    v.wait_ge(*own.all())
                    v.reciprocal(r_den[it], r_den[it]).then_inc(*own.next())
                    v.wait_ge(*own.all())
                    v.tensor_tensor(r_w[it], r_w[it], over(r_den[it], 2, EXPERTS), ALU.mult
                                    ).then_inc(*S["w_made"].up(now))

            def experts(own, now):
                for it in items:
                    v.wait_ge(*S["g_rms"].at(now, it + 1))
                    v.tensor_tensor(g_xn[it], xs[:, it], over(g_r[it], 2, D), ALU.mult).then_inc(*S["g_xn"].up(now))
                for it in items:
                    for zero in (g_PwT[it][:, 0], g_o[it], g_acc[it]):
                        v.memset(zero, 0.0)
                routing(own, now, 0, 1, False)
                for it in items:
                    v.wait_ge(*S["g_count"].at(now, it + 1))
                    cnt = bank(it, 2)[:, 0:TILES * EXPERTS].rearrange("p (t e) -> p t e", e=EXPERTS)
                    real = g_slot[it][:, :, 0:EXPERTS]
                    v.memset(g_slot[it][:, :, EXPERTS:], 0.0)
                    v.memset(g_w[it][:, :, EXPERTS:], 0.0)
                    v.tensor_scalar(real, cnt, -1.0, float(CAP + 1), ALU.mult, ALU.add).then_inc(*own.next())
                    v.wait_ge(*own.all())
                    v.tensor_tensor(real, real, r_sel[it], ALU.mult).then_inc(*own.next())
                    v.wait_ge(*S["w_made"].at(now, it + 1))
                    v.tensor_copy(g_w[it][:, :, 0:EXPERTS], r_w[it]).then_inc(*own.next())
                    v.wait_ge(*own.all())
                    v.tensor_scalar(g_slot[it], g_slot[it], -1.0, None, ALU.add).then_inc(*S["g_slot"].up(now))
                for it in items:
                    v.wait_ge(*S["g_slot"].at(now, it + 1))
                    place(it, 0).then_inc(*S["g_place"].up(now))
                for it in items:
                    keep_tokens(now, it, 0)
                for it in items:
                    v.wait_ge(*S["g_weighted"].at(now, it + 1))
                    place(it, 1).then_inc(*S["g_place"].up(now))
                with v.Fori(0, EXPERTS) as e:
                    inner = now.inner(e, EXPERTS)
                    expert_step(Own(S["dve_own_experts"], inner), inner, e)
                v.wait_ge(*S["g_weighted"].at(now, ITEMS * (EXPERTS + AHEAD)))
                for it in items:
                    add_up(now, it, ITEMS * EXPERTS)
                for it in items:
                    v.wait_ge(*S["g_out_rms"].at(now, it + 1))
                    v.scalar_tensor_tensor(g_onT[it], in0=g_acc[it], scalar=col("g_gnorm"), in1=g_sq[it], op0=ALU.mult,
                                           op1=ALU.mult).then_inc(*S["g_onT"].up(now))
                layernorm(own, now, 2, 2)

            def place(it, e):
                return v.tensor_tensor(g_P[it], over(K("slot"), 1, TILES),
                                       g_slot[it][:, :, bass.ds(e, 1)].broadcast_to([P, TILES, CAP]), ALU.is_equal)

            def add_up(now, it, done):
                v.wait_ge(*S["g_combined"].at(now, done + it + 1))
                v.tensor_tensor(g_acc[it], bank(it, 3), g_acc[it], ALU.add).then_inc(*S["g_sum"].up(now))

            def keep_tokens(now, it, done):
                v.wait_ge(*S["g_xe"].at(now, done + it + 1))
                v.tensor_scalar(g_xe[it].rearrange("p b s -> p (b s)"), bank(it, 3)[:, 0:IB * CAP], col("g_norm"), None,
                                ALU.mult).then_inc(*S["g_xe_kept"].up(now))

            def expert_step(own, now, e):
                for it in items:
                    v.wait_ge(*S["g_exp_f"].at(now, it + 1))
                    v.tensor_scalar(g_ln[it][:, 1], g_ln[it][:, 1], 1e18, None, ALU.min).then_inc(*S["g_cut_f"].up(now))
                def softplus_f(it):
                    v.wait_ge(*S["g_ln_f"].at(now, it + 1))
                    v.scalar_tensor_tensor(g_sp[it][:, 1], in0=bank(it, 3), scalar=-1.0, in1=g_ln[it][:, 1],
                                           op0=ALU.mult, op1=ALU.max).then_inc(*S["g_sp"].up(now))

                def cut_qk(it):
                    v.wait_ge(*S["g_exp_qk"].at(now, it + 1))
                    v.tensor_scalar(g_ln[it][:, 0], g_ln[it][:, 0], 1e18, None, ALU.min).then_inc(*S["g_cut_qk"].up(now))

                softplus_f(0)
                cut_qk(0)
                softplus_f(1)
                cut_qk(1)
                for it in items:
                    v.wait_ge(*S["g_ln_qk"].at(now, it + 1))
                    v.scalar_tensor_tensor(g_sp[it][:, 0], in0=bank(it, 2), scalar=-1.0, in1=g_ln[it][:, 0],
                                           op0=ALU.mult, op1=ALU.max).then_inc(*S["g_sp_qk"].up(now))
                for it in items:
                    v.wait_ge(*S["g_sig"].at(now, it + 1))
                    v.tensor_tensor(g_qk[it].rearrange("p a b s -> p (a b s)"), bank(it, 2), g_sig[it], ALU.mult
                                    ).then_inc(*S["g_qk"].up(now))
                    keep_tokens(now, it, ITEMS)
                for it in items:
                    v.wait_ge(*S["g_A"].at(now, it + 1))
                    mask_heads(it, 1.0).then_inc(*S["g_Am"].up(now))
                    v.wait_ge(*S["g_eg"].at(now, it + 1))
                    v.scalar_tensor_tensor(g_s[it], in0=g_s[it], scalar=1.0, in1=g_inv[it], op0=ALU.subtract,
                                           op1=ALU.mult).then_inc(*S["g_s"].up(now))
                for it in items:
                    v.wait_ge(*S["g_ok"].at(now, it + 1))
                    v.scalar_tensor_tensor(g_ok[it], in0=bank(it, 0), scalar=-1.0, in1=g_dec[it],
                                                   op0=ALU.mult, op1=ALU.mult).then_inc(*own.next())
                    v.wait_ge(*own.all())
                    ok = g_ok[it].rearrange("p (h m) -> p h m", m=GM)
                    v.tensor_reduce(g_mx[it], ok, AX.X, ALU.max).then_inc(*own.next())
                    v.wait_ge(*own.all())
                    v.tensor_tensor(ok, ok, over(g_mx[it], 2, GM), ALU.subtract).then_inc(*S["g_less_max"].up(now))
                for it in items:
                    v.wait_ge(*S["g_p"].at(now, it + 1))
                    v.tensor_tensor(g_qd[it], g_ok[it], g_dec[it], ALU.mult).then_inc(*S["g_qd"].up(now))
                    add_up(now, it, 0)
                for it in items:
                    v.tensor_reduce(g_rs[it], g_ok[it].rearrange("p (h m) -> p h m", m=GM), AX.X, ALU.add
                                    ).then_inc(*own.next())
                    v.wait_ge(*own.all())
                    v.reciprocal(g_rs[it], g_rs[it]).then_inc(*own.next())
                for it in items:
                    v.wait_ge(*S["g_T"].at(now, it + 1))
                    mask_heads(it, -1.0).then_inc(*S["g_Tm"].up(now))
                v.wait_ge(*own.all())
                for it in items:
                    v.wait_ge(*S["g_weighted"].at(now, ITEMS + it + 1))
                    place(it, e + AHEAD).then_inc(*S["g_place"].up(now))
                    v.wait_ge(*S["g_ov"].at(now, it + 1))
                    o = g_o[it].rearrange("p b (h d) -> p (b h) d", d=GK)
                    v.tensor_tensor(o, bank(it, 0)[:, 0:IB * P].rearrange("p (h d) -> p h d", d=GK),
                                    over(g_rs[it], 2, GK), ALU.mult).then_inc(*S[f"g_o{it}"].up(now))

            def mask_heads(it, sign):
                for b in range(IB):
                    i = v.scalar_tensor_tensor(g_A[it][:, :, b], in0=bank(it, 0, 4)[:, :, b * CAP:(b + 1) * CAP],
                                               scalar=sign, in1=over(K("causal"), 1, GH), op0=ALU.mult, op1=ALU.mult)
                return i

            def self_attention(own, now):
                for it in items:
                    v.wait_ge(*S["s_qkv"].at(now, it + 1))
                    v.tensor_scalar(s_qT[it], bank(it, 1), col("s_bq"), 1.0 / D, ALU.add, ALU.mult
                                    ).then_inc(*S["s_q"].up(now))
                for it in items:
                    v.wait_ge(*S["s_scores"].at(now, it + 1))
                    v.tensor_tensor(s_S[it].rearrange("p (b t) n -> p b (t n)", b=IB), bank(it, 0, 2),
                                            over(K("no_self"), 1, IB), ALU.add).then_inc(*own.next())
                    v.wait_ge(*own.all())
                    v.tensor_reduce(s_mx[it], s_S[it], AX.X, ALU.max, negate=True).then_inc(*S["s_max"].up(now))
                for it in items:
                    v.wait_ge(*S["s_exp"].at(now, it + 1))
                    v.reciprocal(s_rs[it], s_sum[it]).then_inc(*own.next())
                for it in items:
                    v.wait_ge(*S["y_made"].at(now, 3 * ITEMS + it + 1))
                    v.wait_ge(*own.all())
                    for t in tiles:
                        v.scalar_tensor_tensor(zs[:, it, t], in0=bank(it, 0)[:, t * P:(t + 1) * P],
                                               scalar=s_rs[it][:, t:t + 1], in1=xs[:, it, t],
                                               op0=ALU.mult, op1=ALU.add).then_inc(*own.next())
                    v.wait_ge(*own.all())
                    variance(own, now, it)
                normalise(own, now, 3)

            def heads_and_experts(own, now):
                for it in items:
                    v.memset(m_V[it][:, :, :, SD:SD + 1], 1.0)
                    v.memset(m_V[it][:, :, :, SD + 1:], 0.0)
                for it in items:
                    v.wait_ge(*S["m_qk"].at(now, it + 1))
                    parts = m_parts[it]
                    v.tensor_tensor(m_r[it], m_qk[it], parts[:, :, 0], ALU.subtract).then_inc(*own.next())
                    v.wait_ge(*own.all())
                    v.tensor_copy(parts[:, :, 1], m_r[it]).then_inc(*own.next())
                    v.wait_ge(*own.all())
                    v.tensor_tensor(parts[:, :, 2], m_r[it], parts[:, :, 1], ALU.subtract
                                    ).then_inc(*S["m_split"].up(now))
                routing(own, now, 1, 0, True)
                for it in items:
                    v.wait_ge(*S["m_bias"].at(now, it + 1))
                    v.tensor_tensor(m_acc[it].rearrange("p t d -> p (t d)"), bank(it, 2),
                                    xs[:, it].rearrange("p t d -> p (t d)"), ALU.add).then_inc(*S["m_acc"].up(now))
                for it in items:
                    if it == 1:
                        moe_sum(now, 1)
                    for n in range(MAX_STEPS):
                        v.wait_ge(*S[f"m_max_scores{it}"].at(now, n + 1))
                        two = bank(it, 2 * (n % 2), 2 * (n % 2) + 2).rearrange("p a (h k) -> p a h k", k=T)
                        v.tensor_reduce(m_mx[it][:, n % TILES, n // TILES * 4:n // TILES * 4 + 4], two, AX.X, ALU.max
                                        ).then_inc(*S[f"m_max_read{it}"].up(now))
                for it in items:
                    v.wait_ge(*S["m_heads"].at(now, it + 1))
                    o = bank(it, 0, 4).rearrange("p t (h l) -> p t h l", l=LANES)
                    v.reciprocal(m_rec[it].unsqueeze(3), o[:, :, :, SD:SD + 1]).then_inc(*own.next())
                    v.wait_ge(*own.all())
                    i = v.tensor_tensor(zs[:, it].rearrange("p t (h d) -> p t h d", d=SD), o[:, :, :, 0:SD],
                                        over(m_rec[it], 3, SD), ALU.mult)
                    i.then_inc(*S["m_attention"].up(now))
                    if it == 0:
                        moe_sum(now, 0)
                    v.wait_ge(*S["m_attention"].at(now, it + 1))
                    v.wait_ge(*S[f"m_moe_sum{it}"].at(now, TILES * EXPERTS))
                    v.tensor_tensor(zs[:, it], zs[:, it], m_acc[it], ALU.add).then_inc(*own.next())
                    v.wait_ge(*own.all())
                    v.tensor_tensor(zs[:, it], zs[:, it], m_acc2[it], ALU.add).then_inc(*own.next())
                    v.wait_ge(*own.all())
                    variance(own, now, it)
                normalise(own, now, 5)

            def moe_sum(now, it):
                for t in tiles:
                    v.wait_ge(*S[f"m_moe{it}"].at(now, t + 1))
                    for e in range(EXPERTS):
                        acc = (m_acc, m_acc2)[e % 2][it][:, t]
                        product, weight = bank(it, 2 * (t % 2) + e // 4)[:, e % 4 * P:(e % 4 + 1) * P], r_w[it][:, t, e:e + 1]
                        if e == 0:
                            v.wait_ge(*S["m_acc"].at(now, it + 1))
                        elif e > 1:
                            v.wait_ge(*S[f"m_moe_sum{it}"].at(now, t * EXPERTS + e - 1))
                        if e == 1:
                            i = v.tensor_scalar(acc, product, weight, None, ALU.mult)
                        else:
                            i = v.scalar_tensor_tensor(acc, in0=product, scalar=weight, in1=acc, op0=ALU.mult, op1=ALU.add)
                        i.then_inc(*S[f"m_moe_sum{it}"].up(now))

            v.sem_inc(S["x_made"].sem, 1)
            v.sem_inc(S["g_o0"].sem, 1)
            v.sem_inc(S["g_o1"].sem, 1)
            v.wait_ge(S["consts_loaded"].sem, 16 * 7)
            v.tensor_scalar(neg_cols[:], cols[:], -1.0, None, ALU.mult).then_inc(S["negated"].sem, 1)
            with v.Fori(0, ROUNDS) as r:
                now = Now(r)
                own = Own(S["dve_own"], now)
                linear_attention(own, now)
                cross_attention(own, now, 1, 0)
                experts(own, now)
                self_attention(own, now)
                cross_attention(own, now, 4, 1)
                heads_and_experts(own, now)

        @block.gpsimd
        def _(pool):
            pool.wait_ge(S["consts_loaded"].sem, 16 * 7)

            def cross_attention(now, c):
                for it in items:
                    pool.wait_ge(*S["x_v"].at(now, c * ITEMS + it + 1))
                    for b in range(IB):
                        i = pool.tensor_tensor(x_V[it][:, b], over(x_v[it][:, b], 1, 4),
                                               K("v_heads").rearrange("p (a d) -> p a d", d=D), ALU.mult)
                    i.then_inc(*S["x_V"].up(now))
                for b in range(IB):
                    for it in items:
                        pool.wait_ge(*S["x_rs"].at(now, (c * IB + b) * ITEMS + it + 1))
                        both = slice(HALF * b, HALF * (b + 1))
                        p = x_P[it][:, both].rearrange("p t (h k) -> p t h k", k=KV)
                        pool.tensor_tensor(p, p, over(x_rs[it][:, both], 3, KV), ALU.mult
                                           ).then_inc(*S["x_norm"].up(now))

            def weigh(now, e, done):
                for it in items:
                    pool.wait_ge(*S["g_place"].at(now, done + it + 1))
                    if done:
                        pool.wait_ge(*S["g_scatter"].at(now, done - ITEMS + it + 1))
                    pool.tensor_tensor(g_Pw[it], g_P[it], g_w[it][:, :, bass.ds(e, 1)].broadcast_to([P, TILES, CAP]),
                                       ALU.mult).then_inc(*S["g_weighted"].up(now))

            with pool.Fori(0, ROUNDS) as r:
                now = Now(r)
                cross_attention(now, 0)
                for e in range(AHEAD):
                    weigh(now, e, e * ITEMS)
                with pool.Fori(0, EXPERTS) as e:
                    weigh(now.inner(e, EXPERTS), e + AHEAD, AHEAD * ITEMS)
                cross_attention(now, 1)
        return S.rises()


def kernel(**inputs):
    import numpy as np
    import concourse.bacc as bacc
    from concourse.bass_utils import run_bass_kernel_spmd

    def of(name):
        return np.asarray(inputs[name])

    def by_expert(w):
        return np.transpose(w, (2, 0, 1)).reshape(w.shape[2], -1)

    qkv, bqkv = of("L1_ffn_W_qkv"), of("L1_ffn_b_qkv")
    w = {
        "a_wq": of("L0_attn_Wq").T, "a_wk": of("L0_attn_Wk").T, "a_wv": of("L0_attn_Wv").T, "a_wo": of("L0_attn_Wo").T,
        "x0_wq": of("L0_xattn_Wq"), "x0_wo": of("L0_xattn_Wo"),
        "g_wg": of("L0_ffn_Wg").T, "g_wq": of("L0_ffn_Wq").T, "g_wo": of("L0_ffn_Wo").T,
        "g_wk": by_expert(of("L0_ffn_Wk")), "g_wv": by_expert(of("L0_ffn_Wv")), "g_wf": by_expert(of("L0_ffn_Wf")),
        "s_wq": of("L1_attn_Wq").T, "s_wk": of("L1_attn_Wk").T, "s_wv": of("L1_attn_Wv").T,
        "x1_wq": of("L1_xattn_W_Q"), "x1_wo": of("L1_xattn_W_O"),
        "m_wq": qkv[:, 0:D], "m_wk": qkv[:, D:2 * D], "m_wv": qkv[:, 2 * D:], "m_wg": of("L1_ffn_W_gate"),
        "m_we": np.transpose(of("L1_ffn_W_experts"), (1, 0, 2)).reshape(D, -1),
    }
    c = {
        "a_wgamma": of("L0_attn_W_gamma"), "a_bgamma": of("L0_attn_b_gamma"), "a_wlambda": of("L0_attn_W_lambda"),
        "a_blambda": of("L0_attn_b_lambda"), "g_norm": of("L0_ffn_norm_w"), "g_gnorm": of("L0_ffn_gnorm_w"),
        "s_bq": of("L1_attn_bq"), "s_bk": of("L1_attn_bk"), "lat_g": of("L1_xattn_ln_lat_g"),
        "lat_b": of("L1_xattn_ln_lat_b"), "m_bq": bqkv[0:D], "m_bk": bqkv[D:2 * D],
    }
    rows = {"bo": of("L0_xattn_bo"), "s_bv": of("L1_attn_bv"), "m_bv": bqkv[2 * D:], "m_bg": of("L1_ffn_b_gate")}
    p, n = np.arange(P)[:, None], np.arange(P)[None, :]
    earlier = (p <= n).astype(np.float32)
    own = np.zeros((P, HALF, T), np.float32)
    for h in range(HALF):
        own[np.arange(P), h, h * P + np.arange(P)] = -np.finfo(np.float32).max
    k = {
        "ident": np.eye(P, dtype=np.float32), "causal": earlier,
        "decay_mask": -np.concatenate([earlier, np.ones((P, P), np.float32), earlier], 1),
        "mid_sum": earlier - (p < P // 2), "suffix": (p >= n), "ones": np.ones((P, T), np.float32),
        "head_sum": (p // 64 == n // 64), "kv_heads": (p // XD == np.arange(XH)[None, :]),
        "v_heads": (np.arange(BANK)[None, :] % D // XD == 2 * (np.arange(BANK)[None, :] // D) + p // KV),
        "slot": np.broadcast_to(n, (P, P)),
        "tie": np.broadcast_to((np.arange(EXPERTS)[None, :] < np.arange(EXPERTS)[:, None]).reshape(1, -1),
                               (P, EXPERTS * EXPERTS)),
        "no_self": own.reshape(P, -1),
    }
    ctx = of("ctx_768")
    arrays = {
        "x": of("x"),
        "ctx_tok": ctx.reshape(B * KV, CC),
        "ctx_T": np.transpose(ctx.reshape(B // IB, IB * KV, CC), (0, 2, 1)),
        "w_pack": np.concatenate([w[name] for name, _ in _WIDTHS], 1),
        "w_ctx": np.concatenate([of("L0_xattn_Wk"), of("L0_xattn_Wv"), of("L1_xattn_W_K"), of("L1_xattn_W_V")], 1),
        "col_pack": np.stack([c[name].reshape(P) for name in _COLS], 1),
        "ctx_cols": np.stack([of("L1_xattn_ln_in_g"), of("L1_xattn_ln_in_b")], 1),
        "const_pack": np.concatenate([k[name].astype(np.float32) for name, _ in _CONSTS], 1),
        "rows": np.concatenate([rows[name] for name, _ in _ROWS])[None, :],
        "b_experts": of("L1_ffn_b_experts"),
        "ones_row": np.ones((1, SH * TOK), mybir.dt.np(BF16)),
    }
    nc = bacc.Bacc("TRN2", target_bir_lowering=False, num_devices=1)
    args = {}
    for name, a in arrays.items():
        arrays[name] = a = np.ascontiguousarray(a)
        args[name] = nc.dram_tensor(name, a.shape, mybir.dt.from_np(a.dtype), kind="ExternalInput").ap()
    args["out"] = nc.dram_tensor("out", (B, T, D), F32, kind="ExternalOutput").ap()
    rises = build(nc, **args)
    assert not RISES or {k: n for k, n in rises.items() if n[0]} == RISES
    return run_bass_kernel_spmd(nc, [arrays], core_ids=[0]).results[0]["out"]
```
